# Optimizing a Trainium2 kernel written in Bass

```python
import numpy as np
import jax
import jax.numpy as jnp

def _softmax(x, axis=-1):
    return jax.nn.softmax(x, axis=axis)

def _gelu(x):
    return jax.nn.gelu(x, approximate=True)

def _silu(x):
    return jax.nn.silu(x)

def _sigmoid(x):
    return jax.nn.sigmoid(x)

def _layernorm(x, axis=-1, eps=1e-05):
    m = jnp.mean(x, axis=axis, keepdims=True)
    v = jnp.var(x, axis=axis, keepdims=True)
    return (x - m) / jnp.sqrt(v + eps)

def _scatter_add(tgt, idx, src, axis=0):
    return tgt.at[idx].add(src)

def _segment_sum(src, seg, n):
    return jax.ops.segment_sum(src, seg, n)
kernel_name = 'mk_flamingo_gated_d4_seqx_r4_dd25b3'

def setup_inputs(seed: int=0):
    np.random.seed(seed)
    _w = jnp.asarray

    def _rec_inputs():
        import jax
        import jax.numpy as jnp
        _rk = jax.random.key(seed)
        x = -0.0003929 + 0.9999 * jax.random.normal(jax.random.fold_in(_rk, 1), (4, 1024, 256), jnp.float32)
        _lenS = 1024 - jax.random.randint(jax.random.fold_in(_rk, 7), (4,), 0, max(1, 1024 // 4) + 1, jnp.int32)
        _lenS2 = 77 - jax.random.randint(jax.random.fold_in(_rk, 8), (4,), 0, max(1, 77 // 4) + 1, jnp.int32)
        _ctx_1024P = jax.random.normal(jax.random.fold_in(_rk, 11), (4, 16, 256), jnp.float32)
        _ctx_1024c = jax.random.dirichlet(jax.random.fold_in(_rk, 511), 0.3 * jnp.ones((16,), jnp.float32), (4, 77))
        _ctx_1024t = jnp.einsum('bsk,bkd->bsd', _ctx_1024c, _ctx_1024P)
        _ctx_1024t = _ctx_1024t * jax.lax.rsqrt(jnp.mean(jnp.square(_ctx_1024t)) + 1e-12) * 0.953939
        ctx_1024 = 4.13588e-05 + 0.999923 * (_ctx_1024t + 0.3 * jax.random.normal(jax.random.fold_in(_rk, 611), (4, 77, 256), jnp.float32))
        _validS = jnp.arange(1024)[None, :] < _lenS[:, None]
        _validS2 = jnp.arange(77)[None, :] < _lenS2[:, None]
        _causal = jnp.tril(jnp.ones((1024, 1024), dtype=bool))
        mask_SxS2_ff0 = jnp.where(jnp.ones((1024, 77), dtype=bool), 0.0, -1000000000.0).astype(jnp.float32)
        mask_BxS2_bf0 = jnp.logical_not(jnp.ones((4, 77), dtype=bool))
        mask_1x1xSxS2_bk0 = jnp.logical_not(jnp.broadcast_to(_validS2[0:1, None, None, :], (1, 1, 1024, 77)))
        _g = jax.random.normal(jax.random.fold_in(_rk, 9001), (2, 4), jnp.float32)
        _g = jnp.sign(_g) * jnp.maximum(jnp.abs(_g), 1.0) + (_g == 0) * 1.0
        g_xattn = _g[0]
        g_ffn = _g[1]
        return (x, ctx_1024, mask_SxS2_ff0, mask_BxS2_bf0, mask_1x1xSxS2_bk0, g_xattn, g_ffn)
    x, ctx_1024, mask_SxS2_ff0, mask_BxS2_bf0, mask_1x1xSxS2_bk0, g_xattn, g_ffn = _rec_inputs()

    def _L0_xattn_setup():
        import jax, jax.numpy as jnp
        import numpy as np
        H = 256
        B = 8
        L_CHAR = 512
        L_SUB = 256

        def _linear(x, W, b):
            return jnp.einsum('blh,oh->blo', x, W) + b

        def _interp_linear(x, out_len):
            L_in = x.shape[1]
            pos = (jnp.arange(out_len, dtype=x.dtype) + 0.5) * (L_in / out_len) - 0.5
            pos = jnp.clip(pos, 0.0, L_in - 1)
            lo = jnp.floor(pos).astype(jnp.int32)
            hi = jnp.minimum(lo + 1, L_in - 1)
            w = (pos - lo.astype(x.dtype))[None, :, None]
            return x[:, lo] * (1 - w) + x[:, hi] * w
        key = jax.random.key(seed)
        ks = jax.random.split(key, 18)
        s = 0.02
        inp = {'char_emb': jax.random.normal(ks[0], (B, L_CHAR, H), jnp.float32), 'subword_emb': jax.random.normal(ks[1], (B, L_SUB, H), jnp.float32)}
        names = ['Wq_c', 'Wk_s', 'Wv_s', 'Wq_s', 'Wk_c', 'Wv_c']
        for i, n in enumerate(names):
            inp[n] = jax.random.normal(ks[2 + 2 * i], (H, H), jnp.float32) * s
            inp['b' + n[1:]] = jax.random.normal(ks[3 + 2 * i], (H,), jnp.float32) * s
        inp['Wg'] = jax.random.normal(ks[14], (H, 2 * H), jnp.float32) * s
        inp['bg'] = jax.random.normal(ks[15], (H,), jnp.float32) * s
        return inp
    _L0_xattn_all = _L0_xattn_setup()
    _L0_xattn_in = {k: v for k, v in _L0_xattn_all.items() if k in ('Wq_c', 'bq_c', 'Wk_s', 'bk_s', 'Wv_s', 'bv_s', 'Wq_s', 'bq_s', 'Wk_c', 'bk_c', 'Wv_c', 'bv_c', 'Wg', 'bg')}
    del _L0_xattn_all

    def _L0_ffn_setup():
        import jax, jax.numpy as jnp
        import numpy as np
        B, S, D_MODEL, D_HIDDEN = (4, 512, 256, 1024)

        def act_quant(x):
            scale = 127.0 / jnp.clip(jnp.max(jnp.abs(x), axis=-1, keepdims=True), 1e-05)
            return jnp.clip(jnp.round(x * scale), -128, 127) / scale

        def weight_quant(w):
            scale = 1.0 / jnp.clip(jnp.mean(jnp.abs(w)), 1e-05)
            return jnp.clip(jnp.round(w * scale), -1, 1) / scale

        def bit_linear(x, w):
            xq = x + jax.lax.stop_gradient(act_quant(x) - x)
            wq = w + jax.lax.stop_gradient(weight_quant(w) - w)
            return jnp.einsum('bsd,hd->bsh', xq, wq)

        def depthwise_conv1d(x_bcl, w, b):
            y = jax.lax.conv_general_dilated(x_bcl, w, window_strides=(1,), padding=[(1, 1)], dimension_numbers=('NCH', 'OIH', 'NCH'), feature_group_count=x_bcl.shape[1])
            return y + b[None, :, None]
        key = jax.random.key(seed)
        ks = jax.random.split(key, 5)
        lim1 = 1.0 / np.sqrt(D_MODEL)
        lim2 = 1.0 / np.sqrt(D_HIDDEN)
        limc = 1.0 / np.sqrt(3.0)
        return {'x': jax.random.normal(ks[0], (B, S, D_MODEL), dtype=jnp.float32), 'w1': jax.random.uniform(ks[1], (D_HIDDEN, D_MODEL), jnp.float32, -lim1, lim1), 'conv_w': jax.random.uniform(ks[2], (D_HIDDEN, 1, 3), jnp.float32, -limc, limc), 'conv_b': jax.random.uniform(ks[3], (D_HIDDEN,), jnp.float32, -limc, limc), 'w2': jax.random.uniform(ks[4], (D_MODEL, D_HIDDEN), jnp.float32, -lim2, lim2)}
    _L0_ffn_all = _L0_ffn_setup()
    _L0_ffn_in = {k: v for k, v in _L0_ffn_all.items() if k in ('w1', 'conv_w', 'conv_b', 'w2')}
    del _L0_ffn_all

    def _L1_xattn_setup():
        import jax, jax.numpy as jnp
        import numpy as np
        B, LQ, LKV, E, H = (4, 512, 512, 256, 16)
        D = E // H
        EPS = 1e-05

        def _freq_cross_attn(query, key_value, gamma, beta, Wqr, bqr, Wqi, bqi, Wkr, bkr, Wki, bki, Wvr, bvr, Wvi, bvi, Wo):
            Bq, Lq, Ee = query.shape
            mu = jnp.mean(query, axis=-1, keepdims=True)
            var = jnp.var(query, axis=-1, keepdims=True)
            qn = (query - mu) / jnp.sqrt(var + EPS) * gamma + beta
            qf = jnp.fft.rfft(qn, axis=1, norm='ortho')
            kvf = jnp.fft.rfft(key_value, axis=1, norm='ortho')

            def proj(x, W, bias):
                return x @ W.T + bias
            Qr = proj(qf.real, Wqr, bqr)
            Qi = proj(qf.imag, Wqi, bqi)
            Kr = proj(kvf.real, Wkr, bkr)
            Ki = proj(kvf.imag, Wki, bki)
            Vr = proj(kvf.real, Wvr, bvr)
            Vi = proj(kvf.imag, Wvi, bvi)
            split = lambda x: x.reshape(x.shape[0], x.shape[1], H, D)
            Qr, Qi, Kr, Ki, Vr, Vi = map(split, (Qr, Qi, Kr, Ki, Vr, Vi))
            scale = D ** (-0.5)
            scores = (jnp.einsum('blhd,bmhd->bhlm', Qr, Kr) + jnp.einsum('blhd,bmhd->bhlm', Qi, Ki)) * scale
            w = jax.nn.softmax(scores, axis=-1)
            out_r = jnp.einsum('bhlm,bmhd->blhd', w, Vr)
            out_i = jnp.einsum('bhlm,bmhd->blhd', w, Vi)
            out_r = out_r.reshape(Bq, -1, Ee)
            out_i = out_i.reshape(Bq, -1, Ee)
            out_freq = jax.lax.complex(out_r, out_i)
            out_time = jnp.fft.irfft(out_freq, n=Lq, axis=1, norm='ortho')
            return out_time @ Wo.T
        key = jax.random.key(seed)
        ks = jax.random.split(key, 16)
        w = lambda k: jax.random.normal(k, (E, E), dtype=jnp.float32) * 0.02
        b = lambda k: jax.random.normal(k, (E,), dtype=jnp.float32) * 0.02
        return {'query': jax.random.normal(ks[0], (B, LQ, E), dtype=jnp.float32), 'key_value': jax.random.normal(ks[1], (B, LKV, E), dtype=jnp.float32), 'gamma': jnp.ones((E,), dtype=jnp.float32), 'beta': jnp.zeros((E,), dtype=jnp.float32), 'Wqr': w(ks[2]), 'bqr': b(ks[3]), 'Wqi': w(ks[4]), 'bqi': b(ks[5]), 'Wkr': w(ks[6]), 'bkr': b(ks[7]), 'Wki': w(ks[8]), 'bki': b(ks[9]), 'Wvr': w(ks[10]), 'bvr': b(ks[11]), 'Wvi': w(ks[12]), 'bvi': b(ks[13]), 'Wo': w(ks[14])}
    _L1_xattn_all = _L1_xattn_setup()
    _L1_xattn_in = {k: v for k, v in _L1_xattn_all.items() if k in ('gamma', 'beta', 'Wqr', 'bqr', 'Wqi', 'bqi', 'Wkr', 'bkr', 'Wki', 'bki', 'Wvr', 'bvr', 'Wvi', 'bvi', 'Wo')}
    del _L1_xattn_all

    def _L1_ffn_setup():
        import jax, jax.numpy as jnp
        import numpy as np
        THRESH_FACTOR = 0.7

        def ternary_quantize(w):
            delta = THRESH_FACTOR * jnp.mean(jnp.abs(w))
            return jnp.where(w > delta, 1.0, jnp.where(w < -delta, -1.0, 0.0)).astype(w.dtype)
        key = jax.random.key(seed)
        k1, k2, k3 = jax.random.split(key, 3)
        B, S, D_IN, D_OUT = (8, 1024, 256, 256)
        inp = {'input': jax.random.normal(k1, (B, S, D_IN), dtype=jnp.float32), 'weight': jax.random.normal(k2, (D_OUT, D_IN), dtype=jnp.float32) * (1.0 / np.sqrt(D_IN)), 'alpha': jnp.ones((1,), dtype=jnp.float32), 'bias': jax.random.normal(k3, (D_OUT,), dtype=jnp.float32) * (1.0 / np.sqrt(D_IN))}
        return inp
    _L1_ffn_all = _L1_ffn_setup()
    _L1_ffn_in = {k: v for k, v in _L1_ffn_all.items() if k in ('weight', 'alpha', 'bias')}
    del _L1_ffn_all

    def _L2_xattn_setup():
        import jax, jax.numpy as jnp
        import numpy as np
        D_MODEL = 256
        NUM_HEADS = 16
        HEAD_DIM = D_MODEL // NUM_HEADS
        B, TQ, TK = (4, 512, 512)
        key = jax.random.key(seed)
        ks = jax.random.split(key, 6)
        s = 1.0 / np.sqrt(D_MODEL)
        return {'x_q': jax.random.normal(ks[0], (B, TQ, D_MODEL), dtype=jnp.float32), 'x_kv': jax.random.normal(ks[1], (B, TK, D_MODEL), dtype=jnp.float32), 'attn_mask': jnp.zeros((TQ, TK), dtype=jnp.float32), 'key_padding_mask': jnp.zeros((B, TK), dtype=bool), 'Wq': jax.random.normal(ks[2], (D_MODEL, D_MODEL), dtype=jnp.float32) * s, 'Wk': jax.random.normal(ks[3], (D_MODEL, D_MODEL), dtype=jnp.float32) * s, 'Wv': jax.random.normal(ks[4], (D_MODEL, D_MODEL), dtype=jnp.float32) * s, 'Wo': jax.random.normal(ks[5], (D_MODEL, D_MODEL), dtype=jnp.float32) * s}
    _L2_xattn_all = _L2_xattn_setup()
    _L2_xattn_in = {k: v for k, v in _L2_xattn_all.items() if k in ('Wq', 'Wk', 'Wv', 'Wo')}
    del _L2_xattn_all

    def _L2_ffn_setup():
        import jax, jax.numpy as jnp
        import numpy as np
        B, S, D, E, H = (2, 256, 256, 16, 512)
        TOP_K = 2
        TEMP = 1.0
        key = jax.random.key(seed)
        ks = jax.random.split(key, 4)
        sc_d = 1.0 / np.sqrt(D)
        sc_h = 1.0 / np.sqrt(H)
        return {'x': jax.random.normal(ks[0], (B, S, D), dtype=jnp.float32), 'Wr': jax.random.normal(ks[1], (D, E), dtype=jnp.float32) * sc_d, 'br': jnp.zeros((E,), dtype=jnp.float32), 'W1': jax.random.normal(ks[2], (E, D, H), dtype=jnp.float32) * sc_d, 'b1': jnp.zeros((E, H), dtype=jnp.float32), 'W2': jax.random.normal(ks[3], (E, H, D), dtype=jnp.float32) * sc_h, 'b2': jnp.zeros((E, D), dtype=jnp.float32)}
    _L2_ffn_all = _L2_ffn_setup()
    _L2_ffn_in = {k: v for k, v in _L2_ffn_all.items() if k in ('Wr', 'br', 'W1', 'b1', 'W2', 'b2')}
    del _L2_ffn_all

    def _L3_xattn_setup():
        import jax, jax.numpy as jnp
        import numpy as np
        D_MODEL = 256
        N_HEADS = 16
        D_K = D_MODEL // N_HEADS
        B, S = (2, 512)
        key = jax.random.key(seed)
        ks = jax.random.split(key, 12)
        scale = 1.0 / np.sqrt(D_MODEL)
        inp = {'query': jax.random.normal(ks[0], (B, S, D_MODEL), jnp.float32), 'key': jax.random.normal(ks[1], (B, S, D_MODEL), jnp.float32), 'value': jax.random.normal(ks[2], (B, S, D_MODEL), jnp.float32), 'mask': jnp.tril(jnp.ones((S, S), dtype=bool))[None, None], 'W_q': jax.random.normal(ks[3], (D_MODEL, D_MODEL), jnp.float32) * scale, 'b_q': jnp.zeros((D_MODEL,), jnp.float32), 'W_k': jax.random.normal(ks[4], (D_MODEL, D_MODEL), jnp.float32) * scale, 'b_k': jnp.zeros((D_MODEL,), jnp.float32), 'W_v': jax.random.normal(ks[5], (D_MODEL, D_MODEL), jnp.float32) * scale, 'b_v': jnp.zeros((D_MODEL,), jnp.float32), 'W_o': jax.random.normal(ks[6], (D_MODEL, D_MODEL), jnp.float32) * scale, 'b_o': jnp.zeros((D_MODEL,), jnp.float32)}
        return inp
    _L3_xattn_all = _L3_xattn_setup()
    _L3_xattn_in = {k: v for k, v in _L3_xattn_all.items() if k in ('W_q', 'b_q', 'W_k', 'b_k', 'W_v', 'b_v', 'W_o', 'b_o')}
    del _L3_xattn_all

    def _L3_ffn_setup():
        import jax, jax.numpy as jnp
        import numpy as np
        from jax import lax
        T, B, I, M, O = (64, 64, 256, 256, 256)

        def _xavier(key, shape):
            fan_out, fan_in = shape
            limit = float(np.sqrt(6.0 / (fan_in + fan_out)))
            return jax.random.uniform(key, shape, jnp.float32, -limit, limit)
        key = jax.random.key(seed)
        ks = jax.random.split(key, 9)
        x = jax.random.normal(ks[0], (T, B, I), jnp.float32)
        return {'x': x, 'wf': _xavier(ks[1], (M, I)), 'uf': _xavier(ks[2], (M, M)), 'bf': jnp.zeros((M,), jnp.float32), 'wi': _xavier(ks[3], (M, I)), 'ui': _xavier(ks[4], (M, M)), 'bi': jnp.zeros((M,), jnp.float32), 'wc': _xavier(ks[5], (M, I)), 'uc': _xavier(ks[6], (M, M)), 'bc': jnp.zeros((M,), jnp.float32), 'wo': _xavier(ks[7], (O, I)), 'uo': _xavier(ks[8], (O, M)), 'bo': jnp.zeros((O,), jnp.float32), 'in_c': jnp.zeros((M,), jnp.float32)}
    _L3_ffn_all = _L3_ffn_setup()
    _L3_ffn_in = {k: v for k, v in _L3_ffn_all.items() if k in ('wf', 'uf', 'bf', 'wi', 'ui', 'bi', 'wc', 'uc', 'bc', 'wo', 'uo', 'bo', 'in_c')}
    del _L3_ffn_all
    return {'x': x, 'ctx_1024': ctx_1024, 'mask_SxS2_ff0': mask_SxS2_ff0, 'mask_BxS2_bf0': mask_BxS2_bf0, 'mask_1x1xSxS2_bk0': mask_1x1xSxS2_bk0, 'g_xattn': g_xattn, 'g_ffn': g_ffn, 'L0_xattn_Wq_c': _L0_xattn_in['Wq_c'], 'L0_xattn_bq_c': _L0_xattn_in['bq_c'], 'L0_xattn_Wk_s': _L0_xattn_in['Wk_s'], 'L0_xattn_bk_s': _L0_xattn_in['bk_s'], 'L0_xattn_Wv_s': _L0_xattn_in['Wv_s'], 'L0_xattn_bv_s': _L0_xattn_in['bv_s'], 'L0_xattn_Wq_s': _L0_xattn_in['Wq_s'], 'L0_xattn_bq_s': _L0_xattn_in['bq_s'], 'L0_xattn_Wk_c': _L0_xattn_in['Wk_c'], 'L0_xattn_bk_c': _L0_xattn_in['bk_c'], 'L0_xattn_Wv_c': _L0_xattn_in['Wv_c'], 'L0_xattn_bv_c': _L0_xattn_in['bv_c'], 'L0_xattn_Wg': _L0_xattn_in['Wg'], 'L0_xattn_bg': _L0_xattn_in['bg'], 'L0_ffn_w1': _L0_ffn_in['w1'], 'L0_ffn_conv_w': _L0_ffn_in['conv_w'], 'L0_ffn_conv_b': _L0_ffn_in['conv_b'], 'L0_ffn_w2': _L0_ffn_in['w2'], 'L1_xattn_gamma': _L1_xattn_in['gamma'], 'L1_xattn_beta': _L1_xattn_in['beta'], 'L1_xattn_Wqr': _L1_xattn_in['Wqr'], 'L1_xattn_bqr': _L1_xattn_in['bqr'], 'L1_xattn_Wqi': _L1_xattn_in['Wqi'], 'L1_xattn_bqi': _L1_xattn_in['bqi'], 'L1_xattn_Wkr': _L1_xattn_in['Wkr'], 'L1_xattn_bkr': _L1_xattn_in['bkr'], 'L1_xattn_Wki': _L1_xattn_in['Wki'], 'L1_xattn_bki': _L1_xattn_in['bki'], 'L1_xattn_Wvr': _L1_xattn_in['Wvr'], 'L1_xattn_bvr': _L1_xattn_in['bvr'], 'L1_xattn_Wvi': _L1_xattn_in['Wvi'], 'L1_xattn_bvi': _L1_xattn_in['bvi'], 'L1_xattn_Wo': _L1_xattn_in['Wo'], 'L1_ffn_weight': _L1_ffn_in['weight'], 'L1_ffn_alpha': _L1_ffn_in['alpha'], 'L1_ffn_bias': _L1_ffn_in['bias'], 'L2_xattn_Wq': _L2_xattn_in['Wq'], 'L2_xattn_Wk': _L2_xattn_in['Wk'], 'L2_xattn_Wv': _L2_xattn_in['Wv'], 'L2_xattn_Wo': _L2_xattn_in['Wo'], 'L2_ffn_Wr': _L2_ffn_in['Wr'], 'L2_ffn_br': _L2_ffn_in['br'], 'L2_ffn_W1': _L2_ffn_in['W1'], 'L2_ffn_b1': _L2_ffn_in['b1'], 'L2_ffn_W2': _L2_ffn_in['W2'], 'L2_ffn_b2': _L2_ffn_in['b2'], 'L3_xattn_W_q': _L3_xattn_in['W_q'], 'L3_xattn_b_q': _L3_xattn_in['b_q'], 'L3_xattn_W_k': _L3_xattn_in['W_k'], 'L3_xattn_b_k': _L3_xattn_in['b_k'], 'L3_xattn_W_v': _L3_xattn_in['W_v'], 'L3_xattn_b_v': _L3_xattn_in['b_v'], 'L3_xattn_W_o': _L3_xattn_in['W_o'], 'L3_xattn_b_o': _L3_xattn_in['b_o'], 'L3_ffn_wf': _L3_ffn_in['wf'], 'L3_ffn_uf': _L3_ffn_in['uf'], 'L3_ffn_bf': _L3_ffn_in['bf'], 'L3_ffn_wi': _L3_ffn_in['wi'], 'L3_ffn_ui': _L3_ffn_in['ui'], 'L3_ffn_bi': _L3_ffn_in['bi'], 'L3_ffn_wc': _L3_ffn_in['wc'], 'L3_ffn_uc': _L3_ffn_in['uc'], 'L3_ffn_bc': _L3_ffn_in['bc'], 'L3_ffn_wo': _L3_ffn_in['wo'], 'L3_ffn_uo': _L3_ffn_in['uo'], 'L3_ffn_bo': _L3_ffn_in['bo'], 'L3_ffn_in_c': _L3_ffn_in['in_c']}

def reference(x, ctx_1024, mask_SxS2_ff0, mask_BxS2_bf0, mask_1x1xSxS2_bk0, g_xattn, g_ffn, L0_xattn_Wq_c, L0_xattn_bq_c, L0_xattn_Wk_s, L0_xattn_bk_s, L0_xattn_Wv_s, L0_xattn_bv_s, L0_xattn_Wq_s, L0_xattn_bq_s, L0_xattn_Wk_c, L0_xattn_bk_c, L0_xattn_Wv_c, L0_xattn_bv_c, L0_xattn_Wg, L0_xattn_bg, L0_ffn_w1, L0_ffn_conv_w, L0_ffn_conv_b, L0_ffn_w2, L1_xattn_gamma, L1_xattn_beta, L1_xattn_Wqr, L1_xattn_bqr, L1_xattn_Wqi, L1_xattn_bqi, L1_xattn_Wkr, L1_xattn_bkr, L1_xattn_Wki, L1_xattn_bki, L1_xattn_Wvr, L1_xattn_bvr, L1_xattn_Wvi, L1_xattn_bvi, L1_xattn_Wo, L1_ffn_weight, L1_ffn_alpha, L1_ffn_bias, L2_xattn_Wq, L2_xattn_Wk, L2_xattn_Wv, L2_xattn_Wo, L2_ffn_Wr, L2_ffn_br, L2_ffn_W1, L2_ffn_b1, L2_ffn_W2, L2_ffn_b2, L3_xattn_W_q, L3_xattn_b_q, L3_xattn_W_k, L3_xattn_b_k, L3_xattn_W_v, L3_xattn_b_v, L3_xattn_W_o, L3_xattn_b_o, L3_ffn_wf, L3_ffn_uf, L3_ffn_bf, L3_ffn_wi, L3_ffn_ui, L3_ffn_bi, L3_ffn_wc, L3_ffn_uc, L3_ffn_bc, L3_ffn_wo, L3_ffn_uo, L3_ffn_bo, L3_ffn_in_c):
    import jax
    import jax.numpy as jnp

    def _L0_xattn_ref(char_emb, subword_emb, Wq_c, bq_c, Wk_s, bk_s, Wv_s, bv_s, Wq_s, bq_s, Wk_c, bk_c, Wv_c, bv_c, Wg, bg):
        import jax, jax.numpy as jnp
        import numpy as np
        H = 256
        B = 8
        L_CHAR = 512
        L_SUB = 256

        def _linear(x, W, b):
            return jnp.einsum('blh,oh->blo', x, W) + b

        def _interp_linear(x, out_len):
            L_in = x.shape[1]
            pos = (jnp.arange(out_len, dtype=x.dtype) + 0.5) * (L_in / out_len) - 0.5
            pos = jnp.clip(pos, 0.0, L_in - 1)
            lo = jnp.floor(pos).astype(jnp.int32)
            hi = jnp.minimum(lo + 1, L_in - 1)
            w = (pos - lo.astype(x.dtype))[None, :, None]
            return x[:, lo] * (1 - w) + x[:, hi] * w
        h = char_emb.shape[-1]
        scale = 1.0 / jnp.sqrt(jnp.asarray(h, char_emb.dtype))
        Q_char = _linear(char_emb, Wq_c, bq_c)
        K_sub = _linear(subword_emb, Wk_s, bk_s)
        V_sub = _linear(subword_emb, Wv_s, bv_s)
        scores = jnp.einsum('bqh,bkh->bqk', Q_char, K_sub) * scale
        char2sub = jnp.einsum('bqk,bkh->bqh', jax.nn.softmax(scores, axis=-1), V_sub)
        Q_sub = _linear(subword_emb, Wq_s, bq_s)
        K_char = _linear(char_emb, Wk_c, bk_c)
        V_char = _linear(char_emb, Wv_c, bv_c)
        scores2 = jnp.einsum('bqh,bkh->bqk', Q_sub, K_char) * scale
        sub2char = jnp.einsum('bqk,bkh->bqh', jax.nn.softmax(scores2, axis=-1), V_char)
        L_char = char_emb.shape[1]
        if sub2char.shape[1] != L_char:
            sub2char = _interp_linear(sub2char, L_char)
        gate_in = jnp.concatenate([char2sub, sub2char], axis=-1)
        gate = jax.nn.sigmoid(jnp.einsum('blh,oh->blo', gate_in, Wg) + bg)
        return gate * char2sub + (1 - gate) * sub2char

    def _L0_ffn_ref(x, w1, conv_w, conv_b, w2):
        import jax, jax.numpy as jnp
        import numpy as np
        B, S, D_MODEL, D_HIDDEN = (4, 512, 256, 1024)

        def act_quant(x):
            scale = 127.0 / jnp.clip(jnp.max(jnp.abs(x), axis=-1, keepdims=True), 1e-05)
            return jnp.clip(jnp.round(x * scale), -128, 127) / scale

        def weight_quant(w):
            scale = 1.0 / jnp.clip(jnp.mean(jnp.abs(w)), 1e-05)
            return jnp.clip(jnp.round(w * scale), -1, 1) / scale

        def bit_linear(x, w):
            xq = x + jax.lax.stop_gradient(act_quant(x) - x)
            wq = w + jax.lax.stop_gradient(weight_quant(w) - w)
            return jnp.einsum('bsd,hd->bsh', xq, wq)

        def depthwise_conv1d(x_bcl, w, b):
            y = jax.lax.conv_general_dilated(x_bcl, w, window_strides=(1,), padding=[(1, 1)], dimension_numbers=('NCH', 'OIH', 'NCH'), feature_group_count=x_bcl.shape[1])
            return y + b[None, :, None]
        h = bit_linear(x, w1)
        h = depthwise_conv1d(h.transpose(0, 2, 1), conv_w, conv_b)
        h = h.transpose(0, 2, 1)
        h = jax.nn.silu(h)
        return bit_linear(h, w2)

    def _L1_xattn_ref(query, key_value, gamma, beta, Wqr, bqr, Wqi, bqi, Wkr, bkr, Wki, bki, Wvr, bvr, Wvi, bvi, Wo):
        import jax, jax.numpy as jnp
        import numpy as np
        B, LQ, LKV, E, H = (4, 512, 512, 256, 16)
        D = E // H
        EPS = 1e-05

        def _freq_cross_attn(query, key_value, gamma, beta, Wqr, bqr, Wqi, bqi, Wkr, bkr, Wki, bki, Wvr, bvr, Wvi, bvi, Wo):
            Bq, Lq, Ee = query.shape
            mu = jnp.mean(query, axis=-1, keepdims=True)
            var = jnp.var(query, axis=-1, keepdims=True)
            qn = (query - mu) / jnp.sqrt(var + EPS) * gamma + beta
            qf = jnp.fft.rfft(qn, axis=1, norm='ortho')
            kvf = jnp.fft.rfft(key_value, axis=1, norm='ortho')

            def proj(x, W, bias):
                return x @ W.T + bias
            Qr = proj(qf.real, Wqr, bqr)
            Qi = proj(qf.imag, Wqi, bqi)
            Kr = proj(kvf.real, Wkr, bkr)
            Ki = proj(kvf.imag, Wki, bki)
            Vr = proj(kvf.real, Wvr, bvr)
            Vi = proj(kvf.imag, Wvi, bvi)
            split = lambda x: x.reshape(x.shape[0], x.shape[1], H, D)
            Qr, Qi, Kr, Ki, Vr, Vi = map(split, (Qr, Qi, Kr, Ki, Vr, Vi))
            scale = D ** (-0.5)
            scores = (jnp.einsum('blhd,bmhd->bhlm', Qr, Kr) + jnp.einsum('blhd,bmhd->bhlm', Qi, Ki)) * scale
            w = jax.nn.softmax(scores, axis=-1)
            out_r = jnp.einsum('bhlm,bmhd->blhd', w, Vr)
            out_i = jnp.einsum('bhlm,bmhd->blhd', w, Vi)
            out_r = out_r.reshape(Bq, -1, Ee)
            out_i = out_i.reshape(Bq, -1, Ee)
            out_freq = jax.lax.complex(out_r, out_i)
            out_time = jnp.fft.irfft(out_freq, n=Lq, axis=1, norm='ortho')
            return out_time @ Wo.T
        return _freq_cross_attn(query, key_value, gamma, beta, Wqr, bqr, Wqi, bqi, Wkr, bkr, Wki, bki, Wvr, bvr, Wvi, bvi, Wo)

    def _L1_ffn_ref(input, weight, alpha, bias):
        import jax, jax.numpy as jnp
        import numpy as np
        THRESH_FACTOR = 0.7

        def ternary_quantize(w):
            delta = THRESH_FACTOR * jnp.mean(jnp.abs(w))
            return jnp.where(w > delta, 1.0, jnp.where(w < -delta, -1.0, 0.0)).astype(w.dtype)
        w_ternary = ternary_quantize(weight)
        w_eff = w_ternary * alpha
        out = jnp.einsum('bsd,od->bso', input, w_eff) + bias
        return out

    def _L2_xattn_ref(x_q, x_kv, attn_mask, key_padding_mask, Wq, Wk, Wv, Wo):
        import jax, jax.numpy as jnp
        import numpy as np
        D_MODEL = 256
        NUM_HEADS = 16
        HEAD_DIM = D_MODEL // NUM_HEADS
        B, TQ, TK = (4, 512, 512)
        b, tq, d = x_q.shape
        tk = x_kv.shape[1]
        h, hd = (NUM_HEADS, HEAD_DIM)
        q = (x_q @ Wq.T).reshape(b, tq, h, hd).transpose(0, 2, 1, 3)
        k = (x_kv @ Wk.T).reshape(b, tk, h, hd).transpose(0, 2, 1, 3)
        v = (x_kv @ Wv.T).reshape(b, tk, h, hd).transpose(0, 2, 1, 3)
        scores = jnp.einsum('bhqd,bhkd->bhqk', q, k) / jnp.sqrt(jnp.float32(hd))
        scores = scores + attn_mask
        scores = jnp.where(key_padding_mask[:, None, None, :], -jnp.inf, scores)
        w = jax.nn.softmax(scores, axis=-1)
        out = jnp.einsum('bhqk,bhkd->bhqd', w, v)
        out = out.transpose(0, 2, 1, 3).reshape(b, tq, d)
        return out @ Wo.T

    def _L2_ffn_ref(x, Wr, br, W1, b1, W2, b2):
        import jax, jax.numpy as jnp
        import numpy as np
        B, S, D, E, H = (2, 256, 256, 16, 512)
        TOP_K = 2
        TEMP = 1.0
        token_shape = x.shape[:-1]
        d = x.shape[-1]
        xt = x.reshape(-1, d)
        T = xt.shape[0]
        logits = (xt @ Wr + br) / TEMP
        probs = jax.nn.softmax(logits, axis=-1)
        w, idx = jax.lax.top_k(probs, TOP_K)
        w = w / jnp.clip(jnp.sum(w, axis=-1, keepdims=True), 1e-09)
        comb = jnp.zeros((T, E), dtype=xt.dtype)
        comb = comb.at[jnp.arange(T)[:, None], idx].add(w)
        h = jax.nn.gelu(jnp.einsum('td,edh->teh', xt, W1) + b1, approximate=False)
        o = jnp.einsum('teh,eho->teo', h, W2) + b2
        y = jnp.einsum('teo,te->to', o, comb)
        y = xt + y
        return y.reshape(*token_shape, d)

    def _L3_xattn_ref(query, key, value, mask, W_q, b_q, W_k, b_k, W_v, b_v, W_o, b_o):
        import jax, jax.numpy as jnp
        import numpy as np
        D_MODEL = 256
        N_HEADS = 16
        D_K = D_MODEL // N_HEADS
        B, S = (2, 512)
        b = query.shape[0]

        def proj(x, W, bias):
            y = x @ W.T + bias
            return y.reshape(b, -1, N_HEADS, D_K).transpose(0, 2, 1, 3)
        q = proj(query, W_q, b_q)
        k = proj(key, W_k, b_k)
        v = proj(value, W_v, b_v)
        scores = jnp.einsum('bhqd,bhkd->bhqk', q, k) / jnp.sqrt(jnp.float32(D_K)).astype(q.dtype)
        scores = jnp.where(mask, scores, jnp.finfo(scores.dtype).min)
        attn = jax.nn.softmax(scores, axis=-1)
        out = jnp.einsum('bhqk,bhkd->bhqd', attn, v)
        out = out.transpose(0, 2, 1, 3).reshape(b, -1, D_MODEL)
        return out @ W_o.T + b_o

    def _L3_ffn_ref(x, wf, uf, bf, wi, ui, bi, wc, uc, bc, wo, uo, bo, in_c):
        import jax, jax.numpy as jnp
        import numpy as np
        from jax import lax
        T, B, I, M, O = (64, 64, 256, 256, 256)

        def _xavier(key, shape):
            fan_out, fan_in = shape
            limit = float(np.sqrt(6.0 / (fan_in + fan_out)))
            return jax.random.uniform(key, shape, jnp.float32, -limit, limit)
        batch = x.shape[1]
        c0 = jnp.broadcast_to(in_c, (batch, in_c.shape[0]))

        def step(c, xt):
            ft = jax.nn.sigmoid(xt @ wf.T + c @ uf.T + bf)
            it = jax.nn.sigmoid(xt @ wi.T + c @ ui.T + bi)
            gt = jnp.tanh(xt @ wc.T + c @ uc.T + bc)
            c = ft * c + it * gt
            return (c, None)
        c_final, _ = lax.scan(step, c0, x)
        h = jnp.tanh(jnp.einsum('tbi,oi->tbo', x, wo) + c_final @ uo.T + bo)
        return h
    x = x + jnp.tanh(g_xattn[0]) * _L0_xattn_ref(_layernorm(x, axis=-1), ctx_1024, L0_xattn_Wq_c, L0_xattn_bq_c, L0_xattn_Wk_s, L0_xattn_bk_s, L0_xattn_Wv_s, L0_xattn_bv_s, L0_xattn_Wq_s, L0_xattn_bq_s, L0_xattn_Wk_c, L0_xattn_bk_c, L0_xattn_Wv_c, L0_xattn_bv_c, L0_xattn_Wg, L0_xattn_bg)
    x = x + jnp.tanh(g_ffn[0]) * _L0_ffn_ref(_layernorm(x, axis=-1), L0_ffn_w1, L0_ffn_conv_w, L0_ffn_conv_b, L0_ffn_w2)
    x = x + jnp.tanh(g_xattn[1]) * _L1_xattn_ref(_layernorm(x, axis=-1), ctx_1024, L1_xattn_gamma, L1_xattn_beta, L1_xattn_Wqr, L1_xattn_bqr, L1_xattn_Wqi, L1_xattn_bqi, L1_xattn_Wkr, L1_xattn_bkr, L1_xattn_Wki, L1_xattn_bki, L1_xattn_Wvr, L1_xattn_bvr, L1_xattn_Wvi, L1_xattn_bvi, L1_xattn_Wo)
    x = x + jnp.tanh(g_ffn[1]) * _L1_ffn_ref(_layernorm(x, axis=-1), L1_ffn_weight, L1_ffn_alpha, L1_ffn_bias)
    x = x + jnp.tanh(g_xattn[2]) * _L2_xattn_ref(_layernorm(x, axis=-1), ctx_1024, mask_SxS2_ff0, mask_BxS2_bf0, L2_xattn_Wq, L2_xattn_Wk, L2_xattn_Wv, L2_xattn_Wo)
    x = x + jnp.tanh(g_ffn[2]) * _L2_ffn_ref(_layernorm(x, axis=-1), L2_ffn_Wr, L2_ffn_br, L2_ffn_W1, L2_ffn_b1, L2_ffn_W2, L2_ffn_b2)
    x = x + jnp.tanh(g_xattn[3]) * _L3_xattn_ref(_layernorm(x, axis=-1), ctx_1024, ctx_1024, mask_1x1xSxS2_bk0, L3_xattn_W_q, L3_xattn_b_q, L3_xattn_W_k, L3_xattn_b_k, L3_xattn_W_v, L3_xattn_b_v, L3_xattn_W_o, L3_xattn_b_o)
    x = x + jnp.tanh(g_ffn[3]) * _L3_ffn_ref(_layernorm(x, axis=-1), L3_ffn_wf, L3_ffn_uf, L3_ffn_bf, L3_ffn_wi, L3_ffn_ui, L3_ffn_bi, L3_ffn_wc, L3_ffn_uc, L3_ffn_bc, L3_ffn_wo, L3_ffn_uo, L3_ffn_bo, L3_ffn_in_c)
    return x

_drawn_inputs = setup_inputs


def setup_inputs(seed=0):
    import zlib

    import numpy as np

    out = dict(_drawn_inputs(seed))
    spreads = {'mask_SxS2_ff0': (0.0, 2.0),
     'L1_xattn_gamma': (1.0, 0.6),
     'L1_xattn_beta': (0.0, 0.8),
     'L2_ffn_br': (0.0, 0.74),
     'L2_ffn_b1': (0.0, 2.0),
     'L2_ffn_b2': (0.0, 0.8),
     'L3_xattn_b_q': (0.0, 2.0),
     'L3_xattn_b_k': (0.0, 2.0),
     'L3_xattn_b_v': (0.0, 0.8),
     'L3_xattn_b_o': (0.0, 0.8),
     'L3_ffn_bf': (0.0, 2.0),
     'L3_ffn_bi': (0.0, 2.0),
     'L3_ffn_bc': (0.0, 2.0),
     'L3_ffn_bo': (0.0, 0.8),
     'L3_ffn_in_c': (0.0, 0.8)}
    factors = {'L0_xattn_Wq_c': 8.0,
     'L0_xattn_bq_c': 8.0,
     'L0_xattn_Wk_s': 8.0,
     'L0_xattn_bk_s': 64.0,
     'L0_xattn_bv_s': 6.907,
     'L0_xattn_Wq_s': 8.0,
     'L0_xattn_bq_s': 8.0,
     'L0_xattn_Wk_c': 8.0,
     'L0_xattn_bk_c': 64.0,
     'L0_xattn_Wv_c': 8.0,
     'L0_xattn_bv_c': 6.882,
     'L0_xattn_Wg': 8.0,
     'L0_xattn_bg': 8.0,
     'L1_xattn_Wqr': 8.0,
     'L1_xattn_bqr': 8.0,
     'L1_xattn_Wqi': 8.0,
     'L1_xattn_bqi': 8.0,
     'L1_xattn_Wkr': 8.0,
     'L1_xattn_bkr': 64.0,
     'L1_xattn_Wki': 8.0,
     'L1_xattn_bki': 64.0,
     'L1_xattn_Wvr': 4.211,
     'L1_xattn_bvr': 33.359,
     'L1_xattn_Wvi': 6.728,
     'L1_xattn_bvi': 8.0,
     'L1_xattn_Wo': 3.167,
     'L1_ffn_bias': 8.0,
     'L2_xattn_Wq': 3.729,
     'L2_xattn_Wk': 3.742,
     'L3_xattn_W_q': 2.712,
     'L3_ffn_wf': 8.0,
     'L3_ffn_uf': 8.0,
     'L3_ffn_wi': 5.969,
     'L3_ffn_ui': 8.0,
     'L3_ffn_uc': 5.277}
    for name, (base, spread) in spreads.items():
        noise = np.random.default_rng([zlib.crc32(name.encode()), seed]).standard_normal(out[name].shape)
        drawn = base * np.exp(spread * noise) if base else spread * noise
        out[name] = jnp.asarray(drawn.astype(out[name].dtype))
    for name, factor in factors.items():
        out[name] = (out[name] * factor).astype(out[name].dtype)
    return out
```

```python
from contextlib import ExitStack

import numpy as np

import concourse.bass as bass
from concourse import mybir

F32 = mybir.dt.float32
BF16 = mybir.dt.bfloat16
I32 = mybir.dt.int32
U32 = mybir.dt.uint32
U8 = mybir.dt.uint8
ALU = mybir.AluOpType
ACT = mybir.ActivationFunctionType
AX = mybir.AxisListType

P = 128
B, S, D = 4, 1024, 256
T = B * S // P
TB = S // P
DC = D // P
SK = 77
HEADS, HD = 16, 16
HH = HEADS // DC
EPS = 1e-5
AHEAD = 2
MAGIC = 1.5 * 2.0 ** 23

STAGES = list(range(8))


def ds(start, size):
    return bass.ds(start, size)


def ev(t, n=1, k=None, back=0):
    return t * n + (AHEAD - back) * n + (n if k is None else k)


def pipeline(eng, n, parts):
    lead = max(x for _, x in parts)
    lead += lead % 2

    def step(s):
        for part, x in parts:
            if 0 <= s + x < n:
                part(s + x, (s + x) % 2)

    for s in range(-lead, 0):
        step(s)
    with eng.Fori(0, (n - lead) // 2) as i:
        for v in range(2):
            for part, x in parts:
                part(i * 2 + (v + x), (v + x) % 2)
    for s in range(n - lead, n):
        step(s)


class Chain:

    def __init__(self, eng, sem, start=0):
        self.eng, self.sem, self.n = eng, sem, start

    def link(self, ins):
        ins.then_inc(self.sem, 1)
        self.n = self.n + 1
        self.eng.wait_ge(self.sem, self.n)


class TileChain(Chain):

    def __init__(self, eng, sem, t, per, first=0):
        super().__init__(eng, sem)
        self.t, self.per, self.n = t, per, first

    def link(self, ins):
        ins.then_inc(self.sem, 1)
        self.n += 1
        assert self.n <= self.per
        self.eng.wait_ge(self.sem, self.t * self.per + self.n)


class Names(dict):

    def __getattr__(self, name):
        return self[name]

    def __setattr__(self, name, value):
        self[name] = value


def scope(nc, name):
    ctx = ExitStack()
    g = Names(ctx=ctx)
    sems = []

    def end():
        if sems:
            nc.clear_and_free_semaphores(sems)
            nc.all_engine_barrier()

    def sem(n):
        sems.append(nc.alloc_semaphore(name=f"{name}_{n}"))
        return sems[-1]

    ctx.callback(end)
    g.sb = lambda n, shape, dt=F32: ctx.enter_context(nc.sbuf_tensor(f"{name}_{n}", shape, dt))
    g.ps = lambda n, shape, dt=F32: ctx.enter_context(nc.psum_tensor(f"{name}_{n}", shape, dt))
    g.sem = sem
    return g


def weight_view(w):
    return w.rearrange("(c p) o -> p c o", p=P)



def norm_vector(nc, dve, sh, s):
    c = Chain(dve, s.norm_step)
    st = sh.stats[:, :].rearrange("p (t s) -> p t s", s=6)
    me, mo, qe, qo = st[:, :, 1], st[:, :, 4], st[:, :, 2], st[:, :, 5]
    a, v = sh.norm_a[:, :], sh.var[:, :]
    c.link(nc.vector.tensor_tensor(a, me, mo, ALU.subtract))
    c.link(nc.vector.scalar_tensor_tensor(a, a, D / 4.0, a, ALU.mult, ALU.mult))
    c.link(nc.vector.tensor_tensor(v, qe, qo, ALU.add))
    c.link(nc.vector.tensor_tensor(v, v, a, ALU.add))
    c.link(nc.vector.tensor_scalar(v, v, 1.0 / D, None, ALU.mult))
    c.link(nc.vector.tensor_scalar(sh.vare[:, :], v, EPS, None, ALU.add))
    c.link(nc.vector.tensor_tensor(sh.mean[:, :], me, mo, ALU.add))
    nc.vector.tensor_scalar(sh.mean[:, :], sh.mean[:, :], 0.5, None, ALU.mult).then_inc(s.var_ready, 1)
    dve.wait_ge(s.var_ready, 1)
    dve.wait_ge(s.pow_ready, 2)
    newton(nc, c, sh.rstd[:, :], sh.vare[:, :], a)
    c.link(nc.vector.scalar_tensor_tensor(sh.shift[:, :], sh.mean[:, :], -1.0, sh.rstd[:, :], ALU.mult, ALU.mult))
    return c


def newton(nc, c, r, v, a):
    c.link(nc.vector.tensor_tensor(a, r, r, ALU.mult))
    c.link(nc.vector.scalar_tensor_tensor(a, a, -0.5, v, ALU.mult, ALU.mult))
    c.link(nc.vector.scalar_tensor_tensor(r, a, 1.5, r, ALU.add, ALU.mult))


def norm_gpsimd(nc, pool, sh, s):
    nc.gpsimd.memset(sh.half[:, :], -0.5).then_inc(s.pow_ready, 1)
    pool.wait_ge(s.pow_ready, 1)
    pool.wait_ge(s.var_ready, 1)
    nc.gpsimd.tensor_tensor(sh.rstd[:, :], sh.vare[:, :], sh.half[:, :], ALU.pow).then_inc(s.pow_ready, 1)


def norm_sems(s):
    s.norm_step, s.var_ready, s.pow_ready = s.sem("norm_step"), s.sem("var_ready"), s.sem("pow_ready")


def x_tile(sh, t):
    return sh.x[:, ds(t * D, D)]


def normalise(nc, sh, out, t):
    return nc.vector.tensor_scalar(out, x_tile(sh, t), sh.rstd[:, ds(t, 1)], sh.shift[:, ds(t, 1)],
                                   ALU.mult, ALU.add)


def tile_stats(nc, sh, t):
    return nc.vector.bn_stats(sh.stats[:, ds(t * 6, 6)], x_tile(sh, t))


def stage_l0_ffn(nc, io, sh):
    s = scope(nc, "l0f")
    HID = 4 * D
    M = HID // P
    with s.ctx:
        norm_sems(s)
        w1, w2 = s.sb("w1", [P, DC, HID]), s.sb("w2", [P, M, D])
        w1q, w2q = s.sb("w1q", [P, DC, HID], BF16), s.sb("w2q", [P, M, D], BF16)
        wsum, wscale, wmean = s.sb("wsum", [P, 2]), s.sb("wscale", [P, 2]), s.sb("wmean", [P, 2])
        cw, cb = s.sb("cw", [P, M, 3]), s.sb("cb", [P, M])
        xn = s.sb("xn", [P, TB, D])
        am, sc, inv1, inv2 = (s.sb(n, [P, TB]) for n in ("am", "sc", "inv1", "inv2"))
        q1 = s.sb("q1", [P, 2, D], BF16)
        qt = s.sb("qt", [P, DC, S], BF16)
        dg = s.sb("dg", [P, 2, P])
        invb = s.sb("invb", [P, S])
        hs = s.sb("hs", [P, 2, S + 2])
        a = s.sb("a", [P, 2, S])
        z = s.sb("z", [P, M, S])
        q2 = s.sb("q2", [P, M, S], BF16)
        amax = s.sb("amax", [P, S])
        az = s.sb("az", [P, 2, S])
        scaled = s.sb("scaled", [P, 2, S])
        hb = [s.ps(f"hb{k}", [P, S]) for k in range(2)]
        bc = s.ps("bc", [P, S])
        b6, b7 = s.ps("b6", [P, 512]), s.ps("b7", [P, 512])
        for n in ["w_loaded", "small_loaded", "wsum_ready", "wtot_ps", "set_step", "wq_ready", "xn_step", "q1_ready", "qt_ps", "qt_ready",
                  "dg_ready", "inv_ps", "invb_ready", "h_ps", "hs_ready", "a_ready", "conv_ready", "z_ready", "step",
                  "amax_ready", "abs_ready", "am_ps", "dg2_ready", "bc_ps", "scaled_ready", "q2_ready", "y_ps", "x_ready", "stats_ready"]:
            s[n] = s.sem(n)
        tg = sh.gates[:, 4:5]

        with nc.Block() as block:
            @block.sync
            def _(sp):
                sp.dma_start(w1[:, :, :], io.L0_ffn_w1_T.rearrange("(c p) o -> p c o", p=P)).then_inc(s.w_loaded, 16)
                sp.dma_start(w2[:, :, :], io.L0_ffn_w2_T.rearrange("(c p) o -> p c o", p=P)).then_inc(s.w_loaded, 16)
                sp.dma_start(cw[:, :, :], io.L0_ffn_conv_w.rearrange("(m p) a k -> p m (a k)", p=P)).then_inc(s.small_loaded, 16)
                sp.dma_start(cb[:, :], io.L0_ffn_conv_b_cols).then_inc(s.small_loaded, 16)

            @block.vector
            def _(dve):
                c = norm_vector(nc, dve, sh, s)
                dve.wait_ge(s.w_loaded, 32)
                for n, w in enumerate((w1, w2)):
                    nc.vector.tensor_reduce(wsum[:, n:n + 1], w[:, :, :], AX.XY, ALU.add, apply_absolute_value=True).then_inc(s.wsum_ready, 1)
                dve.wait_ge(s.wtot_ps, 1)
                c.link(nc.vector.tensor_scalar(wmean[:, :], b6[:, 0:2], 1.0 / (HID * D), 1e-5, ALU.mult, ALU.max))
                c.link(nc.vector.reciprocal(wscale[:, :], wmean[:, :]))
                for n, (w, q) in enumerate(((w1, w1q), (w2, w2q))):
                    c.link(nc.vector.tensor_scalar(w[:, :, :], w[:, :, :], wscale[:, n:n + 1], MAGIC, ALU.mult, ALU.add))
                    c.link(nc.vector.tensor_scalar(w[:, :, :], w[:, :, :], MAGIC, 1.0, ALU.subtract, ALU.min))
                    nc.vector.tensor_scalar(q[:, :, :], w[:, :, :], -1.0, None, ALU.max).then_inc(s.wq_ready, 1)
                c.link(nc.vector.tensor_scalar(wmean[:, 0:1], wmean[:, 0:1], 1.0 / 127.0, None, ALU.mult))
                c.link(nc.vector.tensor_scalar(wmean[:, 1:2], wmean[:, 1:2], 1.0 / 127.0, tg, ALU.mult, ALU.mult))
                c.link(nc.vector.memset(hs[:, :, :], 0.0))
                dve.wait_ge(s.small_loaded, 32)
                PER = 40

                with dve.Fori(0, B) as b:
                    k = TileChain(dve, s.step, b, PER)
                    for j in range(TB):
                        normalise(nc, sh, xn[:, j, :], b * TB + j).then_inc(s.xn_step, 1)
                    dve.wait_ge(s.xn_step, b * TB + TB)
                    k.link(nc.vector.tensor_reduce(am[:, :], xn[:, :, :], AX.X, ALU.max, apply_absolute_value=True))
                    k.link(nc.vector.tensor_scalar(am[:, :], am[:, :], 1e-5, None, ALU.max))
                    k.link(nc.vector.reciprocal(sc[:, :], am[:, :]))
                    k.link(nc.vector.tensor_scalar(sc[:, :], sc[:, :], 127.0, None, ALU.mult))
                    k.link(nc.vector.tensor_scalar(inv1[:, :], am[:, :], wmean[:, 0:1], None, ALU.mult))
                    for j in range(TB):
                        n = b * TB + j
                        k.link(nc.vector.tensor_scalar(xn[:, j, :], xn[:, j, :], sc[:, j:j + 1], MAGIC, ALU.mult, ALU.add))
                        if j >= 2:
                            dve.wait_ge(s.qt_ps, n - 1)
                            dve.wait_ge(s.inv_ps, n - 1)
                        nc.vector.tensor_scalar(q1[:, j % 2, :], xn[:, j, :], MAGIC, 127.0, ALU.subtract, ALU.min).then_inc(s.q1_ready, 1)
                        nc.vector.tensor_scalar(dg[:, j % 2, :], sh.ident[:, :], inv1[:, j:j + 1], None, ALU.mult).then_inc(s.dg_ready, 1)

                    def scale_h(m):
                        dve.wait_ge(s.h_ps, b * M + (m + 1))
                        nc.vector.tensor_tensor(hs[:, m % 2, 1:S + 1], hb[m % 2][:, :], invb[:, :], ALU.mult).then_inc(s.hs_ready, 1)

                    def conv(m):
                        dve.wait_ge(s.a_ready, b * M + (m + 1))
                        k.link(nc.vector.scalar_tensor_tensor(a[:, m % 2, :], hs[:, m % 2, 0:S], cw[:, m, 0:1], a[:, m % 2, :],
                                                              ALU.mult, ALU.add))
                        nc.vector.scalar_tensor_tensor(a[:, m % 2, :], hs[:, m % 2, 2:S + 2], cw[:, m, 2:3], a[:, m % 2, :],
                                                       ALU.mult, ALU.add).then_inc(s.conv_ready, 1)
                        dve.wait_ge(s.conv_ready, b * M + (m + 1))

                    def largest(m):
                        dve.wait_ge(s.abs_ready, b * M + (m + 1))
                        if m == 0:
                            nc.vector.tensor_copy(amax[:, :], az[:, m % 2, :]).then_inc(s.amax_ready, 1)
                        else:
                            nc.vector.tensor_tensor(amax[:, :], az[:, m % 2, :], amax[:, :], ALU.max).then_inc(s.amax_ready, 1)
                        dve.wait_ge(s.amax_ready, b * M + (m + 1))

                    dve.wait_ge(s.invb_ready, b + 1)
                    scale_h(0)
                    for m in range(M):
                        if m + 1 < M:
                            scale_h(m + 1)
                        conv(m)
                        if m:
                            largest(m - 1)
                    largest(M - 1)
                    dve.wait_ge(s.am_ps, b + 1)
                    k.link(nc.vector.tensor_reduce(am[:, :], hb[0][:, :].rearrange("p (t n) -> p t n", n=P), AX.X, ALU.max))
                    k.link(nc.vector.tensor_scalar(am[:, :], am[:, :], 1e-5, None, ALU.max))
                    k.link(nc.vector.reciprocal(sc[:, :], am[:, :]))
                    k.link(nc.vector.tensor_scalar(sc[:, :], sc[:, :], 127.0, None, ALU.mult))
                    k.link(nc.vector.tensor_scalar(inv2[:, :], am[:, :], wmean[:, 1:2], None, ALU.mult))
                    for j in range(TB):
                        if j >= 2:
                            dve.wait_ge(s.bc_ps, b * TB + (j - 1))
                        nc.vector.tensor_scalar(dg[:, j % 2, :], sh.ident[:, :], sc[:, j:j + 1], None, ALU.mult).then_inc(s.dg2_ready, 1)
                    dve.wait_ge(s.bc_ps, b * TB + TB)
                    for m in range(M + 1):
                        if m < M:
                            nc.vector.tensor_tensor(scaled[:, m % 2, :], z[:, m, :], bc[:, :], ALU.mult).then_inc(s.scaled_ready, 1)
                        if m:
                            dve.wait_ge(s.scaled_ready, b * M + m)
                            nc.vector.tensor_scalar(q2[:, m - 1, :], scaled[:, (m - 1) % 2, :], MAGIC, MAGIC,
                                                    ALU.add, ALU.subtract).then_inc(s.q2_ready, 1)
                            if m < M:
                                dve.wait_ge(s.q2_ready, b * M + m)
                    for j in range(TB):
                        n = b * TB + j
                        dve.wait_ge(s.y_ps, n + 1)
                        nc.vector.scalar_tensor_tensor(x_tile(sh, n), (b6, b7)[j % 2][:, 0:D], inv2[:, j:j + 1], x_tile(sh, n),
                                                       ALU.mult, ALU.add).then_inc(s.x_ready, 1)
                        dve.wait_ge(s.x_ready, n + 1)
                        tile_stats(nc, sh, n).then_inc(s.stats_ready, 1)
                    assert k.n <= PER
                    if k.n < PER:
                        dve.sem_inc(s.step, PER - k.n)
                dve.wait_ge(s.stats_ready, T)

            @block.gpsimd
            def _(pool):
                norm_gpsimd(nc, pool, sh, s)

            @block.tensor
            def _(pe):
                pe.wait_ge(s.wsum_ready, 2)
                nc.tensor.matmul(b6[:, 0:2], sh.ones[:, :], wsum[:, :], start=True, stop=True).then_inc(s.wtot_ps, 1)
                pe.wait_ge(s.wq_ready, 2)
                with pe.Fori(0, B) as b:
                    for j in range(TB):
                        n = b * TB + j
                        pe.wait_ge(s.q1_ready, n + 1)
                        if j >= 2:
                            pe.wait_ge(s.qt_ready, n - 1)
                        bank = (b6, b7)[j % 2][:, :].bitcast(BF16)
                        for c in range(DC):
                            ins = nc.tensor.transpose(bank[:, c * P:(c + 1) * P], q1[:, j % 2, c * P:(c + 1) * P], sh.identb[:, :])
                        ins.then_inc(s.qt_ps, 1)
                        pe.wait_ge(s.dg_ready, n + 1)
                        nc.tensor.matmul(bc[:, j * P:(j + 1) * P], sh.ones[:, :], dg[:, j % 2, :], start=True, stop=True).then_inc(s.inv_ps, 1)
                    pe.wait_ge(s.qt_ready, b * TB + TB)
                    for m in range(M):
                        if m >= 2:
                            pe.wait_ge(s.hs_ready, b * M + (m - 1))
                        for j in range(2):
                            for c in range(DC):
                                ins = nc.tensor.matmul(hb[m % 2][:, j * 512:(j + 1) * 512], w1q[:, c, m * P:(m + 1) * P],
                                                       qt[:, c, j * 512:(j + 1) * 512], start=(c == 0), stop=(c == DC - 1))
                        ins.then_inc(s.h_ps, 1)
                    pe.wait_ge(s.amax_ready, b * M + M)
                    for j in range(TB):
                        ins = nc.tensor.transpose(hb[0][:, j * P:(j + 1) * P], amax[:, j * P:(j + 1) * P], sh.ident[:, :])
                    ins.then_inc(s.am_ps, 1)
                    for j in range(TB):
                        pe.wait_ge(s.dg2_ready, b * TB + (j + 1))
                        nc.tensor.matmul(bc[:, j * P:(j + 1) * P], sh.ones[:, :], dg[:, j % 2, :], start=True, stop=True).then_inc(s.bc_ps, 1)
                    pe.wait_ge(s.q2_ready, b * M + M)
                    for j in range(TB):
                        if j >= 2:
                            pe.wait_ge(s.x_ready, b * TB + (j - 1))
                        for m in range(M):
                            ins = nc.tensor.matmul((b6, b7)[j % 2][:, 0:D], q2[:, m, j * P:(j + 1) * P], w2q[:, m, :],
                                                   start=(m == 0), stop=(m == M - 1))
                        ins.then_inc(s.y_ps, 1)

            @block.scalar
            def _(act):
                act.wait_ge(s.small_loaded, 32)
                with act.Fori(0, B) as b:
                    for j in range(TB):
                        n = b * TB + j
                        act.wait_ge(s.qt_ps, n + 1)
                        bank = (b6, b7)[j % 2][:, :].bitcast(BF16)
                        nc.scalar.activation(qt[:, :, j * P:(j + 1) * P], bank[:, 0:D].rearrange("p (c n) -> p c n", c=DC),
                                             ACT.Copy).then_inc(s.qt_ready, 1)
                    act.wait_ge(s.inv_ps, b * TB + TB)
                    nc.scalar.activation(invb[:, :], bc[:, :], ACT.Copy).then_inc(s.invb_ready, 1)

                    def centre(m):
                        act.wait_ge(s.hs_ready, b * M + (m + 1))
                        if m >= 2:
                            act.wait_ge(s.z_ready, b * M + (m - 1))
                        nc.scalar.activation(a[:, m % 2, :], hs[:, m % 2, 1:S + 1], ACT.Identity, scale=cw[:, m, 1:2],
                                             bias=cb[:, m:m + 1]).then_inc(s.a_ready, 1)

                    centre(0)
                    for m in range(M):
                        if m + 1 < M:
                            centre(m + 1)
                        act.wait_ge(s.conv_ready, b * M + (m + 1))
                        nc.scalar.activation(z[:, m, :], a[:, m % 2, :], ACT.Silu).then_inc(s.z_ready, 1)
                        act.wait_ge(s.z_ready, b * M + (m + 1))
                        if m >= 2:
                            act.wait_ge(s.amax_ready, b * M + (m - 1))
                        nc.scalar.activation(az[:, m % 2, :], z[:, m, :], ACT.Abs).then_inc(s.abs_ready, 1)


def stage_l0_xattn(nc, io, sh):
    s = scope(nc, "l0x")
    SC = D ** -0.5
    GT = 4
    GW = GT * SK
    NG = TB // GT
    with s.ctx:
        norm_sems(s)
        names = ["wk_s", "wv_s", "wq_s", "wv_c", "wq", "wk"]
        w = {n: s.sb(n, [P, DC, D]) for n in names}
        wg = s.sb("wg", [P, 2 * DC, D])
        bq, bks, bqs, bkc = (s.sb(n, [P, DC]) for n in ("bq", "bks", "bqs", "bkc"))
        bvs_c, bvc_c = s.sb("bvs_c", [P, DC]), s.sb("bvc_c", [P, DC])
        bvs, bvc, bgr = s.sb("bvs", [SK, D]), s.sb("bvc", [SK, D]), s.sb("bgr", [SK, D])
        interp = s.sb("interp", [SK, S])
        bqb = s.sb("bqb", [P, DC, P])
        kst, qst, vst = (s.sb(n, [P, DC, B * SK]) for n in ("kst", "qst", "vst"))
        keys, queries = s.sb("keys", [P, DC * B * SK]), s.sb("queries", [P, DC, B * SK])
        crow = s.sb("crow", [P, B * SK])
        beta = s.sb("beta", [SK, B])
        r1 = s.sb("r1", [SK, B * 2 * D])
        qb = s.sb("qb", [P, DC, SK])
        xn = s.sb("xn", [P, TB, D])
        xt = s.sb("xt", [P, DC, S])
        p2 = s.sb("p2", [SK, S])
        m2, nb2, sum2, inv2 = (s.sb(n, [SK, 1]) for n in ("m2", "nb2", "sum2", "inv2"))
        p2t = s.sb("p2t", [P, TB, SK])
        uu = s.sb("uu", [SK, D])
        ut = s.sb("ut", [P, DC, SK])
        sct = s.sb("sct", [P, DC, SK])
        sc = s.sb("sc", [SK, D])
        r2 = s.sb("r2", [SK, 2 * D])
        r3 = s.sb("r3", [SK, D])
        p1 = s.sb("p1", [P, TB, SK])
        mx, rs, ri = (s.sb(n, [P, TB]) for n in ("mx", "rs", "ri"))
        p1t = s.sb("p1t", [SK, TB, P])
        th = s.sb("th", [P, 2, D])
        tmp = s.sb("tmp", [P, 2, D])
        halfg = s.sb("halfg", [P, 2])
        s2_bank = s.ps("s2_bank", [P, S])
        b0, b1 = s.ps("b0", [P, 512]), s.ps("b1", [P, 512])
        b4, b5 = s.ps("b4", [P, 512]), s.ps("b5", [P, 512])
        b6, b7 = s.ps("b6", [P, 512]), s.ps("b7", [P, 512])
        for n in ["w_loaded", "small_loaded", "set_ready", "pre_ps", "pre_ready", "fold_ps", "fold_ready", "v_ps", "r1_ready", "r1_step",
                  "xn_ready", "xt_ps", "xt_ready", "qb_ready", "s2_ps", "step", "nb2_ready", "e2_ready",
                  "s1_ps", "shift_ready", "e1_ready", "inv1_ready", "p1_ready", "p2t_ps", "p2t_ready", "u_ps",
                  "u_ready", "ut_ps", "ut_ready", "sc_ps", "sct_ready", "sg_ps", "r2_ready", "p1t_ps", "p1t_ready",
                  "c_ps", "th_ready", "x_ready", "stats_ready"]:
            s[n] = s.sem(n)
        tg = sh.gates[:, 0:1]

        with nc.Block() as block:
            @block.sync
            def _(sp):
                for n, src in (("wk_s", "L0_xattn_Wk_s_T"), ("wq_s", "L0_xattn_Wq_s_T"), ("wv_s", "L0_xattn_Wv_s_T"),
                               ("wq", "L0_xattn_Wq_c"), ("wk", "L0_xattn_Wk_c"), ("wv_c", "L0_xattn_Wv_c_T")):
                    sp.dma_start(w[n][:, :, :], weight_view(io[src])).then_inc(s.w_loaded, 16)
                sp.dma_start(wg[:, :, :], weight_view(io.L0_xattn_Wg_T)).then_inc(s.w_loaded, 16)
                for a, n in ((bq, "bq_c"), (bks, "bk_s"), (bqs, "bq_s"), (bkc, "bk_c"), (bvs_c, "bv_s"), (bvc_c, "bv_c")):
                    sp.dma_start(a[:, :], io[f"L0_xattn_{n}_cols"]).then_inc(s.small_loaded, 16)
                for a, n in ((bvs, "bv_s"), (bvc, "bv_c"), (bgr, "bg")):
                    sp.dma_start(a[:, :], io[f"L0_xattn_{n}"].partition_broadcast(SK)).then_inc(s.small_loaded, 16)
                sp.dma_start(interp[:, :], io.interpolate).then_inc(s.small_loaded, 16)

            @block.vector
            def _(dve):
                c = norm_vector(nc, dve, sh, s)
                dve.wait_ge(s.small_loaded, 160)
                nc.vector.tensor_copy(bqb[:, :, :], bq[:, :].unsqueeze(2).to_broadcast((P, DC, P))).then_inc(s.set_ready, 1)
                c.link(nc.vector.tensor_scalar(halfg[:, 0:1], tg, 0.5, None, ALU.mult))
                c.link(nc.vector.tensor_scalar(halfg[:, 1:2], tg, -0.5, None, ALU.mult))
                dve.wait_ge(s.fold_ps, 5)
                c.link(nc.vector.tensor_scalar(crow[:, :], b4[:, 0:B * SK], SC, None, ALU.mult))
                nc.vector.tensor_scalar(beta[:, :], b5[0:SK, 0:B], SC, None, ALU.mult).then_inc(s.set_ready, 1)
                for b in range(B):
                    dve.wait_ge(s.v_ps, b + 1)
                    at = b * 2 * D
                    c.link(nc.vector.tensor_tensor(r1[:, at:at + D], (b6, b7)[b % 2][0:SK, 0:D], bvs[:, :], ALU.add))
                    c.link(nc.vector.tensor_scalar(r1[:, at:at + D], r1[:, at:at + D], halfg[0:SK, 0:1], None, ALU.mult))
                    nc.vector.tensor_copy(r1[:, at + D:at + 2 * D], (b6, b7)[b % 2][0:SK, D:2 * D]).then_inc(s.r1_ready, 1)
                dve.sem_inc(s.x_ready, 2)
                dve.wait_ge(s.fold_ready, 2 * DC)
                dve.wait_ge(s.r1_ready, B)
                PER = 30

                with dve.Fori(0, B) as b:
                    k = TileChain(dve, s.step, b, PER)
                    for j in range(TB):
                        normalise(nc, sh, xn[:, j, :], b * TB + j).then_inc(s.xn_ready, 1)
                    for kk in range(DC):
                        nc.vector.tensor_copy(qb[:, kk, :], queries[:, kk, ds(b * SK, SK)]).then_inc(s.qb_ready, 1)
                    dve.wait_ge(s.s2_ps, b + 1)
                    k.link(nc.vector.tensor_reduce(m2[:, :], s2_bank[0:SK, :], AX.X, ALU.max))
                    k.link(nc.vector.tensor_tensor(m2[:, :], m2[:, :], beta[:, ds(b, 1)], ALU.add))
                    nc.vector.tensor_tensor(nb2[:, :], beta[:, ds(b, 1)], m2[:, :], ALU.subtract).then_inc(s.nb2_ready, 1)
                    for g in range(NG):
                        bank = (b4, b5)[g]
                        pg = p1[:, g * GT:(g + 1) * GT, :]
                        dve.wait_ge(s.s1_ps, b * NG + (g + 1))
                        k.link(nc.vector.tensor_tensor(pg, bank[:, 0:GW].rearrange("p (h k) -> p h k", k=SK),
                                                       crow[:, ds(b * SK, SK)].unsqueeze(1).to_broadcast((P, GT, SK)), ALU.add))
                        k.link(nc.vector.tensor_reduce(mx[:, g * GT:(g + 1) * GT], pg, AX.X, ALU.max))
                        nc.vector.tensor_tensor(pg, pg, mx[:, g * GT:(g + 1) * GT].unsqueeze(2).to_broadcast((P, GT, SK)),
                                                ALU.subtract).then_inc(s.shift_ready, 1)
                    for g in range(NG):
                        pg = p1[:, g * GT:(g + 1) * GT, :]
                        dve.wait_ge(s.e1_ready, b * NG + (g + 1))
                        k.link(nc.vector.tensor_reduce(rs[:, g * GT:(g + 1) * GT], pg, AX.X, ALU.add))
                        nc.vector.reciprocal(ri[:, g * GT:(g + 1) * GT], rs[:, g * GT:(g + 1) * GT]).then_inc(s.inv1_ready, 1)
                    dve.wait_ge(s.e2_ready, b + 1)
                    k.link(nc.vector.reciprocal(inv2[:, :], sum2[:, :]))
                    dve.wait_ge(s.u_ps, b + 1)
                    nc.vector.tensor_scalar(uu[:, :], b6[0:SK, 0:D], inv2[:, 0:1], None, ALU.mult).then_inc(s.u_ready, 1)
                    dve.wait_ge(s.sc_ps, b + 1)
                    k.link(nc.vector.tensor_tensor(sc[:, :], b6[0:SK, 0:D], bvc[:, :], ALU.add))
                    k.link(nc.vector.tensor_scalar(r2[:, 0:D], sc[:, :], halfg[0:SK, 1:2], None, ALU.mult))
                    k.link(nc.vector.tensor_scalar(r3[:, :], sc[:, :], sh.gates[0:SK, 0:1], None, ALU.mult))
                    dve.wait_ge(s.sg_ps, b + 1)
                    nc.vector.tensor_tensor(r2[:, D:2 * D], b7[0:SK, 0:D], bgr[:, :], ALU.add).then_inc(s.r2_ready, 1)
                    for j in range(TB):
                        u = j % 2
                        n = b * TB + j
                        dve.wait_ge(s.th_ready, n + 1)
                        k.link(nc.vector.scalar_tensor_tensor(tmp[:, u, :], th[:, u, :], 1.0, s2_bank[:, u * 512:u * 512 + D],
                                                              ALU.add, ALU.mult))
                        k.link(nc.vector.tensor_tensor(tmp[:, u, :], tmp[:, u, :], (b0, b1)[u][:, 0:D], ALU.add))
                        nc.vector.tensor_tensor(x_tile(sh, n), tmp[:, u, :], x_tile(sh, n), ALU.add).then_inc(s.x_ready, 1)
                        dve.wait_ge(s.x_ready, n + 3)
                        tile_stats(nc, sh, n).then_inc(s.stats_ready, 1)
                    assert k.n <= PER
                    if k.n < PER:
                        dve.sem_inc(s.step, PER - k.n)
                dve.wait_ge(s.stats_ready, T)

            @block.gpsimd
            def _(pool):
                norm_gpsimd(nc, pool, sh, s)
                with pool.Fori(0, B) as b:
                    for g in range(NG):
                        pg = p1[:, g * GT:(g + 1) * GT, :]
                        pool.wait_ge(s.inv1_ready, b * NG + (g + 1))
                        nc.gpsimd.tensor_tensor(pg, pg, ri[:, g * GT:(g + 1) * GT].unsqueeze(2).to_broadcast((P, GT, SK)),
                                                ALU.mult).then_inc(s.p1_ready, 1)

            @block.tensor
            def _(pe):
                pe.wait_ge(s.w_loaded, 112)
                for n, (name, at) in enumerate((("wk_s", 0), ("wq_s", 1), ("wv_s", 2))):
                    for m in range(DC):
                        bank = [b0, b1, b4, b5, b6, b7][2 * n + m]
                        for k in range(DC):
                            ins = nc.tensor.matmul(bank[:, 0:B * SK], w[name][:, k, m * P:(m + 1) * P], sh.ctx_t[:, k, :],
                                                   start=(k == 0), stop=(k == DC - 1))
                        ins.then_inc(s.pre_ps, 1)
                pe.wait_ge(s.pre_ready, 6)
                for n, (name, src) in enumerate((("wq", kst), ("wk", qst))):
                    for m in range(DC):
                        bank = (b0, b1)[m] if n == 0 else s2_bank[:, m * 512:(m + 1) * 512]
                        for k in range(DC):
                            ins = nc.tensor.matmul(bank[:, 0:B * SK], w[name][:, k, m * P:(m + 1) * P], src[:, k, :],
                                                   start=(k == 0), stop=(k == DC - 1))
                        ins.then_inc(s.fold_ps, 1)
                pe.wait_ge(s.set_ready, 1)
                for k in range(DC):
                    nc.tensor.matmul(b4[:, 0:B * SK], bqb[:, k, :], kst[:, k, :], start=(k == 0), stop=(k == DC - 1))
                for b in range(B):
                    for k in range(DC):
                        ins = nc.tensor.matmul(b5[0:SK, b:b + 1], qst[:, k, b * SK:(b + 1) * SK], bkc[:, k:k + 1],
                                               start=(k == 0), stop=(k == DC - 1))
                ins.then_inc(s.fold_ps, 1)
                for b in range(B):
                    bank = (b6, b7)[b % 2]
                    if b >= 2:
                        pe.wait_ge(s.r1_ready, b - 1)
                    for k in range(DC):
                        nc.tensor.matmul(bank[0:SK, 0:D], sh.ctx_t[:, k, b * SK:(b + 1) * SK], w["wv_s"][:, k, :],
                                         start=(k == 0), stop=(k == DC - 1))
                    for k in range(DC):
                        ins = nc.tensor.matmul(bank[0:SK, D:2 * D], vst[:, k, b * SK:(b + 1) * SK], wg[:, k, :],
                                               start=(k == 0), stop=(k == DC - 1))
                    ins.then_inc(s.v_ps, 1)
                pe.wait_ge(s.fold_ready, 4)
                pe.wait_ge(s.set_ready, 2)
                pe.wait_ge(s.r1_ready, B)
                pe.sem_inc(s.xt_ps, 2)

                with pe.Fori(0, B) as b:
                    for j in range(TB):
                        n = b * TB + j
                        pe.wait_ge(s.xn_ready, n + 1)
                        pe.wait_ge(s.xt_ready, n + 1)
                        for c in range(DC):
                            ins = nc.tensor.transpose((b0, b1)[j % 2][:, c * P:(c + 1) * P], xn[:, j, c * P:(c + 1) * P], sh.ident[:, :])
                        ins.then_inc(s.xt_ps, 1)
                    pe.wait_ge(s.xt_ready, b * TB + (TB + 2))
                    pe.wait_ge(s.qb_ready, b * DC + DC)
                    for j in range(2):
                        for k in range(DC):
                            ins = nc.tensor.matmul(s2_bank[0:SK, j * 512:(j + 1) * 512], qb[:, k, :],
                                                   xt[:, k, j * 512:(j + 1) * 512], start=(k == 0), stop=(k == DC - 1))
                    ins.then_inc(s.s2_ps, 1)
                    for g in range(NG):
                        for j in range(GT):
                            for k in range(DC):
                                ins = nc.tensor.matmul((b4, b5)[g][:, j * SK:(j + 1) * SK],
                                                       xt[:, k, (g * GT + j) * P:(g * GT + j + 1) * P],
                                                       keys[:, ds(b * SK + k * B * SK, SK)], start=(k == 0), stop=(k == DC - 1))
                        ins.then_inc(s.s1_ps, 1)
                    pe.wait_ge(s.e2_ready, b + 1)
                    for g in range(NG):
                        for j in range(GT):
                            t = g * GT + j
                            ins = nc.tensor.transpose((b0, b1)[g][:, j * SK:(j + 1) * SK], p2[:, t * P:(t + 1) * P], sh.ident[0:SK, 0:SK])
                        ins.then_inc(s.p2t_ps, 1)
                    for t in range(TB):
                        if t % GT == 0:
                            pe.wait_ge(s.p2t_ready, b * NG + (t // GT + 1))
                        ins = nc.tensor.matmul(b6[0:SK, 0:D], p2t[:, t, :], xn[:, t, :], start=(t == 0), stop=(t == TB - 1))
                    ins.then_inc(s.u_ps, 1)
                    for g in range(NG):
                        pe.wait_ge(s.p1_ready, b * NG + (g + 1))
                        for j in range(GT):
                            ins = nc.tensor.transpose((b4, b5)[g][0:SK, j * P:(j + 1) * P], p1[:, g * GT + j, :], sh.ident[:, :])
                        ins.then_inc(s.p1t_ps, 1)
                    pe.wait_ge(s.u_ready, b + 1)
                    for k in range(DC):
                        ins = nc.tensor.transpose(b7[:, k * SK:(k + 1) * SK], uu[:, k * P:(k + 1) * P], sh.ident[0:SK, 0:SK])
                    ins.then_inc(s.ut_ps, 1)
                    pe.wait_ge(s.ut_ready, b + 1)
                    for m in range(DC):
                        for k in range(DC):
                            nc.tensor.matmul(b7[:, m * SK:(m + 1) * SK], w["wv_c"][:, k, m * P:(m + 1) * P], ut[:, k, :],
                                             start=(k == 0), stop=(k == DC - 1))
                    for k in range(DC):
                        ins = nc.tensor.matmul(b6[0:SK, 0:D], ut[:, k, :], w["wv_c"][:, k, :], start=(k == 0), stop=(k == DC - 1))
                    ins.then_inc(s.sc_ps, 1)
                    pe.wait_ge(s.sct_ready, b * DC + DC)
                    for k in range(DC):
                        ins = nc.tensor.matmul(b7[0:SK, 0:D], sct[:, k, :], wg[:, DC + k, :], start=(k == 0), stop=(k == DC - 1))
                    ins.then_inc(s.sg_ps, 1)
                    pe.wait_ge(s.r2_ready, b + 1)
                    pe.wait_ge(s.p1t_ready, b * NG + NG)
                    for j in range(TB):
                        u = j % 2
                        pe.wait_ge(s.x_ready, b * TB + (j + 1))
                        nc.tensor.matmul(s2_bank[:, u * 512:(u + 1) * 512], p1t[:, j, :], r1[:, ds(b * 2 * D, 2 * D)], start=True, stop=False)
                        nc.tensor.matmul(s2_bank[:, u * 512:(u + 1) * 512], interp[:, j * P:(j + 1) * P], r2[:, :], start=False, stop=True)
                        nc.tensor.matmul((b0, b1)[u][:, 0:D], interp[:, j * P:(j + 1) * P], r3[:, :],
                                         start=True, stop=True).then_inc(s.c_ps, 1)

            @block.scalar
            def _(act):
                act.wait_ge(s.small_loaded, 160)
                for n, (dst, bias) in enumerate(((kst, bks), (qst, bqs), (vst, bvs_c))):
                    for m in range(DC):
                        bank = [b0, b1, b4, b5, b6, b7][2 * n + m]
                        act.wait_ge(s.pre_ps, 2 * n + m + 1)
                        nc.scalar.activation(dst[:, m, :], bank[:, 0:B * SK], ACT.Identity, bias=bias[:, m:m + 1]).then_inc(s.pre_ready, 1)
                for n, dst in enumerate((keys[:, :].rearrange("p (c n) -> p c n", c=DC), queries[:, :, :])):
                    for m in range(DC):
                        bank = (b0, b1)[m] if n == 0 else s2_bank[:, m * 512:(m + 1) * 512]
                        act.wait_ge(s.fold_ps, 2 * n + m + 1)
                        nc.scalar.activation(dst[:, m, :], bank[:, 0:B * SK], ACT.Copy, scale=SC).then_inc(s.fold_ready, 1)
                act.sem_inc(s.xt_ready, 2)
                with act.Fori(0, B) as b:
                    for j in range(TB):
                        n = b * TB + j
                        act.wait_ge(s.xt_ps, n + 3)
                        nc.scalar.activation(xt[:, :, j * P:(j + 1) * P], (b0, b1)[j % 2][:, 0:D].rearrange("p (c n) -> p c n", c=DC),
                                             ACT.Copy).then_inc(s.xt_ready, 1)
                    act.wait_ge(s.nb2_ready, b + 1)
                    nc.scalar.activation(p2[:, :], s2_bank[0:SK, :], ACT.Exp, bias=nb2[:, 0:1], accum_out=sum2[:, :]).then_inc(s.e2_ready, 1)
                    for g in range(NG):
                        act.wait_ge(s.shift_ready, b * NG + (g + 1))
                        pg = p1[:, g * GT:(g + 1) * GT, :]
                        nc.scalar.activation(pg, pg, ACT.Exp).then_inc(s.e1_ready, 1)
                    for g in range(NG):
                        act.wait_ge(s.p2t_ps, b * NG + (g + 1))
                        nc.scalar.activation(p2t[:, g * GT:(g + 1) * GT, :], (b0, b1)[g][:, 0:GW].rearrange("p (h k) -> p h k", k=SK),
                                             ACT.Copy).then_inc(s.p2t_ready, 1)
                    for g in range(NG):
                        act.wait_ge(s.p1t_ps, b * NG + (g + 1))
                        nc.scalar.activation(p1t[:, g * GT:(g + 1) * GT, :], (b4, b5)[g][0:SK, :].rearrange("p (h k) -> p h k", k=P),
                                             ACT.Copy).then_inc(s.p1t_ready, 1)
                    act.wait_ge(s.ut_ps, b + 1)
                    nc.scalar.activation(ut[:, :, :], b7[:, 0:DC * SK].rearrange("p (c n) -> p c n", c=DC), ACT.Copy).then_inc(s.ut_ready, 1)
                    act.wait_ge(s.sc_ps, b + 1)
                    for m in range(DC):
                        nc.scalar.activation(sct[:, m, :], b7[:, m * SK:(m + 1) * SK], ACT.Identity, bias=bvc_c[:, m:m + 1]).then_inc(s.sct_ready, 1)
                    for j in range(TB):
                        u = j % 2
                        n = b * TB + j
                        act.wait_ge(s.c_ps, n + 1)
                        act.wait_ge(s.x_ready, n + 1)
                        nc.scalar.activation(th[:, u, :], s2_bank[:, u * 512 + D:(u + 1) * 512], ACT.Tanh, scale=0.5).then_inc(s.th_ready, 1)


def stage_l1_ffn(nc, io, sh):
    s = scope(nc, "l1f")
    with s.ctx:
        norm_sems(s)
        w = s.sb("w", [P, DC, D])
        neg = s.sb("neg", [P, DC, D])
        alpha = s.sb("alpha", [P, 1])
        bias = s.sb("bias", [P, D])
        wsum = s.sb("wsum", [P, 1])
        delta = s.sb("delta", [P, 2])
        xn = s.sb("xn", [P, AHEAD, D])
        xt = s.sb("xt", [P, AHEAD, D])
        ps_t = [s.ps(f"ps_t{u}", [P, D]) for u in range(AHEAD)]
        ps_y = [s.ps(f"ps_y{u}", [P, D]) for u in range(AHEAD)]
        ps_w = s.ps("ps_w", [P, 8])
        loaded, wsum_ready, wtot_ready = s.sem("loaded"), s.sem("wsum_ready"), s.sem("wtot_ready")
        step = s.sem("step")
        w_ready = s.sem("w_ready")
        xn_ready, xt_ps, xt_ready, y_ready = s.sem("xn_ready"), s.sem("xt_ps"), s.sem("xt_ready"), s.sem("y_ready")
        biased, x_ready, stats_ready = s.sem("biased"), s.sem("x_ready"), s.sem("stats_ready")
        tg = sh.gates[:, 5:6]

        with nc.Block() as block:
            @block.sync
            def _(sp):
                sp.dma_start(w[:, :, :], weight_view(io.L1_ffn_weight_T)).then_inc(loaded, 16)
                sp.dma_start(alpha[:, :], io.L1_ffn_alpha.partition_broadcast(P)).then_inc(loaded, 16)
                sp.dma_start(bias[:, :], io.L1_ffn_bias.partition_broadcast(P)).then_inc(loaded, 16)

            @block.vector
            def _(dve):
                c = norm_vector(nc, dve, sh, s)
                dve.wait_ge(loaded, 48)
                nc.vector.tensor_reduce(wsum[:, :], w[:, :, :], AX.XY, ALU.add,
                                        apply_absolute_value=True).then_inc(wsum_ready, 1)
                dve.wait_ge(wtot_ready, 1)
                c.link(nc.vector.tensor_scalar(delta[:, 0:1], ps_w[:, 0:1], 1.0 / (D * D), 0.7, ALU.mult, ALU.mult))
                c.link(nc.vector.tensor_scalar(delta[:, 1:2], delta[:, 0:1], -1.0, None, ALU.mult))
                c.link(nc.vector.tensor_scalar(neg[:, :, :], w[:, :, :], delta[:, 1:2], None, ALU.is_lt))
                c.link(nc.vector.scalar_tensor_tensor(w[:, :, :], w[:, :, :], delta[:, 0:1], neg[:, :, :],
                                                      ALU.is_gt, ALU.subtract))
                nc.vector.tensor_scalar(w[:, :, :], w[:, :, :], alpha[:, 0:1], tg, ALU.mult,
                                        ALU.mult).then_inc(w_ready, 1)
                c.link(nc.vector.tensor_scalar(bias[:, :], bias[:, :], tg, None, ALU.mult))
                dve.sem_inc(xn_ready, AHEAD)
                dve.sem_inc(x_ready, AHEAD)

                def front(t, u):
                    dve.wait_ge(xt_ps, ev(t, back=2))
                    normalise(nc, sh, xn[:, u, :], t).then_inc(xn_ready, 1)

                def back(t, u):
                    dve.wait_ge(y_ready, ev(t))
                    dve.wait_ge(biased, ev(t))
                    nc.vector.tensor_tensor(x_tile(sh, t), ps_y[u][:, :], x_tile(sh, t), ALU.add).then_inc(x_ready, 1)
                    dve.wait_ge(x_ready, ev(t))
                    tile_stats(nc, sh, t).then_inc(stats_ready, 1)

                pipeline(dve, T, [(back, 0), (front, 4)])
                dve.wait_ge(stats_ready, T)

            @block.gpsimd
            def _(pool):
                norm_gpsimd(nc, pool, sh, s)
                pool.wait_ge(w_ready, 1)
                pool.wait_ge(xn_ready, AHEAD)
                pool.sem_inc(biased, AHEAD)

                def part(t, u):
                    pool.wait_ge(xn_ready, ev(t))
                    nc.gpsimd.tensor_tensor(x_tile(sh, t), x_tile(sh, t), bias[:, :], ALU.add).then_inc(biased, 1)

                pipeline(pool, T, [(part, 0)])

            @block.tensor
            def _(pe):
                pe.wait_ge(wsum_ready, 1)
                nc.tensor.matmul(ps_w[:, 0:1], sh.ones[:, :], wsum[:, :], start=True, stop=True).then_inc(wtot_ready, 1)
                pe.wait_ge(w_ready, 1)
                pe.sem_inc(xt_ps, AHEAD)
                pe.sem_inc(y_ready, AHEAD)

                def front(t, u):
                    pe.wait_ge(xn_ready, ev(t))
                    pe.wait_ge(xt_ready, ev(t, back=2))
                    for c in range(DC):
                        ins = nc.tensor.transpose(ps_t[u][:, c * P:(c + 1) * P], xn[:, u, c * P:(c + 1) * P], sh.ident[:, :])
                    ins.then_inc(xt_ps, 1)

                def back(t, u):
                    pe.wait_ge(xt_ready, ev(t))
                    pe.wait_ge(x_ready, ev(t, back=2))
                    for c in range(DC):
                        ins = nc.tensor.matmul(ps_y[u][:, :], xt[:, u, c * P:(c + 1) * P], w[:, c, :],
                                               start=(c == 0), stop=(c == DC - 1))
                    ins.then_inc(y_ready, 1)

                pipeline(pe, T, [(back, 0), (front, 2)])

            @block.scalar
            def _(act):
                act.sem_inc(xt_ready, AHEAD)

                def part(t, u):
                    act.wait_ge(xt_ps, ev(t))
                    act.wait_ge(y_ready, ev(t, back=2))
                    nc.scalar.activation(xt[:, u, :], ps_t[u][:, :], ACT.Copy).then_inc(xt_ready, 1)

                pipeline(act, T, [(part, 0)])


NF = S // 2 + 1
NE, NO = S // 4 + 1, S // 4
FW = 103
FT = -(-NF // FW)
NFP = FT * FW
PARITY = [[f for f in range(FT) if f * FW < NE], [f for f in range(FT) if (f + 1) * FW > NE]]
HT = TB // 2
KF = SK // 2 + 1


def stage_l1_xattn(nc, io, sh):
    s = scope(nc, "l1x")
    GW = HH * KF
    NG = DC
    W = 104
    NW = HEADS * KF // W
    HWN = GW // W
    CUT = [(0, NE, 0), (NE, 2 * NE, 0), (2 * NE, 2 * NF, 1)]
    NS = 3
    HALF = [(0, 258), (258, NFP)]
    with s.ctx:
        norm_sems(s)
        w = {n: s.sb(n, [P, DC, D]) for n in ("Wkr", "Wki", "Wvr", "Wvi", "Wqr", "Wqi", "Wo")}
        bias = {n: s.sb(n, [P, DC]) for n in ("bqr", "bqi", "bkr", "bki", "gamma", "beta")}
        fwd = s.sb("fwd", [P, HT, 2 * NF])
        inv = s.sb("inv", [FW, 2 * len(PARITY[0]) * 2, S // 2])
        f77 = s.sb("f77", [SK, 2 * KF])
        ctx = s.sb("ctx", [SK, B, D])
        hm = s.sb("hm", [P, HH])
        kvf = s.sb("kvf", [P, DC, B * 2 * KF])
        kt = s.sb("kt", [P, 2, DC, B * KF])
        vt = s.sb("vt", [P, 2, DC, B * KF])
        bvrow = s.sb("bvrow", [FW, DC, 2, P])
        kbd = s.sb("kbd", [P, 2, DC, GW])
        vbd = s.sb("vbd", [P, 2, DC, GW])
        vrow = s.sb("vrow", [W, NW, 2 * P])
        v2, scale2, shift2 = s.sb("v2", [P, T]), s.sb("scale2", [P, T]), s.sb("shift2", [P, T])
        xn = s.sb("xn", [P, 2, 2, D])
        halves = s.sb("halves", [P, HT, 2, D])
        qf = s.sb("qf", [P, DC, 2, NFP])
        qt = s.sb("qt", [P, 2, DC, NFP])
        pr = s.sb("pr", [FW, NS, HEADS * KF])
        mx, rs, ri = (s.sb(n, [FW, NS, HEADS]) for n in ("mx", "rs", "ri"))
        pt = s.sb("pt", [W, 2, NW, FW])
        of = s.sb("of", [FW, FT, DC, 2, P])
        yt = s.sb("yt", [P, DC, S])
        bank = [s.ps(f"bank{k}", [P, 512]) for k in range(8)]
        for n in ["w_loaded", "small_loaded", "fwd_loaded", "inv_loaded", "kvf_ps", "kvf_ready", "kv_ps", "kv_ready",
                  "pad_set", "xn_ready", "halves_ready", "dft_ps", "qf_ready", "beta_ready", "q_ps", "q_ready",
                  "bd_ready", "v_ps", "v_ready", "s_ps", "max_ready", "shifted", "exp_ready", "sum_ready", "inv_ready",
                  "pt_ps", "pt_ready", "o_ps", "o_ready", "of_ready", "it_ps", "yt_ready", "y_ps", "x_ready", "stats_ready"]:
            s[n] = s.sem(n)
        tg = sh.gates[:, 1:2]
        SMALL = 16 * (5 + len(bias))

        def heads(ap):
            return ap.rearrange("p (h k) -> p h k", k=KF)

        def per_head(t_, u, g):
            return t_[:, u, g * HH:(g + 1) * HH].unsqueeze(2).to_broadcast((FW, HH, KF))

        def at(b, per, k):
            return b * per + (k + 1)

        with nc.Block() as block:
            @block.sync
            def _(sp):
                sp.dma_start(ctx[:, :, :], io.ctx.rearrange("b k d -> k b d")).then_inc(s.small_loaded, 16)
                sp.dma_start(f77[:, :], io.fourier_context).then_inc(s.small_loaded, 16)
                sp.dma_start(hm[:, :], io.head_mask).then_inc(s.small_loaded, 16)
                for r, n in enumerate(("bvr", "bvi")):
                    sp.dma_start(bvrow[:, :, r, :], io[f"L1_xattn_{n}_row"].partition_broadcast(FW)).then_inc(s.small_loaded, 16)
                for n, a in bias.items():
                    sp.dma_start(a[:, :], io[f"L1_xattn_{n}_cols"]).then_inc(s.small_loaded, 16)
                for n, a in w.items():
                    sp.dma_start(a[:, :, :], weight_view(io[f"L1_xattn_{n}_T"])).then_inc(s.w_loaded, 16)
                for j in range(HT):
                    sp.dma_start(fwd[:, j, :], io.fourier[j * P:(j + 1) * P, :]).then_inc(s.fwd_loaded, 16)
                sp.dma_start(inv[:, :, :], io.fourier_inverse.rearrange("f p n -> p f n")).then_inc(s.inv_loaded, 16)

            @block.vector
            def _(dve):
                c = norm_vector(nc, dve, sh, s)
                c.link(nc.vector.tensor_tensor(v2[:, :], sh.rstd[:, :], sh.rstd[:, :], ALU.mult))
                c.link(nc.vector.tensor_tensor(v2[:, :], v2[:, :], sh.var[:, :], ALU.mult))
                nc.vector.tensor_scalar(v2[:, :], v2[:, :], EPS, None, ALU.add).then_inc(s.var_ready, 1)
                dve.wait_ge(s.var_ready, 2)
                dve.wait_ge(s.pow_ready, 3)
                newton(nc, c, scale2[:, :], v2[:, :], sh.norm_a[:, :])
                c.link(nc.vector.tensor_tensor(scale2[:, :], scale2[:, :], sh.rstd[:, :], ALU.mult))
                c.link(nc.vector.scalar_tensor_tensor(shift2[:, :], sh.mean[:, :], -1.0, scale2[:, :], ALU.mult, ALU.mult))
                dve.wait_ge(s.small_loaded, SMALL)
                for n in ("bkr", "bki"):
                    c.link(nc.vector.tensor_scalar(bias[n][:, :], bias[n][:, :], HD ** -0.5, None, ALU.mult))
                c.link(nc.vector.tensor_scalar(bias["beta"][:, :], bias["beta"][:, :], float(S) ** 0.5, None, ALU.mult))
                c.link(nc.vector.memset(qf[:, :, :, NF:NFP], 0.0))
                dve.sem_inc(s.pad_set, 1)
                dve.wait_ge(s.kv_ready, 8)
                hmb = hm[:, :].unsqueeze(2).to_broadcast((P, HH, KF))
                for n in (s.halves_ready, s.beta_ready, s.bd_ready, s.max_ready, s.shifted, s.sum_ready, s.inv_ready, s.o_ready,
                          s.yt_ready, s.x_ready):
                    dve.sem_inc(n, 1)

                def prepare(b):
                    for j in range(HT):
                        for h in range(2):
                            n = b * TB + (h * HT + j)
                            nc.vector.tensor_scalar(xn[:, j % 2, h, :], x_tile(sh, n), scale2[:, ds(n, 1)], shift2[:, ds(n, 1)],
                                                    ALU.mult, ALU.add).then_inc(s.xn_ready, 1)
                        dve.wait_ge(s.xn_ready, b * TB + (2 * j + 2))
                        for h, op in enumerate((ALU.add, ALU.subtract)):
                            nc.vector.tensor_tensor(halves[:, j, h, :], xn[:, j % 2, 0, :], xn[:, j % 2, 1, :], op).then_inc(s.halves_ready, 1)
                    for r in range(2):
                        for k in range(DC):
                            for dst, src in ((kbd, kt), (vbd, vt)):
                                nc.vector.tensor_tensor(heads(dst[:, r, k, :]),
                                                        src[:, r, k, ds(b * KF, KF)].unsqueeze(1).to_broadcast((P, HH, KF)),
                                                        hmb, ALU.mult).then_inc(s.bd_ready, 1)

                def batch(b, last):
                    for k in range(DC):
                        dve.wait_ge(s.qf_ready, at(b, 6, 3 * k + 3))
                        nc.vector.tensor_scalar(qf[:, k, 0, 0:1], qf[:, k, 0, 0:1], bias["beta"][:, k:k + 1], None, ALU.add).then_inc(s.beta_ready, 1)

                    def shift(f):
                        u = f % NS
                        dve.wait_ge(s.pt_ps, at(b, FT * 2, 2 * (f - NS + 1) if f >= NS else 0))
                        for g in range(NG):
                            dve.wait_ge(s.s_ps, at(b, FT * NG, f * NG + g + 1))
                            nc.vector.tensor_reduce(mx[:, u, g * HH:(g + 1) * HH], heads(bank[g][0:FW, 0:GW]), AX.X, ALU.max).then_inc(s.max_ready, 1)
                            dve.wait_ge(s.max_ready, at(b, FT * NG, f * NG + g + 1))
                            nc.vector.tensor_tensor(heads(pr[:, u, g * GW:(g + 1) * GW]), heads(bank[g][0:FW, 0:GW]),
                                                    per_head(mx, u, g), ALU.subtract).then_inc(s.shifted, 1)

                    def sums(f):
                        u = f % NS
                        dve.wait_ge(s.exp_ready, at(b, FT * NG, f * NG + NG))
                        nc.vector.tensor_reduce(rs[:, u, :], heads(pr[:, u, :]), AX.X, ALU.add).then_inc(s.sum_ready, 1)
                        dve.wait_ge(s.sum_ready, at(b, FT, f + 1))
                        nc.vector.reciprocal(ri[:, u, :], rs[:, u, :]).then_inc(s.inv_ready, 1)

                    def result(f):
                        dve.wait_ge(s.o_ps, at(b, FT, f + 1))
                        dve.wait_ge(s.inv_ready, at(b, FT, f + 1))
                        for g in range(DC):
                            nc.vector.tensor_tensor(of[:, f, g, :, :].rearrange("p r (h d) -> p r h d", d=HD),
                                                    bank[4 + f % 2][0:FW, g * 2 * P:(g + 1) * 2 * P].rearrange("p (r h d) -> p r h d", r=2, d=HD),
                                                    ri[:, f % NS, g * HH:(g + 1) * HH].unsqueeze(1).unsqueeze(3).to_broadcast((FW, 2, HH, HD)),
                                                    ALU.mult).then_inc(s.o_ready, 1)

                    shift(0)
                    shift(1)
                    for f in range(FT):
                        if f + 2 < FT:
                            shift(f + 2)
                        sums(f)
                        result(f)
                    if not last:
                        prepare(b + 1)
                    for m in range(DC):
                        dve.wait_ge(s.it_ps, at(b, DC, m + 1))
                        nc.vector.tensor_copy(yt[:, m, S // 2:], bank[2 * m + 1][:, :]).then_inc(s.yt_ready, 1)
                        dve.wait_ge(s.yt_ready, at(b, 3 * DC, 3 * m + 1))
                        nc.vector.tensor_tensor(yt[:, m, 0:S // 2], bank[2 * m][:, :], yt[:, m, S // 2:], ALU.add).then_inc(s.yt_ready, 1)
                        dve.wait_ge(s.yt_ready, at(b, 3 * DC, 3 * m + 2))
                        nc.vector.tensor_tensor(yt[:, m, S // 2:], bank[2 * m][:, :], yt[:, m, S // 2:], ALU.subtract).then_inc(s.yt_ready, 1)
                    for j in range(TB):
                        n = b * TB + j
                        dve.wait_ge(s.y_ps, n + 2)
                        nc.vector.scalar_tensor_tensor(x_tile(sh, n), bank[6 + j % 2][:, 0:D], tg, x_tile(sh, n),
                                                       ALU.mult, ALU.add).then_inc(s.x_ready, 1)
                        dve.wait_ge(s.x_ready, n + 2)
                        tile_stats(nc, sh, n).then_inc(s.stats_ready, 1)

                prepare(0)
                with dve.Fori(0, B - 1) as b:
                    batch(b, False)
                batch(B - 1, True)
                dve.wait_ge(s.stats_ready, T)

            @block.gpsimd
            def _(pool):
                norm_gpsimd(nc, pool, sh, s)
                pool.wait_ge(s.var_ready, 2)
                nc.gpsimd.tensor_tensor(scale2[:, :], v2[:, :], sh.half[:, :], ALU.pow).then_inc(s.pow_ready, 1)
                pool.wait_ge(s.small_loaded, SMALL)
                pool.sem_inc(s.of_ready, 1)
                with pool.Fori(0, B) as b:
                    for f in range(FT):
                        pool.wait_ge(s.o_ready, at(b, FT * DC, f * DC + DC))
                        nc.gpsimd.tensor_tensor(of[:, f, :, :, :], of[:, f, :, :, :], bvrow[:, :, :, :], ALU.add).then_inc(s.of_ready, 1)

            @block.tensor
            def _(pe):
                pe.wait_ge(s.small_loaded, SMALL)
                for m in range(DC):
                    for b in range(B):
                        ins = nc.tensor.matmul(bank[m][:, b * 2 * KF:(b + 1) * 2 * KF], ctx[:, b, m * P:(m + 1) * P], f77[:, :],
                                               start=True, stop=True)
                    ins.then_inc(s.kvf_ps, 1)
                pe.wait_ge(s.w_loaded, 16 * 7)
                pe.wait_ge(s.kvf_ready, 2)
                for n, name in enumerate(("Wkr", "Wki", "Wvr", "Wvi")):
                    r = n % 2
                    for m in range(DC):
                        i = n * DC + m
                        if i >= 2:
                            pe.wait_ge(s.kv_ready, i - 1)
                        for k in range(DC):
                            part = kvf[:, k, :].rearrange("p (b r n) -> p b r n", b=B, r=2)[:, :, r, :]
                            ins = nc.tensor.matmul(bank[2 + m][:, 0:B * KF], w[name][:, k, m * P:(m + 1) * P], part,
                                                   start=(k == 0), stop=(k == DC - 1))
                        ins.then_inc(s.kv_ps, 1)
                pe.wait_ge(s.fwd_loaded, 16 * HT)
                pe.wait_ge(s.inv_loaded, 16)
                for n in (s.dft_ps, s.v_ps, s.q_ps, s.s_ps, s.pt_ps, s.o_ps, s.it_ps, s.y_ps):
                    pe.sem_inc(n, 1)

                with pe.Fori(0, B) as b:
                    pe.wait_ge(s.yt_ready, at(b, 3 * DC, 0))
                    for m in range(DC):
                        for j in range(HT):
                            if m == 0:
                                pe.wait_ge(s.halves_ready, at(b, TB, 2 * j + 2))
                            for i, (lo, hi, h) in enumerate(CUT):
                                ins = nc.tensor.matmul(bank[3 * m + i][:, 0:hi - lo], halves[:, j, h, m * P:(m + 1) * P],
                                                       fwd[:, j, lo:hi], start=(j == 0), stop=(j == HT - 1))
                        ins.then_inc(s.dft_ps, 1)
                    pe.wait_ge(s.bd_ready, at(b, 8, 8))
                    for i in range(NW):
                        k, col = i // HWN, (i % HWN) * W
                        if i >= 2:
                            pe.wait_ge(s.v_ready, at(b, NW, i - 1))
                        else:
                            pe.wait_ge(s.x_ready, at(b, TB, 0))
                        for r in range(2):
                            ins = nc.tensor.transpose(bank[6 + i % 2][0:W, r * P:(r + 1) * P], vbd[:, r, k, col:col + W], sh.ident[:, :])
                        ins.then_inc(s.v_ps, 1)
                    pe.wait_ge(s.v_ready, at(b, NW, NW))
                    pe.wait_ge(s.beta_ready, at(b, DC, DC))
                    for i in range(8):
                        r, m, (lo, hi) = i // 4, i // 2 % 2, HALF[i % 2]
                        if i >= 2:
                            pe.wait_ge(s.q_ready, at(b, 8, i - 1))
                        for k in range(DC):
                            ins = nc.tensor.matmul(bank[6 + i % 2][:, 0:hi - lo], w[("Wqr", "Wqi")[r]][:, k, m * P:(m + 1) * P],
                                                   qf[:, k, r, lo:hi], start=(k == 0), stop=(k == DC - 1))
                        ins.then_inc(s.q_ps, 1)
                    pe.wait_ge(s.q_ready, at(b, 8, 8))

                    def scores(f):
                        for g in range(NG):
                            if f:
                                pe.wait_ge(s.shifted, at(b, FT * NG, (f - 1) * NG + g + 1))
                            for r in range(2):
                                ins = nc.tensor.matmul(bank[g][0:FW, 0:GW], qt[:, r, g, f * FW:(f + 1) * FW], kbd[:, r, g, :],
                                                       start=(r == 0), stop=(r == 1))
                            ins.then_inc(s.s_ps, 1)

                    def values(f):
                        for g in range(DC):
                            pe.wait_ge(s.exp_ready, at(b, FT * NG, f * NG + g + 1))
                            if f:
                                pe.wait_ge(s.pt_ready, at(b, FT * DC, (f - 1) * DC + g + 1))
                            for i in range(HWN):
                                ins = nc.tensor.transpose(bank[2 + g][0:W, i * FW:(i + 1) * FW],
                                                          pr[:, f % NS, (g * HWN + i) * W:(g * HWN + i + 1) * W], sh.ident[0:FW, 0:FW])
                            ins.then_inc(s.pt_ps, 1)
                        if f >= 2:
                            pe.wait_ge(s.o_ready, at(b, FT * DC, (f - 1) * DC))
                        for g in range(DC):
                            pe.wait_ge(s.pt_ready, at(b, FT * DC, f * DC + g + 1))
                            for i in range(HWN):
                                ins = nc.tensor.matmul(bank[4 + f % 2][0:FW, g * 2 * P:(g + 1) * 2 * P], pt[:, f % 2, g * HWN + i, :],
                                                       vrow[:, g * HWN + i, :], start=(i == 0), stop=(i == HWN - 1))
                        ins.then_inc(s.o_ps, 1)

                    scores(0)
                    scores(1)
                    for f in range(FT):
                        if f + 2 < FT:
                            scores(f + 2)
                        values(f)
                    for m in range(DC):
                        for h in range(2):
                            steps = [(n, f, r) for n, f in enumerate(PARITY[h]) for r in range(2)]
                            for n, f, r in steps:
                                pe.wait_ge(s.of_ready, at(b, FT, f + 1))
                                ins = nc.tensor.matmul(bank[2 * m + h][:, :], of[:, f, m, r, :], inv[:, (h * 2 + r) * len(PARITY[0]) + n, :],
                                                       start=(n == 0 and r == 0), stop=((n, f, r) == steps[-1]))
                        ins.then_inc(s.it_ps, 1)
                    for j in range(TB):
                        if j < 2:
                            pe.wait_ge(s.yt_ready, at(b, 3 * DC, 3 * DC))
                        else:
                            pe.wait_ge(s.x_ready, at(b, TB, j - 1))
                        for k in range(DC):
                            ins = nc.tensor.matmul(bank[6 + j % 2][:, 0:D], yt[:, k, j * P:(j + 1) * P], w["Wo"][:, k, :],
                                                   start=(k == 0), stop=(k == DC - 1))
                        ins.then_inc(s.y_ps, 1)

            @block.scalar
            def _(act):
                act.wait_ge(s.small_loaded, SMALL)
                act.wait_ge(s.pad_set, 1)
                for m in range(DC):
                    act.wait_ge(s.kvf_ps, m + 1)
                    nc.scalar.activation(kvf[:, m, :], bank[m][:, 0:B * 2 * KF], ACT.Copy).then_inc(s.kvf_ready, 1)
                for i in range(8):
                    n, m = i // DC, i % DC
                    act.wait_ge(s.kv_ps, i + 1)
                    src = bank[2 + m][:, 0:B * KF]
                    if n < 2:
                        nc.scalar.activation(kt[:, n, m, :], src, ACT.Identity, scale=HD ** -0.5,
                                             bias=bias[("bkr", "bki")[n]][:, m:m + 1]).then_inc(s.kv_ready, 1)
                    else:
                        nc.scalar.activation(vt[:, n - 2, m, :], src, ACT.Copy).then_inc(s.kv_ready, 1)
                for n in (s.qf_ready, s.v_ready, s.q_ready, s.exp_ready, s.pt_ready):
                    act.sem_inc(n, 1)
                with act.Fori(0, B) as b:
                    act.wait_ge(s.q_ps, at(b, 8, 0))
                    for m in range(DC):
                        act.wait_ge(s.dft_ps, at(b, DC, m + 1))
                        for i in range(3):
                            lo, hi, h = CUT[i]
                            if h:
                                dst, src = qf[:, m, :, NE:NF], bank[3 * m + i][:, 0:hi - lo].rearrange("p (r n) -> p r n", r=2)
                            else:
                                dst, src = qf[:, m, i, 0:NE], bank[3 * m + i][:, 0:hi - lo]
                            nc.scalar.activation(dst, src, ACT.Copy, scale=bias["gamma"][:, m:m + 1]).then_inc(s.qf_ready, 1)
                    for i in range(NW):
                        act.wait_ge(s.v_ps, at(b, NW, i + 1))
                        nc.scalar.activation(vrow[:, i, :], bank[6 + i % 2][0:W, 0:2 * P], ACT.Copy).then_inc(s.v_ready, 1)
                    for i in range(8):
                        r, m, (lo, hi) = i // 4, i // 2 % 2, HALF[i % 2]
                        act.wait_ge(s.q_ps, at(b, 8, i + 1))
                        nc.scalar.activation(qt[:, r, m, lo:hi], bank[6 + i % 2][:, 0:hi - lo], ACT.Identity,
                                             bias=bias[("bqr", "bqi")[r]][:, m:m + 1]).then_inc(s.q_ready, 1)

                    def exps(f):
                        for g in range(NG):
                            act.wait_ge(s.shifted, at(b, FT * NG, f * NG + g + 1))
                            pg = pr[:, f % NS, g * GW:(g + 1) * GW]
                            nc.scalar.activation(pg, pg, ACT.Exp).then_inc(s.exp_ready, 1)

                    def copy_p(f):
                        for g in range(DC):
                            act.wait_ge(s.pt_ps, at(b, FT * DC, f * DC + g + 1))
                            nc.scalar.activation(pt[:, f % 2, g * HWN:(g + 1) * HWN, :],
                                                 bank[2 + g][0:W, 0:HWN * FW].rearrange("p (a b) -> p a b", b=FW),
                                                 ACT.Copy).then_inc(s.pt_ready, 1)

                    exps(0)
                    exps(1)
                    for f in range(FT):
                        if f + 2 < FT:
                            exps(f + 2)
                        copy_p(f)


def stage_l3_ffn(nc, io, sh):
    s = scope(nc, "l3f")
    G = 512
    NJ = S // G
    HU = NJ * DC
    with s.ctx:
        norm_sems(s)
        wx = s.sb("wx", [P, 3, DC, D])
        wc = s.sb("wc", [P, 3, DC, D])
        wo = s.sb("wo", [P, DC, D])
        uo = s.sb("uo", [P, DC, D])
        bg = s.sb("bg", [P, 3, DC])
        c0 = s.sb("c0", [P, DC])
        bo = s.sb("bo", [P, D])
        xt_all = s.sb("xt_all", [P, DC, B * S])
        ct = s.sb("ct", [P, 2, DC, S])
        gate = s.sb("gate", [P, 2, 3, G])
        prod = s.sb("prod", [P, 2, 2, G])
        xn = s.sb("xn", [P, AHEAD, D])
        cu = s.sb("cu", [P, TB, D])
        xc = s.sb("xc", [P, AHEAD, DC, P])
        z = s.sb("z", [P, AHEAD, D])
        h = s.sb("h", [P, AHEAD, D])
        bank = [s.ps(f"bank{k}", [P, G]) for k in range(8)]
        loaded, small = s.sem("loaded"), s.sem("small")
        xn_ready, xt_ps, xt_ready = s.sem("xn_ready"), s.sem("xt_ps"), s.sem("xt_ready")
        gate_ps, gate_ready, ig_ready, fc_step, c_ready = (
            s.sem("gate_ps"), s.sem("gate_ready"), s.sem("ig_ready"), s.sem("fc_step"), s.sem("c_ready"))
        cc_ready, cu_ps, cu_ready = s.sem("cc_ready"), s.sem("cu_ps"), s.sem("cu_ready")
        xc_ready, y_ps, z_ready, h_ready, x_ready = (
            s.sem("xc_ready"), s.sem("y_ps"), s.sem("z_ready"), s.sem("h_ready"), s.sem("x_ready"))

        with nc.Block() as block:
            @block.sync
            def _(sp):
                for k, n in enumerate("fic"):
                    sp.dma_start(wx[:, k, :, :], weight_view(io[f"L3_ffn_w{n}_T"])).then_inc(loaded, 16)
                    sp.dma_start(wc[:, k, :, :], weight_view(io[f"L3_ffn_u{n}_T"])).then_inc(loaded, 16)
                sp.dma_start(wo[:, :, :], weight_view(io.L3_ffn_wo_T)).then_inc(loaded, 16)
                sp.dma_start(uo[:, :, :], weight_view(io.L3_ffn_uo_T)).then_inc(loaded, 16)
                sp.dma_start(bo[:, :], io.L3_ffn_bo.partition_broadcast(P)).then_inc(small, 16)
                sp.dma_start(c0[:, :], io.L3_ffn_in_c_cols).then_inc(small, 16)
                for k, n in enumerate("fic"):
                    sp.dma_start(bg[:, k, :], io[f"L3_ffn_b{n}_cols"]).then_inc(small, 16)

            @block.vector
            def _(dve):
                norm_vector(nc, dve, sh, s)
                dve.sem_inc(xn_ready, AHEAD)

                def norm(t, u):
                    dve.wait_ge(xt_ps, ev(t, back=2))
                    normalise(nc, sh, xn[:, u, :], t).then_inc(xn_ready, 1)

                pipeline(dve, T, [(norm, 0)])
                dve.wait_ge(small, 16 * 5)
                for c in range(DC):
                    nc.vector.tensor_copy(ct[:, 0, c, :], c0[:, c:c + 1].to_broadcast((P, S))).then_inc(c_ready, HU - 1 if c else 1)

                def cell(b, v, j, m):
                    n = b * HU + (j * DC + m)
                    u = m
                    old, new = ct[:, v, m, j * G:(j + 1) * G], ct[:, 1 - v, m, j * G:(j + 1) * G]
                    dve.wait_ge(gate_ready, (n + 3) * 3)
                    dve.wait_ge(c_ready, n + HU)
                    nc.vector.tensor_tensor(prod[:, u, 0, :], gate[:, u, 0, :], old, ALU.mult).then_inc(fc_step, 1)
                    dve.wait_ge(fc_step, n + 1)
                    dve.wait_ge(ig_ready, n + 3)
                    nc.vector.tensor_tensor(new, prod[:, u, 0, :], prod[:, u, 1, :], ALU.add).then_inc(c_ready, 1)

                with dve.Fori(0, B // 2) as bb:
                    for v in range(2):
                        for j in range(NJ):
                            for m in range(DC):
                                cell(bb * 2 + v, v, j, m)

                dve.wait_ge(c_ready, (B + 1) * HU)
                for q in range(TB):
                    dve.wait_ge(cu_ps, q + 1)
                    nc.vector.tensor_tensor(cu[:, q, :], bank[q % 2][:, 0:D], bo[:, :], ALU.add).then_inc(cu_ready, 1)
                dve.wait_ge(cu_ready, TB)
                dve.sem_inc(z_ready, AHEAD)
                dve.sem_inc(x_ready, AHEAD)

                def pre(t, u):
                    dve.wait_ge(y_ps, ev(t))
                    dve.wait_ge(h_ready, ev(t, back=2))
                    nc.vector.tensor_tensor(z[:, u, :], bank[2 + u][:, 0:D], cu[:, ds(t % TB, 1), :].squeeze(1), ALU.add).then_inc(z_ready, 1)

                def update(t, u):
                    dve.wait_ge(h_ready, ev(t))
                    nc.vector.scalar_tensor_tensor(x_tile(sh, t), h[:, u, :], sh.gates[:, 7:8], x_tile(sh, t),
                                                   ALU.mult, ALU.add).then_inc(x_ready, 1)

                pipeline(dve, T, [(pre, 1), (update, 0)])
                dve.wait_ge(x_ready, T + AHEAD)

            @block.gpsimd
            def _(pool):
                norm_gpsimd(nc, pool, sh, s)
                pool.sem_inc(ig_ready, 2)

                def product(b, j, m):
                    n = b * HU + (j * DC + m)
                    pool.wait_ge(gate_ready, (n + 3) * 3)
                    pool.wait_ge(c_ready, n + HU - 1)
                    nc.gpsimd.tensor_tensor(prod[:, m, 1, :], gate[:, m, 1, :], gate[:, m, 2, :], ALU.mult).then_inc(ig_ready, 1)

                with pool.Fori(0, B) as b:
                    for j in range(NJ):
                        for m in range(DC):
                            product(b, j, m)
                pool.wait_ge(c_ready, (B + 1) * HU)
                pool.sem_inc(xc_ready, AHEAD)

                def copy(t, u):
                    pool.wait_ge(y_ps, ev(t, back=2))
                    nc.gpsimd.tensor_copy(xc[:, u, :, :], xt_all[:, :, ds(t * P, P)]).then_inc(xc_ready, 1)

                pipeline(pool, T, [(copy, 0)])

            @block.tensor
            def _(pe):
                pe.sem_inc(xt_ps, AHEAD)

                def front(t, u):
                    pe.wait_ge(xn_ready, ev(t))
                    pe.wait_ge(xt_ready, ev(t, back=2))
                    for c in range(DC):
                        ins = nc.tensor.transpose(bank[6 + u][:, c * P:(c + 1) * P], xn[:, u, c * P:(c + 1) * P], sh.ident[:, :])
                    ins.then_inc(xt_ps, 1)

                pipeline(pe, T, [(front, 0)])
                pe.wait_ge(xt_ready, T + AHEAD)
                pe.wait_ge(loaded, 16 * 8)

                def gates(b, v, j, m):
                    n = b * HU + (j * DC + m)
                    pe.wait_ge(gate_ready, (n + 1) * 3)
                    for k in range(3):
                        for c in range(DC):
                            nc.tensor.matmul(bank[3 * m + k][:, :], wx[:, k, c, m * P:(m + 1) * P],
                                             xt_all[:, c, ds(b * S + j * G, G)], start=(c == 0), stop=False)
                    pe.wait_ge(c_ready, b * HU + (j * DC + 2))
                    for k in range(3):
                        for c in range(DC):
                            ins = nc.tensor.matmul(bank[3 * m + k][:, :], wc[:, k, c, m * P:(m + 1) * P],
                                                   ct[:, v, c, j * G:(j + 1) * G], start=False, stop=(c == DC - 1))
                        ins.then_inc(gate_ps, 1)

                with pe.Fori(0, B // 2) as bb:
                    for v in range(2):
                        for j in range(NJ):
                            for m in range(DC):
                                gates(bb * 2 + v, v, j, m)

                pe.wait_ge(c_ready, (B + 1) * HU)
                for q in range(TB):
                    if q >= 2:
                        pe.wait_ge(cu_ready, q - 1)
                    else:
                        pe.wait_ge(gate_ready, (B * HU + 2) * 3)
                    for c in range(DC):
                        ins = nc.tensor.matmul(bank[q % 2][:, 0:D], ct[:, B % 2, c, q * P:(q + 1) * P], uo[:, c, :],
                                               start=(c == 0), stop=(c == DC - 1))
                    ins.then_inc(cu_ps, 1)
                pe.sem_inc(y_ps, AHEAD)

                def out(t, u):
                    pe.wait_ge(xc_ready, ev(t))
                    pe.wait_ge(z_ready, ev(t, back=2))
                    for c in range(DC):
                        ins = nc.tensor.matmul(bank[2 + u][:, 0:D], xc[:, u, c, :], wo[:, c, :],
                                               start=(c == 0), stop=(c == DC - 1))
                    ins.then_inc(y_ps, 1)

                pipeline(pe, T, [(out, 0)])

            @block.scalar
            def _(act):
                act.sem_inc(xt_ready, AHEAD)

                def copy(t, u):
                    act.wait_ge(xt_ps, ev(t))
                    nc.scalar.activation(xt_all[:, :, ds(t * P, P)], bank[6 + u][:, 0:D].rearrange("p (c n) -> p c n", c=DC),
                                         ACT.Copy).then_inc(xt_ready, 1)

                pipeline(act, T, [(copy, 0)])
                act.wait_ge(small, 16 * 5)
                act.sem_inc(gate_ready, 6)

                def squash(b, j, m):
                    n = b * HU + (j * DC + m)
                    act.wait_ge(c_ready, n + HU - 1)
                    act.wait_ge(ig_ready, n + 1)
                    for k, f in enumerate((ACT.Sigmoid, ACT.Sigmoid, ACT.Tanh)):
                        act.wait_ge(gate_ps, n * 3 + (k + 1))
                        nc.scalar.activation(gate[:, m, k, :], bank[3 * m + k][:, :], f, bias=bg[:, k, m:m + 1]).then_inc(gate_ready, 1)

                with act.Fori(0, B) as b:
                    for j in range(NJ):
                        for m in range(DC):
                            squash(b, j, m)
                act.sem_inc(h_ready, AHEAD)

                def tanh(t, u):
                    act.wait_ge(z_ready, ev(t))
                    act.wait_ge(x_ready, ev(t, back=2))
                    nc.scalar.activation(h[:, u, :], z[:, u, :], ACT.Tanh).then_inc(h_ready, 1)

                pipeline(act, T, [(tanh, 0)])


def stage_mha(nc, io, sh, name, names, gate, mask, key_padding, bias_names, masked):
    s = scope(nc, name)
    GH = 4
    NG = HEADS // GH
    GW = GH * SK
    HW_ = HH * SK
    NV = -(-HW_ // P)
    LAST = HW_ - (NV - 1) * P
    TURNS = [[(m, i) for i in range(NV - 1)] for m in range(DC)] + [[(m, NV - 1) for m in range(DC)]]
    NB = len(TURNS)
    BIG = -2.0 ** 100
    wq_T, wk_T, wv_T, wo_T = names
    with s.ctx:
        norm_sems(s)
        wq, wk, wv, wo = (s.sb(n, [P, DC, D]) for n in ("wq", "wk", "wv", "wo"))
        bq, bk, bv = (s.sb(n, [P, DC]) for n in ("bq", "bk", "bv"))
        brow = s.sb("brow", [P, D])
        bvb = s.sb("bvb", [P, DC, P])
        hm = s.sb("hm", [P, HH])
        kt = s.sb("kt", [P, DC, B * SK])
        vt = s.sb("vt", [P, DC, B * SK])
        kbd = s.sb("kbd", [P, B * DC * HW_])
        vbd = s.sb("vbd", [P, 2, DC, HW_])
        vrow = s.sb("vrow", [P, B * DC * NV * P])
        keyrow = s.sb("keyrow", [P, B, SK], U8)
        mraw = s.sb("mraw", [P, TB, SK], U8 if masked else F32)
        mask_t = s.sb("mask_t", [P, T, SK])
        xn = s.sb("xn", [P, AHEAD, D])
        xt = s.sb("xt", [P, AHEAD, D])
        qt = s.sb("qt", [P, AHEAD, D])
        mx = s.sb("mx", [P, AHEAD, HEADS])
        rs = s.sb("rs", [P, AHEAD, HEADS])
        ri = s.sb("ri", [P, AHEAD, HEADS])
        pr = s.sb("pr", [P, AHEAD, HEADS * SK])
        pt = s.sb("pt", [P, AHEAD, NB, 4 * P])
        o = s.sb("o", [P, AHEAD, D])
        ot = s.sb("ot", [P, AHEAD, D])
        x_bank, o_bank = s.ps("x_bank", [P, 512]), s.ps("o_bank", [P, 512])
        score = s.ps("score", [P, NG, 512])
        p_bank = [s.ps(f"p_bank{k}", [P, 512]) for k in range(2)]
        sems = ["w_loaded", "small_loaded", "kv_ps", "kv_ready", "bd_ready", "v_ps", "v_ready", "brow_ps",
                "brow_ready", "bvb_ready", "set_step", "mask_set", "xn_ready", "xt_ps", "xt_ready", "q_ps", "q_ready",
                "s_ps", "added", "max_ready", "shifted", "exp_ready", "sum_ready", "inv_ready", "pt_ps", "pt_ready",
                "o_ps", "o_ready", "ot_ps", "ot_ready", "y_ps", "biased", "x_ready", "stats_ready"]
        for n in sems:
            s[n] = s.sem(n)
        tg = sh.gates[:, gate:gate + 1]

        def heads(ap):
            return ap.rearrange("p (h k) -> p h k", k=SK)

        def prob(u, m):
            return pr[:, u, m * HW_:(m + 1) * HW_]

        def rows(i):
            return LAST if i == NV - 1 else P

        with nc.Block() as block:
            @block.sync
            def _(sp):
                for a, n in ((wk, wk_T), (wv, wv_T), (wq, wq_T), (wo, wo_T)):
                    sp.dma_start(a[:, :, :], weight_view(io[n])).then_inc(s.w_loaded, 16)
                sp.dma_start(hm[:, :], io.head_mask).then_inc(s.small_loaded, 16)
                sp.dma_start(mraw[:, :, :], mask.rearrange("(t p) k -> p t k", p=P)).then_inc(s.small_loaded, 16)
                if bias_names:
                    for a, n in zip((bq, bk, bv), bias_names):
                        sp.dma_start(a[:, :], io[n]).then_inc(s.small_loaded, 16)
                    sp.dma_start(brow[:, :], io[bias_names[3]].partition_broadcast(P)).then_inc(s.small_loaded, 16)
                if key_padding is not None:
                    sp.dma_start(keyrow[:, :, :], key_padding.partition_broadcast(P)).then_inc(s.small_loaded, 16)

            smalls = 16 * (2 + (4 if bias_names else 0) + (1 if key_padding is not None else 0))

            @block.vector
            def _(dve):
                c = norm_vector(nc, dve, sh, s)
                if not bias_names:
                    for a in (bq, bk, bv):
                        c.link(nc.vector.memset(a[:, :], 0.0))
                    c.link(nc.vector.memset(brow[:, :], 0.0))
                dve.wait_ge(s.small_loaded, smalls)
                c.link(nc.vector.tensor_scalar(bk[:, :], bk[:, :], HD ** -0.5, None, ALU.mult))
                nc.vector.tensor_copy(bvb[:, :, :], bv[:, :].unsqueeze(2).to_broadcast((P, DC, P))).then_inc(s.bvb_ready, 1)
                dve.wait_ge(s.kv_ready, 2 * DC)
                hmb = hm[:, :].unsqueeze(2).to_broadcast((P, HH, SK))
                for b in range(B):
                    if b >= 2:
                        dve.wait_ge(s.v_ps, (b - 1) * NB)
                    for k in range(DC):
                        at = (b * DC + k) * HW_
                        nc.vector.tensor_tensor(heads(kbd[:, at:at + HW_]),
                                                kt[:, k, b * SK:(b + 1) * SK].unsqueeze(1).to_broadcast((P, HH, SK)),
                                                hmb, ALU.mult).then_inc(s.bd_ready, 1)
                        nc.vector.tensor_tensor(heads(vbd[:, b % 2, k, :]),
                                                vt[:, k, b * SK:(b + 1) * SK].unsqueeze(1).to_broadcast((P, HH, SK)),
                                                hmb, ALU.mult).then_inc(s.bd_ready, 1)
                for b in range(B):
                    mb = mask_t[:, b * TB:(b + 1) * TB, :]
                    if masked:
                        c.link(nc.vector.tensor_scalar(mb, mraw[:, :, :], -1.0, -BIG, ALU.add, ALU.mult))
                    else:
                        c.link(nc.vector.scalar_tensor_tensor(mb, keyrow[:, b:b + 1, :].to_broadcast((P, TB, SK)), BIG, mraw[:, :, :],
                                                              ALU.mult, ALU.add))
                dve.wait_ge(s.brow_ps, 1)
                c.link(nc.vector.tensor_tensor(brow[:, :], o_bank[:, 0:D], brow[:, :], ALU.add))
                nc.vector.tensor_scalar(brow[:, :], brow[:, :], tg, None, ALU.mult).then_inc(s.brow_ready, 1)
                for n, k in ((s.xn_ready, 1), (s.x_ready, 1), (s.added, DC), (s.shifted, DC), (s.inv_ready, 1), (s.max_ready, DC),
                             (s.sum_ready, 1), (s.o_ready, 1)):
                    dve.sem_inc(n, AHEAD * k)

                def norm(t, u):
                    dve.wait_ge(s.xt_ps, ev(t, back=2))
                    normalise(nc, sh, xn[:, u, :], t).then_inc(s.xn_ready, 1)

                def shift(m):
                    def part(t, u):
                        if m == 0:
                            dve.wait_ge(s.pt_ps, ev(t, NB, back=2))
                        pm = prob(u, m)
                        hw = pm.rearrange("p (g h k) -> p g h k", g=NG // DC, k=SK)
                        hs = heads(pm)
                        half = score[:, m * (NG // DC):(m + 1) * (NG // DC), 0:GW].rearrange("p g (h k) -> p g h k", k=SK)
                        tile_mask = mask_t[:, ds(t, 1), :].unsqueeze(1).to_broadcast((P, NG // DC, GH, SK))
                        mh = mx[:, u, m * HH:(m + 1) * HH]
                        dve.wait_ge(s.s_ps, ev(t, DC, m + 1))
                        nc.vector.tensor_tensor(hw, half, tile_mask, ALU.add).then_inc(s.added, 1)
                        dve.wait_ge(s.added, ev(t, DC, m + 1))
                        nc.vector.tensor_reduce(mh, hs, AX.X, ALU.max).then_inc(s.max_ready, 1)
                        dve.wait_ge(s.max_ready, ev(t, DC, m + 1))
                        nc.vector.tensor_tensor(hs, hs, mh.unsqueeze(2).to_broadcast((P, HH, SK)), ALU.subtract).then_inc(s.shifted, 1)
                    return part

                def sums(t, u):
                    dve.wait_ge(s.exp_ready, ev(t, DC))
                    nc.vector.tensor_reduce(rs[:, u, :], heads(pr[:, u, :]), AX.X, ALU.add).then_inc(s.sum_ready, 1)
                    dve.wait_ge(s.sum_ready, ev(t))
                    nc.vector.reciprocal(ri[:, u, :], rs[:, u, :]).then_inc(s.inv_ready, 1)

                def scale_o(t, u):
                    dve.wait_ge(s.o_ps, ev(t))
                    dve.wait_ge(s.inv_ready, ev(t))
                    dve.wait_ge(s.ot_ps, ev(t, back=2))
                    nc.vector.tensor_tensor(o[:, u, :].rearrange("p (h d) -> p h d", d=HD),
                                            o_bank[:, 0:D].rearrange("p (h d) -> p h d", d=HD),
                                            ri[:, u, :].unsqueeze(2).to_broadcast((P, HEADS, HD)), ALU.mult).then_inc(s.o_ready, 1)

                def update(t, u):
                    dve.wait_ge(s.y_ps, ev(t))
                    dve.wait_ge(s.biased, ev(t))
                    nc.vector.tensor_tensor(x_tile(sh, t), o_bank[:, 0:D], x_tile(sh, t), ALU.add).then_inc(s.x_ready, 1)
                    dve.wait_ge(s.x_ready, ev(t))
                    tile_stats(nc, sh, t).then_inc(s.stats_ready, 1)

                pipeline(dve, T, [(scale_o, 0), (sums, 1), (norm, 4), (shift(0), 2), (update, 0), (shift(1), 2)])
                dve.wait_ge(s.stats_ready, T)

            @block.gpsimd
            def _(pool):
                norm_gpsimd(nc, pool, sh, s)
                pool.wait_ge(s.brow_ready, 1)
                pool.sem_inc(s.biased, AHEAD)

                def bias(t, u):
                    pool.wait_ge(s.xn_ready, ev(t))
                    nc.gpsimd.tensor_tensor(x_tile(sh, t), x_tile(sh, t), brow[:, :], ALU.add).then_inc(s.biased, 1)

                pipeline(pool, T, [(bias, 2)])

            @block.tensor
            def _(pe):
                pe.wait_ge(s.w_loaded, 64)
                for j, w_ in enumerate((wk, wv)):
                    for m in range(DC):
                        for k in range(DC):
                            ins = nc.tensor.matmul(score[:, j * DC + m, 0:B * SK], w_[:, k, m * P:(m + 1) * P], sh.ctx_t[:, k, :],
                                                   start=(k == 0), stop=(k == DC - 1))
                        ins.then_inc(s.kv_ps, 1)
                pe.wait_ge(s.bvb_ready, 1)
                for k in range(DC):
                    ins = nc.tensor.matmul(o_bank[:, 0:D], bvb[:, k, :], wo[:, k, :], start=(k == 0), stop=(k == DC - 1))
                ins.then_inc(s.brow_ps, 1)
                for b in range(B):
                    pe.wait_ge(s.bd_ready, 2 * DC * (b + 1))
                    for n, turn_ in enumerate(TURNS):
                        if b * NB + n >= 2:
                            pe.wait_ge(s.v_ready, b * NB + n - 1)
                        for j, (m, i) in enumerate(turn_):
                            ins = nc.tensor.transpose(p_bank[(b * NB + n) % 2][0:rows(i), j * P:(j + 1) * P],
                                                      vbd[:, b % 2, m, i * P:i * P + rows(i)], sh.ident[:, :])
                        ins.then_inc(s.v_ps, 1)
                pe.wait_ge(s.brow_ready, 1)
                pe.wait_ge(s.kv_ready, 2 * DC)
                pe.wait_ge(s.v_ready, B * NB)
                for n, k in ((s.xt_ps, 1), (s.q_ps, 1), (s.s_ps, DC), (s.pt_ps, NB), (s.o_ps, 1), (s.ot_ps, 1), (s.y_ps, 1)):
                    pe.sem_inc(n, AHEAD * k)

                def turn(t, u):
                    pe.wait_ge(s.xn_ready, ev(t))
                    pe.wait_ge(s.q_ready, ev(t, back=1))
                    for c in range(DC):
                        ins = nc.tensor.transpose(x_bank[:, c * P:(c + 1) * P], xn[:, u, c * P:(c + 1) * P], sh.ident[:, :])
                    ins.then_inc(s.xt_ps, 1)

                def query(t, u):
                    pe.wait_ge(s.xt_ready, ev(t))
                    for m in range(DC):
                        for k in range(DC):
                            ins = nc.tensor.matmul(x_bank[:, D + m * P:D + (m + 1) * P], wq[:, k, m * P:(m + 1) * P],
                                                   xt[:, u, k * P:(k + 1) * P], start=(k == 0), stop=(k == DC - 1))
                    ins.then_inc(s.q_ps, 1)

                def scores(t, u):
                    pe.wait_ge(s.q_ready, ev(t))
                    for k in range(DC):
                        pe.wait_ge(s.added, ev(t, DC, k + 1, back=1))
                        for g in range(k * NG // DC, (k + 1) * NG // DC):
                            ins = nc.tensor.matmul(score[:, g, 0:GW], qt[:, u, k * P:(k + 1) * P],
                                                   kbd[:, ds((t // TB) * (DC * HW_) + g * GW, GW)], start=True, stop=True)
                        ins.then_inc(s.s_ps, 1)

                def values(t, u):
                    for n, turn_ in enumerate(TURNS):
                        pe.wait_ge(s.exp_ready, ev(t, DC, min(n + 1, DC)))
                        pe.wait_ge(s.pt_ready, ev(t, NB, NB - 1 + n, back=1) if n < 2 else ev(t, NB, n - 1))
                        for j, (m, i) in enumerate(turn_):
                            ins = nc.tensor.transpose(p_bank[n % 2][0:rows(i), j * P:(j + 1) * P],
                                                      pr[:, u, m * HW_ + i * P:m * HW_ + i * P + rows(i)], sh.ident[:, :])
                        ins.then_inc(s.pt_ps, 1)
                    pe.wait_ge(s.x_ready, ev(t, back=1))
                    for m in range(DC):
                        for i in range(NV):
                            n = [n for n in range(NB) if (m, i) in TURNS[n]][0]
                            j = TURNS[n].index((m, i))
                            if i in (0, NV - 1):
                                pe.wait_ge(s.pt_ready, ev(t, NB, n + 1))
                            ins = nc.tensor.matmul(o_bank[:, m * P:(m + 1) * P], pt[0:rows(i), u, n, j * P:(j + 1) * P],
                                                   vrow[0:rows(i), ds((t // TB) * (DC * NV * P) + (m * NV + i) * P, P)],
                                                   start=(i == 0), stop=(i == NV - 1))
                    ins.then_inc(s.o_ps, 1)

                def turn_o(t, u):
                    pe.wait_ge(s.o_ready, ev(t))
                    for c in range(DC):
                        ins = nc.tensor.transpose(o_bank[:, D + c * P:D + (c + 1) * P], o[:, u, c * P:(c + 1) * P], sh.ident[:, :])
                    ins.then_inc(s.ot_ps, 1)

                def output(t, u):
                    pe.wait_ge(s.ot_ready, ev(t))
                    for k in range(DC):
                        ins = nc.tensor.matmul(o_bank[:, 0:D], ot[:, u, k * P:(k + 1) * P], wo[:, k, :], start=(k == 0), stop=(k == DC - 1))
                    ins.then_inc(s.y_ps, 1)

                pipeline(pe, T, [(turn, 3), (scores, 2), (turn_o, 0), (query, 3), (output, 0), (values, 1)])

            @block.scalar
            def _(act):
                act.wait_ge(s.small_loaded, smalls)
                act.wait_ge(s.bvb_ready, 1)
                for j, (a, scale) in enumerate(((kt, HD ** -0.5), (kt, HD ** -0.5), (vt, 1.0), (vt, 1.0))):
                    act.wait_ge(s.kv_ps, j + 1)
                    if j < 2:
                        nc.scalar.activation(a[:, j % 2, :], score[:, j, 0:B * SK], ACT.Identity, scale=scale,
                                             bias=bk[:, j:j + 1]).then_inc(s.kv_ready, 1)
                    else:
                        nc.scalar.activation(a[:, j % 2, :], score[:, j, 0:B * SK], ACT.Copy).then_inc(s.kv_ready, 1)
                for b in range(B):
                    for n, turn_ in enumerate(TURNS):
                        act.wait_ge(s.v_ps, b * NB + n + 1)
                        r = rows(turn_[0][1])
                        for j, (m, i) in enumerate(turn_ if n == NB - 1 else turn_[:1]):
                            k = 1 if n == NB - 1 else len(turn_)
                            at = ((b * DC + m) * NV + i) * P
                            ins = nc.scalar.activation(vrow[0:r, at:at + k * P], p_bank[(b * NB + n) % 2][0:r, j * P:(j + k) * P],
                                                       ACT.Copy, scale=sh.gates[0:r, gate:gate + 1])
                        ins.then_inc(s.v_ready, 1)
                for n, k in ((s.xt_ready, 1), (s.q_ready, 1), (s.exp_ready, DC), (s.pt_ready, NB), (s.ot_ready, 1)):
                    act.sem_inc(n, AHEAD * k)

                def copy_x(t, u):
                    act.wait_ge(s.xt_ps, ev(t))
                    act.wait_ge(s.q_ps, ev(t, back=2))
                    nc.scalar.activation(xt[:, u, :], x_bank[:, 0:D], ACT.Copy).then_inc(s.xt_ready, 1)

                def copy_q(t, u):
                    act.wait_ge(s.q_ps, ev(t))
                    act.wait_ge(s.s_ps, ev(t, DC, back=2))
                    for m in range(DC):
                        ins = nc.scalar.activation(qt[:, u, m * P:(m + 1) * P], x_bank[:, D + m * P:D + (m + 1) * P],
                                                   ACT.Identity, bias=bq[:, m:m + 1])
                    ins.then_inc(s.q_ready, 1)

                def copy_o(t, u):
                    act.wait_ge(s.ot_ps, ev(t))
                    act.wait_ge(s.y_ps, ev(t, back=2))
                    nc.scalar.activation(ot[:, u, :], o_bank[:, D:2 * D], ACT.Copy).then_inc(s.ot_ready, 1)

                def exps(m):
                    def part(t, u):
                        act.wait_ge(s.shifted, ev(t, DC, m + 1))
                        nc.scalar.activation(prob(u, m), prob(u, m), ACT.Exp).then_inc(s.exp_ready, 1)
                    return part

                def copy_p(t, u):
                    act.wait_ge(s.o_ps, ev(t, back=2))
                    for n, turn_ in enumerate(TURNS):
                        r, k = rows(turn_[0][1]), len(turn_)
                        act.wait_ge(s.pt_ps, ev(t, NB, n + 1))
                        nc.scalar.activation(pt[0:r, u, n, 0:k * P], p_bank[n % 2][0:r, 0:k * P], ACT.Copy).then_inc(s.pt_ready, 1)

                pipeline(act, T, [(copy_x, 3), (copy_o, 0), (copy_q, 3), (exps(0), 2), (copy_p, 1), (exps(1), 2)])


def stage_l2_xattn(nc, io, sh):
    stage_mha(nc, io, sh, "l2x", [f"L2_xattn_W{n}_T" for n in "qkvo"], 2, io.mask_SxS2_ff0, io.mask_BxS2_bf0,
              None, masked=False)


def stage_l3_xattn(nc, io, sh):
    stage_mha(nc, io, sh, "l3x", [f"L3_xattn_W_{n}_T" for n in "qkvo"], 3, io.mask_1x1xSxS2_bk0, None,
              ["L3_xattn_b_q_cols", "L3_xattn_b_k_cols", "L3_xattn_b_v_cols", "L3_xattn_b_o"], masked=True)


EXPERTS, TOP = 16, 2
HID = 512
ET = -(-(B * S * TOP) // P) + EXPERTS


def stage_l2_ffn(nc, io, sh):
    s = scope(nc, "moe")
    HC = HID // P
    ROW = D + 2
    RES = TOP * B * S
    SEL = 80
    with s.ctx:
        norm_sems(s)
        w1 = s.sb("w1", [P, EXPERTS * DC * HID])
        w2 = s.sb("w2", [P, EXPERTS * HC * D])
        wr = s.sb("wr", [P, DC, EXPERTS])
        brr = s.sb("brr", [P, EXPERTS])
        bf = s.sb("bf", [SEL, HID + D])
        bs = s.sb("bs", [SEL, HID + D], BF16)
        zero = s.sb("zero", [P, ROW])
        xin, xt = s.sb("xin", [P, 2, ROW]), s.sb("xt", [P, 2, D])
        w1e = s.sb("w1e", [P, 2 * DC * HID])
        lg = w1e[:, 0:T * EXPERTS]
        cnt, run_a, run_b = (w1e[:, k * T * EXPERTS:(k + 1) * T * EXPERTS].rearrange("p (t e) -> p t e", e=EXPERTS)
                             for k in range(1, 4))
        v8 = s.sb("v8", [P, T, 8])
        i8 = s.sb("i8", [P, T, 8], U32)
        idx = s.sb("idx", [P, TOP, T])
        wt = s.sb("wt", [P, TOP, T])
        dv = s.sb("dv", [P, T])
        iota = s.sb("iota", [P, EXPERTS])
        oh = s.sb("oh", [P, TOP, T, EXPERTS])
        ohb = s.sb("ohb", [P, T * EXPERTS], BF16)
        tri, onesb = s.sb("tri", [P, P], BF16), s.sb("onesb", [P, P], BF16)
        tot_i = s.sb("tot_i", [P, EXPERTS], I32)
        nt, st_a, st_b = s.sb("nt", [P, EXPERTS]), s.sb("st_a", [P, EXPERTS]), s.sb("st_b", [P, EXPERTS])
        slot_f = s.sb("slot_f", [P, TOP, T])
        slot = s.sb("slot", [P, TOP * T], U32)
        tile_no = s.sb("tile_no", [P, ET])
        eid = s.sb("eid", [P, ET])
        eid_i = s.sb("eid_i", [P, ET], I32)
        pexp = s.sb("pexp", [SEL, 1])
        sel = s.sb("sel", [SEL, ET], BF16)
        cmp_ = oh[:, :, :, :].rearrange("p a t e -> p (a t e)")
        pay = s.sb("pay", [P, 2, TOP, ROW])
        ht = pay[:, :, :, :].rearrange("p u k r -> p u (k r)")[:, :, 0:HID]
        y = s.sb("y", [P, 2, D])
        slots = s.sb("slots", [P, 2 * TOP], U32)
        tag = s.sb("tag", [P, T, TOP, 2])
        keep, keep_b = s.sb("keep", [P, T]), s.sb("keep_b", [P, T])
        meta = s.sb("meta", [P, 2, ET])
        spare = s.sb("spare", [P, ET])
        unused = s.sb("unused", [P, 2])
        row = s.sb("row", [P, 2], U32)
        results = w1[:, :].rearrange("p (k t d) -> p k t d", k=TOP, d=D)
        xs = nc.dram_tensor("moe_sorted", (ET * P, ROW), F32, kind="Internal").ap()
        ys = nc.dram_tensor("moe_results", (RES + ET * P, D), F32, kind="Internal").ap()
        bank = [s.ps(f"bank{k}", [P, 512]) for k in range(8)]
        for n in ["w_loaded", "small_loaded", "b_loaded", "zero_ready", "zero_filled", "iota_ready", "xn_ready", "xt_ps", "xt_ready",
                  "lg_ps", "lg_ready", "max_step", "dv_ready", "wt_ready", "set_step", "oh_ready", "cnt_ps",
                  "pay0_ready", "pay1_ready", "slots_ready", "scatter_begun", "kept", "xs_loaded0", "xs_loaded1", "scattered0", "scattered1",
                  "et_ps", "et_ready", "meta_ready", "w1e_ready", "h_ps", "ht_ready", "y_ps", "y_ready", "unused_ready", "row_ready",
                  "store_begun", "y_stored0", "y_stored1", "summed", "x_ready", "stats_ready"] + [f"results_loaded{b}" for b in range(B)]:
            s[n] = s.sem(n)
        tg = sh.gates[:, 6:7]
        IOTAS = 11

        with nc.Block() as block:
            @block.sync
            def _(sp):
                sp.dma_start(wr[:, :, :], weight_view(io.L2_ffn_Wr)).then_inc(s.small_loaded, 16)
                sp.dma_start(brr[:, :], io.L2_ffn_br.partition_broadcast(P)).then_inc(s.small_loaded, 16)
                sp.wait_ge(s.zero_ready, 3)
                for k in range(3):
                    sp.dma_start(bf[32 * k:32 * k + EXPERTS, 0:HID], io.L2_ffn_b1).then_inc(s.b_loaded, 16)
                    sp.dma_start(bf[32 * k:32 * k + EXPERTS, HID:HID + D], io.L2_ffn_b2).then_inc(s.b_loaded, 16)
                sp.dma_start(xs.rearrange("(t p) d -> p t d", p=P), zero[:, :].unsqueeze(1).to_broadcast((P, ET, ROW))).then_inc(s.zero_filled, 16)
                for e in range(EXPERTS):
                    sp.dma_start(w1[:, e * DC * HID:(e + 1) * DC * HID].rearrange("p (c n) -> p c n", c=DC),
                                 weight_view(io.L2_ffn_W1[e])).then_inc(s.w_loaded, 16)
                    sp.dma_start(w2[:, e * HC * D:(e + 1) * HC * D].rearrange("p (c n) -> p c n", c=HC),
                                 weight_view(io.L2_ffn_W2[e])).then_inc(s.w_loaded, 16)

            @block.vector
            def _(dve):
                nc.vector.memset(zero[:, :], 0.0).then_inc(s.zero_ready, 1)
                nc.vector.memset(bf[:, :], 0.0).then_inc(s.zero_ready, 1)
                nc.vector.memset(bs[:, :], 0.0).then_inc(s.zero_ready, 1)
                c = norm_vector(nc, dve, sh, s)
                dve.wait_ge(s.b_loaded, 96)
                for k in range(3):
                    rows = slice(32 * k, 32 * k + EXPERTS)
                    for i in range(k):
                        c.link(nc.vector.tensor_copy(bs[rows, :], bf[rows, :]))
                        c.link(nc.vector.tensor_tensor(bf[rows, :], bf[rows, :], bs[rows, :], ALU.subtract))
                    c.link(nc.vector.tensor_copy(bs[rows, :], bf[rows, :]))
                dve.wait_ge(s.small_loaded, 32)
                dve.sem_inc(s.xn_ready, AHEAD)
                dve.sem_inc(s.lg_ready, AHEAD)

                def norm(t, u):
                    dve.wait_ge(s.xt_ps, ev(t, back=2))
                    normalise(nc, sh, xin[:, u, 0:D], t).then_inc(s.xn_ready, 1)

                def logits(t, u):
                    dve.wait_ge(s.lg_ps, ev(t))
                    nc.vector.tensor_tensor(lg[:, ds(t * EXPERTS, EXPERTS)], bank[2 + u][:, 0:EXPERTS], brr[:, :], ALU.add).then_inc(s.lg_ready, 1)

                pipeline(dve, T, [(norm, 4), (logits, 0)])
                dve.wait_ge(s.lg_ready, T + AHEAD)
                for t in range(T):
                    nc.vector.max(v8[:, t, :], lg[:, t * EXPERTS:(t + 1) * EXPERTS]).then_inc(s.max_step, 1)
                dve.wait_ge(s.max_step, T)
                for t in range(T):
                    nc.vector.max_index(i8[:, t, :], v8[:, t, :], lg[:, t * EXPERTS:(t + 1) * EXPERTS]).then_inc(s.max_step, 1)
                dve.wait_ge(s.max_step, 2 * T)
                nc.vector.tensor_tensor(dv[:, :], v8[:, :, 0], v8[:, :, 1], ALU.subtract).then_inc(s.dv_ready, 1)
                for k in range(TOP):
                    c.link(nc.vector.tensor_copy(idx[:, k, :], i8[:, :, k]))
                dve.wait_ge(s.iota_ready, IOTAS)
                for k in range(TOP):
                    c.link(nc.vector.tensor_tensor(oh[:, k, :, :], idx[:, k, :].unsqueeze(2).to_broadcast((P, T, EXPERTS)),
                                                   iota[:, :].unsqueeze(1).to_broadcast((P, T, EXPERTS)), ALU.is_equal))
                nc.vector.tensor_tensor(ohb[:, :].rearrange("p (t e) -> p t e", e=EXPERTS), oh[:, 0, :, :], oh[:, 1, :, :], ALU.add).then_inc(s.oh_ready, 1)
                dve.wait_ge(s.cnt_ps, 1)
                c.link(nc.vector.tensor_copy(cnt[:, :, :].rearrange("p t e -> p (t e)"), bank[1][:, :]))
                src, dst = cnt, run_a
                for shift in (1, 2, 4, 8, 16):
                    c.link(nc.vector.tensor_tensor(dst[:, shift:T, :], src[:, shift:T, :], src[:, 0:T - shift, :], ALU.add))
                    c.link(nc.vector.tensor_copy(dst[:, 0:shift, :], src[:, 0:shift, :]))
                    src, dst = dst, (run_b if dst is run_a else run_a)
                total = src
                c.link(nc.vector.tensor_scalar(tot_i[:, :], total[:, T - 1, :], float(P - 1), None, ALU.add))
                c.link(nc.vector.tensor_scalar(tot_i[:, :], tot_i[:, :], 7, None, ALU.arith_shift_right))
                c.link(nc.vector.tensor_copy(nt[:, :], tot_i[:, :]))
                a, b_ = nt, st_a
                for shift in (1, 2, 4, 8):
                    c.link(nc.vector.tensor_tensor(b_[:, shift:], a[:, shift:], a[:, 0:EXPERTS - shift], ALU.add))
                    c.link(nc.vector.tensor_copy(b_[:, 0:shift], a[:, 0:shift]))
                    a, b_ = b_, (st_b if b_ is st_a else st_a)
                c.link(nc.vector.tensor_tensor(b_[:, :], a[:, :], nt[:, :], ALU.subtract))
                start = b_
                c.link(nc.vector.tensor_tensor(dst[:, :, :], total[:, :, :], cnt[:, :, :], ALU.subtract))
                c.link(nc.vector.scalar_tensor_tensor(dst[:, :, :], start[:, :].unsqueeze(1).to_broadcast((P, T, EXPERTS)), float(P),
                                                      dst[:, :, :], ALU.mult, ALU.add))
                c.link(nc.vector.tensor_tensor(dst[:, :, :].rearrange("p t e -> p (t e)"), dst[:, :, :].rearrange("p t e -> p (t e)"),
                                               bank[0][:, :], ALU.add))
                for k in range(TOP):
                    c.link(nc.vector.tensor_tensor(oh[:, k, :, :], oh[:, k, :, :], dst[:, :, :], ALU.mult))
                    c.link(nc.vector.tensor_reduce(slot_f[:, k, :], oh[:, k, :, :], AX.X, ALU.add))
                c.link(nc.vector.tensor_copy(slot[:, :].rearrange("p (t k) -> p k t", k=TOP), slot_f[:, :, :]))
                ge = cmp_[:, 0:EXPERTS * (ET // 2)].rearrange("p (j e) -> p j e", e=EXPERTS)
                for half in range(2):
                    part = slice(half * (ET // 2), (half + 1) * (ET // 2))
                    c.link(nc.vector.tensor_tensor(ge, tile_no[:, part].unsqueeze(2).to_broadcast((P, ET // 2, EXPERTS)),
                                                   start[:, :].unsqueeze(1).to_broadcast((P, ET // 2, EXPERTS)), ALU.is_ge))
                    c.link(nc.vector.tensor_reduce(eid[:, part], ge, AX.X, ALU.add))
                c.link(nc.vector.tensor_scalar(eid[:, :], eid[:, :], -1.0, None, ALU.add))
                c.link(nc.vector.tensor_copy(eid_i[:, :], eid[:, :]))
                c.link(nc.vector.tensor_scalar(sel[:, :], eid[0:SEL, :], pexp[:, 0:1], None, ALU.is_equal))
                dve.wait_ge(s.wt_ready, 2)
                for k in range(TOP):
                    c.link(nc.vector.tensor_scalar(tag[:, :, k, 1], wt[:, k, :], tg, None, ALU.mult))
                c.link(nc.vector.tensor_scalar(keep[:, :], sh.rstd[:, :], tg, 1.0, ALU.mult, ALU.add))
                c.link(nc.vector.tensor_scalar(keep_b[:, :], sh.shift[:, :], tg, None, ALU.mult))

            @block.gpsimd
            def _(pool):
                norm_gpsimd(nc, pool, sh, s)
                c = Chain(pool, s.iota_ready)
                c.link(nc.gpsimd.iota(iota[:, :], [[1, EXPERTS]], base=0, channel_multiplier=0, allow_small_or_imprecise_dtypes=True))
                c.link(nc.gpsimd.iota(tile_no[:, :], [[1, ET]], base=0, channel_multiplier=0, allow_small_or_imprecise_dtypes=True))
                c.link(nc.gpsimd.memset(pexp[:, :], -1.0))
                for k in range(3):
                    c.link(nc.gpsimd.iota(pexp[32 * k:32 * k + EXPERTS, :], [[0, 1]], base=0, channel_multiplier=1,
                                          allow_small_or_imprecise_dtypes=True))
                for k in range(TOP):
                    c.link(nc.gpsimd.iota(tag[:, :, k, 0], [[P, T]], base=k * B * S + 1, channel_multiplier=1,
                                          allow_small_or_imprecise_dtypes=True))
                c.link(nc.gpsimd.iota(spare[:, :], [[P, ET]], base=RES + 1, channel_multiplier=1, allow_small_or_imprecise_dtypes=True))
                c.link(nc.gpsimd.memset(onesb[:, :], 1.0))
                c.link(nc.gpsimd.affine_select(out=tri[:, :], in_=onesb[:, :], compare_op=ALU.is_gt, fill=0.0, base=0, pattern=[[1, P]],
                                               channel_multiplier=-1))

            @block.tensor
            def _(pe):
                pe.wait_ge(s.small_loaded, 32)
                pe.sem_inc(s.xt_ps, AHEAD)
                pe.sem_inc(s.lg_ps, AHEAD)

                def front(t, u):
                    pe.wait_ge(s.xn_ready, ev(t))
                    pe.wait_ge(s.xt_ready, ev(t, back=2))
                    for c in range(DC):
                        ins = nc.tensor.transpose(bank[u][:, c * P:(c + 1) * P], xin[:, u, c * P:(c + 1) * P], sh.ident[:, :])
                    ins.then_inc(s.xt_ps, 1)

                def back(t, u):
                    pe.wait_ge(s.xt_ready, ev(t))
                    pe.wait_ge(s.lg_ready, ev(t, back=2))
                    for c in range(DC):
                        ins = nc.tensor.matmul(bank[2 + u][:, 0:EXPERTS], xt[:, u, c * P:(c + 1) * P], wr[:, c, :],
                                               start=(c == 0), stop=(c == DC - 1))
                    ins.then_inc(s.lg_ps, 1)

                pipeline(pe, T, [(back, 0), (front, 2)])
                pe.wait_ge(s.oh_ready, 1)
                pe.wait_ge(s.iota_ready, IOTAS)
                pe.wait_ge(s.xt_ready, T + AHEAD)
                nc.tensor.matmul(bank[0][:, :], tri[:, :], ohb[:, :], start=True, stop=True)
                nc.tensor.matmul(bank[1][:, :], onesb[:, :], ohb[:, :], start=True, stop=True).then_inc(s.cnt_ps, 1)

            @block.scalar
            def _(act):
                act.sem_inc(s.xt_ready, AHEAD)

                def part(t, u):
                    act.wait_ge(s.xt_ps, ev(t))
                    act.wait_ge(s.lg_ps, ev(t, back=2))
                    nc.scalar.activation(xt[:, u, :], bank[u][:, 0:D], ACT.Copy).then_inc(s.xt_ready, 1)

                pipeline(act, T, [(part, 0)])
                act.wait_ge(s.dv_ready, 1)
                nc.scalar.activation(wt[:, 0, :], dv[:, :], ACT.Sigmoid).then_inc(s.wt_ready, 1)
                nc.scalar.activation(wt[:, 1, :], dv[:, :], ACT.Sigmoid, scale=-1.0).then_inc(s.wt_ready, 1)
                act.wait_ge(s.wt_ready, 2)

        with nc.Block() as block:
            @block.vector
            def _(dve):
                dve.sem_inc(s.slots_ready, AHEAD)
                dve.sem_inc(s.pay0_ready, AHEAD)

                def fill(t, u):
                    if not (isinstance(t, int) and t < 2):
                        dve.wait_ge((s.scattered0, s.scattered1)[u], (t // 2) * 32)
                    normalise(nc, sh, pay[:, u, 0, 0:D], t)
                    nc.vector.tensor_copy(pay[:, u, :, D:ROW], tag[:, ds(t, 1), :, :].rearrange("p t k r -> p (t k) r")).then_inc(s.pay0_ready, 1)
                    nc.vector.tensor_copy(slots[:, u * TOP:(u + 1) * TOP], slot[:, ds(t * TOP, TOP)]).then_inc(s.slots_ready, 1)

                def residual(t, u):
                    dve.wait_ge(s.pay1_ready, ev(t))
                    dve.wait_ge(s.pay0_ready, ev(t))
                    nc.vector.tensor_scalar(x_tile(sh, t), x_tile(sh, t), keep[:, ds(t, 1)], keep_b[:, ds(t, 1)],
                                            ALU.mult, ALU.add).then_inc(s.kept, 1)

                pipeline(dve, T, [(fill, 2), (residual, 0)])
                dve.wait_ge(s.kept, T)

            @block.scalar
            def _(act):
                act.sem_inc(s.pay1_ready, AHEAD)

                def fill(t, u):
                    if not (isinstance(t, int) and t < 2):
                        act.wait_ge((s.scattered0, s.scattered1)[u], (t // 2) * 32)
                    nc.scalar.activation(pay[:, u, 1, 0:D], x_tile(sh, t), ACT.Identity, bias=sh.shift[:, ds(t, 1)],
                                         scale=sh.rstd[:, ds(t, 1)]).then_inc(s.pay1_ready, 1)

                pipeline(act, T, [(fill, 2)])

            @block.gpsimd
            def _(pool):
                pool.wait_ge(s.zero_filled, 16)

                def part(t, u):
                    pool.wait_ge(s.pay0_ready, ev(t))
                    pool.wait_ge(s.pay1_ready, ev(t))
                    pool.wait_ge(s.slots_ready, ev(t))
                    pool.sem_inc(s.scatter_begun, 1)
                    for k in range(TOP):
                        nc.gpsimd.indirect_dma_start(
                            out=xs, out_offset=bass.IndirectOffsetOnAxis(ap=slots[:, u * TOP + k:u * TOP + k + 1], axis=0),
                            in_=pay[:, u, k, :], in_offset=None).then_inc((s.scattered0, s.scattered1)[u], 16)

                pipeline(pool, T, [(part, 0)])
                pool.wait_ge(s.scattered0, 32 * (T // 2))
                pool.wait_ge(s.scattered1, 32 * (T // 2))

        with nc.Block() as block:
            @block.sync
            def _(sp):
                def load(t, u):
                    sp.wait_ge(s.et_ps, ev(t, back=2))
                    sp.wait_ge(s.meta_ready, ev(t, back=2))
                    sp.dma_start(xin[:, u, :], xs[ds(t * P, P), :]).then_inc((s.xs_loaded0, s.xs_loaded1)[u], 16)

                pipeline(sp, ET, [(load, 2)])

            @block.gpsimd
            def _(pool):
                def store(t, u):
                    pool.wait_ge(s.y_ready, ev(t))
                    pool.wait_ge(s.row_ready, ev(t))
                    pool.sem_inc(s.store_begun, 1)
                    nc.gpsimd.indirect_dma_start(
                        out=ys, out_offset=bass.IndirectOffsetOnAxis(ap=row[:, u:u + 1], axis=0),
                        in_=y[:, u, :], in_offset=None).then_inc((s.y_stored0, s.y_stored1)[u], 16)

                pipeline(pool, ET, [(store, 0)])
                pool.wait_ge(s.y_stored0, 16 * (ET // 2))
                pool.wait_ge(s.y_stored1, 16 * (ET // 2))

            @block.tensor
            def _(pe):
                pe.wait_ge(s.w_loaded, 32 * EXPERTS)
                for n in (s.et_ps, s.h_ps, s.y_ps):
                    pe.sem_inc(n, AHEAD)

                def turn(t, u):
                    pe.wait_ge((s.xs_loaded0, s.xs_loaded1)[u], (t // 2) * 16 + 16)
                    pe.wait_ge(s.et_ready, ev(t, back=1))
                    for c in range(DC):
                        ins = nc.tensor.transpose(bank[0][:, c * P:(c + 1) * P], xin[:, u, c * P:(c + 1) * P], sh.ident[:, :])
                    ins.then_inc(s.et_ps, 1)

                def up(t, u):
                    pe.wait_ge(s.et_ready, ev(t))
                    pe.wait_ge(s.w1e_ready, ev(t))
                    pe.wait_ge(s.ht_ready, ev(t, back=2))
                    for m in range(HC):
                        out = bank[1 + u][:, m * P:(m + 1) * P]
                        nc.tensor.matmul(out, bs[:, m * P:(m + 1) * P], sel[:, ds(t, 1)].to_broadcast((SEL, P)), start=True, stop=False)
                        for c in range(DC):
                            at = (u * DC + c) * HID + m * P
                            ins = nc.tensor.matmul(out, w1e[:, at:at + P], xt[:, u, c * P:(c + 1) * P],
                                                   start=False, stop=(c == DC - 1))
                    ins.then_inc(s.h_ps, 1)

                def down(t, u):
                    e = pe.value_load(eid_i[0:1, ds(t, 1)], min_val=0, max_val=EXPERTS - 1)
                    pe.wait_ge(s.ht_ready, ev(t))
                    pe.wait_ge(s.y_ready, ev(t, back=2))
                    nc.tensor.matmul(bank[5 + u][:, 0:D], sel[:, ds(t, 1)].to_broadcast((SEL, P)), bs[:, HID:HID + D], start=True, stop=False)
                    for c in range(HC):
                        ins = nc.tensor.matmul(bank[5 + u][:, 0:D], ht[:, u, c * P:(c + 1) * P], w2[:, ds(e * (HC * D) + c * D, D)],
                                               start=False, stop=(c == HC - 1))
                    ins.then_inc(s.y_ps, 1)

                pipeline(pe, ET, [(up, 1), (turn, 2), (down, 0)])

            @block.scalar
            def _(act):
                act.sem_inc(s.w1e_ready, AHEAD)
                act.sem_inc(s.ht_ready, AHEAD)
                act.wait_ge(s.w_loaded, 32 * EXPERTS)

                def weights(t, u):
                    e = act.value_load(eid_i[0:1, ds(t, 1)], min_val=0, max_val=EXPERTS - 1)
                    act.wait_ge(s.h_ps, ev(t, back=2))
                    nc.scalar.activation(w1e[:, u * DC * HID:(u + 1) * DC * HID], w1[:, ds(e * (DC * HID), DC * HID)], ACT.Copy).then_inc(s.w1e_ready, 1)

                def gelu(t, u):
                    act.wait_ge(s.h_ps, ev(t))
                    act.wait_ge(s.y_ps, ev(t, back=2))
                    nc.scalar.activation(ht[:, u, :], bank[1 + u][:, :], ACT.Gelu).then_inc(s.ht_ready, 1)

                pipeline(act, ET, [(weights, 2), (gelu, 1)])

            @block.vector
            def _(dve):
                for n in (s.et_ready, s.meta_ready, s.unused_ready, s.row_ready, s.y_ready):
                    dve.sem_inc(n, AHEAD)

                def copy_x(t, u):
                    dve.wait_ge(s.et_ps, ev(t))
                    dve.wait_ge(s.h_ps, ev(t, back=2))
                    nc.vector.tensor_copy(xt[:, u, :], bank[0][:, 0:D]).then_inc(s.et_ready, 1)
                    nc.vector.tensor_copy(meta[:, :, ds(t, 1)], xin[:, u, D:ROW].unsqueeze(2)).then_inc(s.meta_ready, 1)

                def result(t, u):
                    if not (isinstance(t, int) and t < 2):
                        dve.wait_ge((s.y_stored0, s.y_stored1)[u], (t // 2) * 16)
                    dve.wait_ge(s.meta_ready, ev(t))
                    nc.vector.tensor_scalar(unused[:, u:u + 1], meta[:, 0, ds(t, 1)], 0.0, spare[:, ds(t, 1)], ALU.is_equal, ALU.mult).then_inc(s.unused_ready, 1)
                    dve.wait_ge(s.unused_ready, ev(t))
                    nc.vector.scalar_tensor_tensor(row[:, u:u + 1], unused[:, u:u + 1], -1.0, meta[:, 0, ds(t, 1)], ALU.add, ALU.add).then_inc(s.row_ready, 1)
                    dve.wait_ge(s.y_ps, ev(t))
                    nc.vector.tensor_scalar(y[:, u, :], bank[5 + u][:, 0:D], meta[:, 1, ds(t, 1)], None, ALU.mult).then_inc(s.y_ready, 1)

                pipeline(dve, ET, [(copy_x, 4), (result, 2)])

        with nc.Block() as block:
            @block.sync
            def _(sp):
                for b in range(B):
                    for k in range(TOP):
                        at = (k * B + b) * S
                        sp.dma_start(results[:, k, b * TB:(b + 1) * TB, :],
                                     ys[at:at + S, :].rearrange("(t p) d -> p t d", p=P)).then_inc(s[f"results_loaded{b}"], 32 // TOP)

            @block.gpsimd
            def _(pool):
                for b in range(B):
                    pool.wait_ge(s[f"results_loaded{b}"], 32)
                    with pool.Fori(b * TB, (b + 1) * TB) as t:
                        r = [results[:, k, ds(t, 1), :].rearrange("p t d -> p (t d)") for k in range(TOP)]
                        nc.gpsimd.tensor_tensor(r[0], r[0], r[1], ALU.add).then_inc(s.summed, 1)

            @block.vector
            def _(dve):
                dve.sem_inc(s.x_ready, AHEAD)

                def add(t, u):
                    dve.wait_ge(s.summed, t + 1)
                    nc.vector.tensor_tensor(x_tile(sh, t), x_tile(sh, t), results[:, 0, ds(t, 1), :].rearrange("p t d -> p (t d)"),
                                            ALU.add).then_inc(s.x_ready, 1)

                def stats(t, u):
                    dve.wait_ge(s.x_ready, ev(t))
                    tile_stats(nc, sh, t).then_inc(s.stats_ready, 1)

                pipeline(dve, T, [(add, 1), (stats, 0)])
                dve.wait_ge(s.stats_ready, T)


TRANSPOSED = ["L0_xattn_Wk_s", "L0_xattn_Wv_s", "L0_xattn_Wq_s", "L0_xattn_Wv_c", "L0_xattn_Wg", "L0_ffn_w1", "L0_ffn_w2",
              "L1_xattn_Wqr", "L1_xattn_Wqi", "L1_xattn_Wkr", "L1_xattn_Wki", "L1_xattn_Wvr", "L1_xattn_Wvi",
              "L1_xattn_Wo", "L1_ffn_weight", "L2_xattn_Wq", "L2_xattn_Wk", "L2_xattn_Wv", "L2_xattn_Wo",
              "L3_xattn_W_q", "L3_xattn_W_k", "L3_xattn_W_v", "L3_xattn_W_o", "L3_ffn_wf", "L3_ffn_uf",
              "L3_ffn_wi", "L3_ffn_ui", "L3_ffn_wc", "L3_ffn_uc", "L3_ffn_wo", "L3_ffn_uo"]

COLUMNS = ["L3_ffn_in_c", "L3_ffn_bf", "L3_ffn_bi", "L3_ffn_bc", "L0_ffn_conv_b", "L0_xattn_bq_c", "L0_xattn_bk_s",
           "L0_xattn_bq_s", "L0_xattn_bk_c", "L0_xattn_bv_s", "L0_xattn_bv_c", "L1_xattn_bqr", "L1_xattn_bqi", "L1_xattn_bkr", "L1_xattn_bki",
           "L3_xattn_b_q", "L3_xattn_b_k", "L3_xattn_b_v", "L1_xattn_gamma", "L1_xattn_beta"]


def host_layout(inputs):
    a = {k: np.asarray(v) for k, v in inputs.items()}
    laid = {}
    for k, v in a.items():
        if k in TRANSPOSED:
            laid[k + "_T"] = v.T
        elif k in COLUMNS:
            laid[k + "_cols"] = v.reshape(-1, P).T
            if k in ("L0_xattn_bv_s", "L0_xattn_bv_c"):
                laid[k] = v
        elif k in ("L1_xattn_bvr", "L1_xattn_bvi"):
            laid[k + "_row"] = v.reshape(DC, P)
        elif k == "ctx_1024":
            laid["ctx_T"] = v.reshape(B * SK, D).T
            laid["ctx"] = v
        elif k == "mask_1x1xSxS2_bk0":
            laid[k] = v[0, 0]
        else:
            laid[k] = v
    return laid


def shape_constants():
    c = {"identity": np.eye(P, dtype=np.float32)}
    c["head_mask"] = (np.arange(P)[:, None] // HD == np.arange(HH)[None, :]).astype(np.float32)
    pos = (np.arange(S, dtype=np.float32) + np.float32(0.5)) * np.float32(SK / S) - np.float32(0.5)
    pos = np.clip(pos, np.float32(0.0), np.float32(SK - 1))
    lo = np.floor(pos).astype(np.int32)
    hi = np.minimum(lo + 1, SK - 1)
    w = (pos - lo.astype(np.float32)).astype(np.float32)
    m = np.zeros((SK, S), np.float32)
    m[lo, np.arange(S)] += np.float32(1) - w
    m[hi, np.arange(S)] += w
    c["interpolate"] = m
    def forward(n, rows, freqs):
        angle = 2 * np.pi * (np.outer(np.arange(rows), freqs) % n) / n
        return np.concatenate([np.cos(angle), -np.sin(angle)], 1) / np.sqrt(n)

    even, odd = np.arange(0, NF, 2), np.arange(1, NF, 2)
    c["fourier"] = np.concatenate([forward(S, S // 2, even), forward(S, S // 2, odd)], 1).astype(np.float32)
    c["fourier_context"] = forward(SK, SK, np.arange(KF)).astype(np.float32)
    order = np.concatenate([even, odd])
    angle = 2 * np.pi * (np.outer(order, np.arange(S // 2)) % S) / S
    edge = (order == 0) | (order == S // 2)
    twice = np.where(edge, 1.0, 2.0)[:, None] / np.sqrt(S)
    g = np.zeros((2, 2, NFP, S // 2))
    for h in range(2):
        mine = np.where(order % 2 == h, 1.0, 0.0)[:, None]
        g[h, 0, :NF] = mine * twice * np.cos(angle)
        g[h, 1, :NF] = mine * np.where(edge, 0.0, 1.0)[:, None] * -twice * np.sin(angle)
    g = g.reshape(2, 2, FT, FW, S // 2)
    c["fourier_inverse"] = np.concatenate([g[h, :, PARITY[h]].transpose(1, 0, 2, 3).reshape(-1, FW, S // 2)
                                           for h in range(2)]).astype(np.float32)
    return c


def stage_begin(nc, io, sh):
    s = scope(nc, "begin")
    with s.ctx:
        x_loaded = [s.sem(f"x_loaded{b}") for b in range(B)]
        loaded, gates_loaded, gates_ready, stats_ready, ones_ready = (
            s.sem("loaded"), s.sem("gates_loaded"), s.sem("gates_ready"), s.sem("stats_ready"), s.sem("ones_ready"))
        with nc.Block() as block:
            @block.sync
            def _(sp):
                for b in range(B):
                    sp.dma_start(sh.x[:, b * TB * D:(b + 1) * TB * D].rearrange("p (t d) -> p t d", d=D),
                                 io.x[b].rearrange("(t p) d -> p t d", p=P)).then_inc(x_loaded[b], 16)
                sp.dma_start(sh.ident[:, :], io.identity).then_inc(loaded, 16)
                sp.dma_start(sh.ctx_t[:, :, :], io.ctx_T.rearrange("(c p) n -> p c n", p=P)).then_inc(loaded, 16)
                sp.wait_ge(loaded, 32)

            @block.scalar
            def _(act):
                act.dma_start(sh.gates[:, 0:4], io.g_xattn.partition_broadcast(P)).then_inc(gates_loaded, 16)
                act.dma_start(sh.gates[:, 4:8], io.g_ffn.partition_broadcast(P)).then_inc(gates_loaded, 16)
                act.wait_ge(gates_loaded, 32)
                nc.scalar.activation(sh.gates[:, :], sh.gates[:, :], ACT.Tanh).then_inc(gates_ready, 1)
                act.wait_ge(gates_ready, 1)

            @block.vector
            def _(dve):
                nc.vector.memset(sh.ones[:, :], 1.0).then_inc(ones_ready, 1)
                dve.wait_ge(loaded, 32)
                nc.vector.tensor_copy(sh.identb[:, :], sh.ident[:, :]).then_inc(ones_ready, 1)
                for t in range(T):
                    if t % TB == 0:
                        dve.wait_ge(x_loaded[t // TB], 16)
                    tile_stats(nc, sh, t).then_inc(stats_ready, 1)
                dve.wait_ge(stats_ready, T)


def stage_end(nc, io, sh, out):
    s = scope(nc, "end")
    with s.ctx:
        stored = s.sem("stored")
        with nc.Block() as block:
            @block.sync
            def _(sp):
                for b in range(B):
                    sp.dma_start(out[b].rearrange("(t p) d -> p t d", p=P),
                                 sh.x[:, b * TB * D:(b + 1) * TB * D].rearrange("p (t d) -> p t d", d=D)).then_inc(stored, 16)
                sp.wait_ge(stored, 16 * B)


def program(nc, io, out):
    sh = scope(nc, "all")
    with sh.ctx:
        sh.x = sh.sb("x", [P, T * D])
        sh.stats = sh.sb("stats", [P, T * 6])
        for n in ("mean", "var", "vare", "norm_a", "rstd", "shift", "half"):
            sh[n] = sh.sb(n, [P, T])
        sh.gates = sh.sb("gates", [P, 8])
        sh.ident = sh.sb("ident", [P, P])
        sh.identb = sh.sb("identb", [P, P], BF16)
        sh.ones = sh.sb("ones", [P, P])
        sh.ctx_t = sh.sb("ctx_t", [P, DC, B * SK])
        stage_begin(nc, io, sh)
        stages = [stage_l0_xattn, stage_l0_ffn, stage_l1_xattn, stage_l1_ffn,
                  stage_l2_xattn, stage_l2_ffn, stage_l3_xattn, stage_l3_ffn]
        for k in STAGES:
            stages[k](nc, io, sh)
        stage_end(nc, io, sh, out)


def kernel(**inputs):
    import numpy as _np
    import concourse.bacc as _bacc
    from concourse import mybir as _mybir
    from concourse.bass_utils import run_bass_kernel_spmd as _run

    nc = _bacc.Bacc("TRN2", target_bir_lowering=False, num_devices=1)
    laid = host_layout(inputs)
    laid.update(shape_constants())
    arrays, io = {}, Names()
    for name, a in laid.items():
        a = _np.ascontiguousarray(a)
        arrays[f"in_{name}"] = a
        io[name] = nc.dram_tensor(f"in_{name}", a.shape, _mybir.dt.from_np(a.dtype), kind="ExternalInput").ap()
    out = nc.dram_tensor("out_x", (B, S, D), F32, kind="ExternalOutput").ap()
    program(nc, io, out)
    r = _run(nc, [arrays], core_ids=[0])
    return r.results[0]["out_x"]
```

```python
from contextlib import ExitStack

import numpy as np

import concourse.bass as bass
from concourse import mybir

F32 = mybir.dt.float32
BF16 = mybir.dt.bfloat16
I32 = mybir.dt.int32
U32 = mybir.dt.uint32
U8 = mybir.dt.uint8
ALU = mybir.AluOpType
ACT = mybir.ActivationFunctionType
AX = mybir.AxisListType

P = 128
B, S, D = 4, 1024, 256
T = B * S // P
TB = S // P
DC = D // P
SK = 77
HEADS, HD = 16, 16
HH = HEADS // DC
EPS = 1e-5
AHEAD = 2
MAGIC = 1.5 * 2.0 ** 23

def ds(start, size):
    return bass.ds(start, size)


def ev(t, n=1, k=None, back=0):
    return t * n + (AHEAD - back) * n + (n if k is None else k)


def pipeline(eng, n, parts):
    lead = max(x for _, x in parts)
    lead += lead % 2

    def step(s):
        for part, x in parts:
            if 0 <= s + x < n:
                part(s + x, (s + x) % 2)

    for s in range(-lead, 0):
        step(s)
    with eng.Fori(0, (n - lead) // 2) as i:
        for v in range(2):
            for part, x in parts:
                part(i * 2 + (v + x), (v + x) % 2)
    for s in range(n - lead, n):
        step(s)


class Chain:

    def __init__(self, eng, sem, start=0):
        self.eng, self.sem, self.n = eng, sem, start

    def link(self, ins):
        ins.then_inc(self.sem, 1)
        self.n = self.n + 1
        self.eng.wait_ge(self.sem, self.n)


class TileChain(Chain):

    def __init__(self, eng, sem, t, per, first=0):
        super().__init__(eng, sem)
        self.t, self.per, self.n = t, per, first

    def link(self, ins):
        ins.then_inc(self.sem, 1)
        self.n += 1
        assert self.n <= self.per
        self.eng.wait_ge(self.sem, self.t * self.per + self.n)


class Names(dict):

    def __getattr__(self, name):
        return self[name]

    def __setattr__(self, name, value):
        self[name] = value


def scope(nc, name):
    ctx = ExitStack()
    g = Names(ctx=ctx)
    sems = []

    def end():
        if sems:
            nc.clear_and_free_semaphores(sems)
            nc.all_engine_barrier()

    def sem(n):
        sems.append(nc.alloc_semaphore(name=f"{name}_{n}"))
        return sems[-1]

    ctx.callback(end)
    g.sb = lambda n, shape, dt=F32: ctx.enter_context(nc.sbuf_tensor(f"{name}_{n}", shape, dt))
    g.ps = lambda n, shape, dt=F32: ctx.enter_context(nc.psum_tensor(f"{name}_{n}", shape, dt))
    g.sem = sem
    return g


def weight_view(w):
    return w.rearrange("(c p) o -> p c o", p=P)



def norm_vector(nc, dve, sh, s):
    c = Chain(dve, s.norm_step)
    st = sh.stats[:, :].rearrange("p (t s) -> p t s", s=6)
    me, mo, qe, qo = st[:, :, 1], st[:, :, 4], st[:, :, 2], st[:, :, 5]
    a, v = sh.norm_a[:, :], sh.var[:, :]
    c.link(nc.vector.tensor_tensor(a, me, mo, ALU.subtract))
    c.link(nc.vector.scalar_tensor_tensor(a, a, D / 4.0, a, ALU.mult, ALU.mult))
    c.link(nc.vector.tensor_tensor(v, qe, qo, ALU.add))
    c.link(nc.vector.tensor_tensor(v, v, a, ALU.add))
    c.link(nc.vector.tensor_scalar(v, v, 1.0 / D, None, ALU.mult))
    c.link(nc.vector.tensor_scalar(sh.vare[:, :], v, EPS, None, ALU.add))
    c.link(nc.vector.tensor_tensor(sh.mean[:, :], me, mo, ALU.add))
    c.link(nc.vector.tensor_scalar(sh.mean[:, :], sh.mean[:, :], 0.5, None, ALU.mult))
    inverse_root(nc, c, sh.rstd[:, :], sh.vare[:, :], a)
    c.link(nc.vector.scalar_tensor_tensor(sh.shift[:, :], sh.mean[:, :], -1.0, sh.rstd[:, :], ALU.mult, ALU.mult))
    return c


def inverse_root(nc, c, r, v, a):
    bits = r.bitcast(I32)
    c.link(nc.vector.tensor_scalar(bits, v.bitcast(I32), 1, None, ALU.arith_shift_right))
    c.link(nc.vector.tensor_scalar(bits, bits, -1.0, float(0x5F3759DF), ALU.mult, ALU.add))
    for _ in range(4):
        c.link(nc.vector.tensor_tensor(a, r, r, ALU.mult))
        c.link(nc.vector.scalar_tensor_tensor(a, a, -0.5, v, ALU.mult, ALU.mult))
        c.link(nc.vector.scalar_tensor_tensor(a, a, 0.5, r, ALU.add, ALU.mult))
        c.link(nc.vector.tensor_tensor(r, r, a, ALU.add))


def norm_sems(s):
    s.norm_step = s.sem("norm_step")


def x_tile(sh, t):
    return sh.x[:, ds(t * D, D)]


def normalise(nc, sh, out, t):
    return nc.vector.tensor_scalar(out, x_tile(sh, t), sh.rstd[:, ds(t, 1)], sh.shift[:, ds(t, 1)],
                                   ALU.mult, ALU.add)


def tile_stats(nc, sh, t):
    return nc.vector.bn_stats(sh.stats[:, ds(t * 6, 6)], x_tile(sh, t))


def stage_l0_ffn(nc, io, sh):
    s = scope(nc, "l0f")
    HID = 4 * D
    M = HID // P
    with s.ctx:
        norm_sems(s)
        w1, w2 = s.sb("w1", [P, DC, HID]), s.sb("w2", [P, M, D])
        w1q, w2q = s.sb("w1q", [P, DC, HID], BF16), s.sb("w2q", [P, M, D], BF16)
        wsum, wscale, wmean = s.sb("wsum", [P, 2]), s.sb("wscale", [P, 2]), s.sb("wmean", [P, 2])
        cw, cb = s.sb("cw", [P, M, 3]), s.sb("cb", [P, M])
        xn = s.sb("xn", [P, TB, D])
        am, sc, inv1, inv2 = (s.sb(n, [P, TB]) for n in ("am", "sc", "inv1", "inv2"))
        q1 = s.sb("q1", [P, 2, D], BF16)
        qt = s.sb("qt", [P, DC, S], BF16)
        dg = s.sb("dg", [P, TB, P])
        invb = s.sb("invb", [P, S])
        hs = s.sb("hs", [P, 2, S + 2])
        a = s.sb("a", [P, 2, S])
        z = s.sb("z", [P, M, S])
        q2 = s.sb("q2", [P, M, S], BF16)
        amax = s.sb("amax", [P, S])
        az = s.sb("az", [P, 2, S])
        scaled = s.sb("scaled", [P, 2, S // 2])
        hb = [s.ps(f"hb{k}", [P, S]) for k in range(2)]
        bc = s.ps("bc", [P, S])
        b6, b7 = s.ps("b6", [P, 512]), s.ps("b7", [P, 512])
        for n in ["w_loaded", "small_loaded", "wsum_ready", "wtot_ps", "set_step", "wq_ready", "w2sum_ready", "wscale_ready", "w2_step", "w2q_ready", "xn_step", "xmax_ready", "q1_ready", "qt_ps", "qt_ready",
                  "dg_ready", "inv_ps", "invb_ready", "h_ps", "pad_set", "table_loaded", "dve_hs_ready", "copied", "hs_ready", "a_ready", "conv_ready", "z_ready", "step",
                  "amax_ready", "abs_ready", "am_ps", "dg2_ready", "bc_ps", "scaled_ready", "q2_ready", "y_ps", "x_ready", "stats_ready"]:
            s[n] = s.sem(n)
        tg = sh.gates[:, 4:5]

        SHARED = (3, 5, 7)

        def wait_hs(eng, b, m):
            if m in SHARED:
                eng.wait_ge(s.hs_ready, b * len(SHARED) + (SHARED.index(m) + 1))
            else:
                alone = [k for k in range(M) if k not in SHARED]
                eng.wait_ge(s.dve_hs_ready, b * len(alone) + (alone.index(m) + 1))

        with nc.Block() as block:
            @block.sync
            def _(sp):
                sp.dma_start(w1[:, :, :], io.L0_ffn_w1_T.rearrange("(c p) o -> p c o", p=P)).then_inc(s.w_loaded, 16)
                sp.dma_start(w2[:, :, :], io.L0_ffn_w2_T.rearrange("(c p) o -> p c o", p=P)).then_inc(s.w_loaded, 16)
                sp.dma_start(cw[:, :, :], io.L0_ffn_conv_w.rearrange("(m p) a k -> p m (a k)", p=P)).then_inc(s.small_loaded, 16)
                sp.dma_start(cb[:, :], io.L0_ffn_conv_b_cols).then_inc(s.small_loaded, 16)

            @block.vector
            def _(dve):
                c = norm_vector(nc, dve, sh, s)
                dve.wait_ge(s.w_loaded, 32)
                nc.vector.tensor_reduce(wsum[:, 0:1], w1[:, :, :], AX.XY, ALU.add, apply_absolute_value=True).then_inc(s.wsum_ready, 1)
                dve.wait_ge(s.wtot_ps, 1)
                c.link(nc.vector.tensor_scalar(wmean[:, :], b6[:, 0:2], 1.0 / (HID * D), 1e-5, ALU.mult, ALU.max))
                nc.vector.reciprocal(wscale[:, :], wmean[:, :]).then_inc(s.wscale_ready, 1)
                dve.wait_ge(s.wscale_ready, 1)
                c.link(nc.vector.tensor_scalar(w1[:, :, :], w1[:, :, :], wscale[:, 0:1], MAGIC, ALU.mult, ALU.add))
                c.link(nc.vector.tensor_scalar(w1[:, :, :], w1[:, :, :], MAGIC, 1.0, ALU.subtract, ALU.min))
                nc.vector.tensor_scalar(w1q[:, :, :], w1[:, :, :], -1.0, None, ALU.max).then_inc(s.wq_ready, 1)
                c.link(nc.vector.tensor_scalar(wmean[:, 0:1], wmean[:, 0:1], 1.0 / 127.0, None, ALU.mult))
                c.link(nc.vector.tensor_scalar(wmean[:, 1:2], wmean[:, 1:2], 1.0 / 127.0, tg, ALU.mult, ALU.mult))
                dve.wait_ge(s.pad_set, 2)
                dve.wait_ge(s.small_loaded, 32)
                PER = 40

                def norm(b):
                    for j in range(TB):
                        normalise(nc, sh, xn[:, j, :], b * TB + j).then_inc(s.xn_step, 1)
                    dve.wait_ge(s.xn_step, b * TB + TB)
                    nc.vector.tensor_reduce(am[:, :], xn[:, :, :], AX.X, ALU.max, apply_absolute_value=True).then_inc(s.xmax_ready, 1)

                def batch(b, last):
                    k = TileChain(dve, s.step, b, PER)
                    dve.wait_ge(s.xmax_ready, b + 1)
                    k.link(nc.vector.tensor_scalar(am[:, :], am[:, :], 1e-5, None, ALU.max))
                    k.link(nc.vector.reciprocal(sc[:, :], am[:, :]))
                    k.link(nc.vector.tensor_scalar(sc[:, :], sc[:, :], 127.0, None, ALU.mult))
                    k.link(nc.vector.tensor_scalar(inv1[:, :], am[:, :], wmean[:, 0:1], None, ALU.mult))
                    for j in range(TB):
                        n = b * TB + j
                        k.link(nc.vector.tensor_scalar(xn[:, j, :], xn[:, j, :], sc[:, j:j + 1], MAGIC, ALU.mult, ALU.add))
                        if j >= 2:
                            dve.wait_ge(s.qt_ps, n - 1)
                        nc.vector.tensor_scalar(q1[:, j % 2, :], xn[:, j, :], MAGIC, 127.0, ALU.subtract, ALU.min).then_inc(s.q1_ready, 1)
                        nc.vector.tensor_scalar(dg[:, j, :], sh.ident[:, :], inv1[:, j:j + 1], None, ALU.mult).then_inc(s.dg_ready, 1)

                    def conv(m):
                        dve.wait_ge(s.a_ready, b * M + (m + 1))
                        k.link(nc.vector.scalar_tensor_tensor(a[:, m % 2, :], hs[:, m % 2, 0:S], cw[:, m, 0:1], a[:, m % 2, :],
                                                              ALU.mult, ALU.add))
                        nc.vector.scalar_tensor_tensor(a[:, m % 2, :], hs[:, m % 2, 2:S + 2], cw[:, m, 2:3], a[:, m % 2, :],
                                                       ALU.mult, ALU.add).then_inc(s.conv_ready, 1)
                        dve.wait_ge(s.conv_ready, b * M + (m + 1))

                    def largest(m):
                        dve.wait_ge(s.abs_ready, b * M + (m + 1))
                        if m == 0:
                            nc.vector.tensor_copy(amax[:, :], az[:, m % 2, :]).then_inc(s.amax_ready, 1)
                        else:
                            nc.vector.tensor_tensor(amax[:, :], az[:, m % 2, :], amax[:, :], ALU.max).then_inc(s.amax_ready, 1)
                        dve.wait_ge(s.amax_ready, b * M + (m + 1))

                    def scale_h(m):
                        if m < M and m not in SHARED:
                            dve.wait_ge(s.h_ps, b * M + (m + 1))
                            nc.vector.tensor_tensor(hs[:, m % 2, 1:S + 1], hb[m % 2][:, :], invb[:, :], ALU.mult).then_inc(s.dve_hs_ready, 1)

                    dve.wait_ge(s.invb_ready, b + 1)
                    scale_h(0)
                    for m in range(M):
                        scale_h(m + 1)
                        conv(m)
                        if m:
                            largest(m - 1)
                    largest(M - 1)
                    dve.wait_ge(s.am_ps, b + 1)
                    k.link(nc.vector.tensor_reduce(am[:, :], hb[0][:, :].rearrange("p (t n) -> p t n", n=P), AX.X, ALU.max))
                    k.link(nc.vector.tensor_scalar(am[:, :], am[:, :], 1e-5, None, ALU.max))
                    k.link(nc.vector.reciprocal(sc[:, :], am[:, :]))
                    k.link(nc.vector.tensor_scalar(sc[:, :], sc[:, :], 127.0, None, ALU.mult))
                    k.link(nc.vector.tensor_scalar(inv2[:, :], am[:, :], wmean[:, 1:2], None, ALU.mult))
                    for j in range(TB):
                        nc.vector.tensor_scalar(dg[:, j, :], sh.ident[:, :], sc[:, j:j + 1], None, ALU.mult).then_inc(s.dg2_ready, 1)

                    def update(j):
                        n = b * TB + j
                        dve.wait_ge(s.y_ps, n + 1)
                        nc.vector.scalar_tensor_tensor(x_tile(sh, n), (b6, b7)[j % 2][:, 0:D], inv2[:, j:j + 1], x_tile(sh, n),
                                                       ALU.mult, ALU.add).then_inc(s.x_ready, 1)
                        dve.wait_ge(s.x_ready, n + 1)
                        tile_stats(nc, sh, n).then_inc(s.stats_ready, 1)

                    for half in range(2):
                        dve.wait_ge(s.bc_ps, b * TB + (half + 1) * TB // 2)
                        cols = slice(half * S // 2, (half + 1) * S // 2)
                        for m in range(M + 1):
                            n = b * (2 * M) + (half * M + m)
                            if m < M:
                                nc.vector.tensor_tensor(scaled[:, m % 2, :], z[:, m, cols], bc[:, cols], ALU.mult).then_inc(s.scaled_ready, 1)
                            if m:
                                dve.wait_ge(s.scaled_ready, n)
                                nc.vector.tensor_scalar(q2[:, m - 1, cols], scaled[:, (m - 1) % 2, :], MAGIC, MAGIC,
                                                        ALU.add, ALU.subtract).then_inc(s.q2_ready, 1)
                                dve.wait_ge(s.q2_ready, n)
                            if half and m % 2 == 1:
                                update(m // 2)
                    if not last:
                        norm(b + 1)
                    for j in range(TB // 2, TB):
                        update(j)
                    assert k.n <= PER
                    if k.n < PER:
                        dve.sem_inc(s.step, PER - k.n)

                norm(0)
                with dve.Fori(0, B - 1) as b:
                    batch(b, False)
                batch(B - 1, True)
                dve.wait_ge(s.stats_ready, T)

            @block.gpsimd
            def _(pool):
                nc.gpsimd.memset(hs[:, :, 0:1], 0.0).then_inc(s.pad_set, 1)
                nc.gpsimd.memset(hs[:, :, S + 1:S + 2], 0.0).then_inc(s.pad_set, 1)
                pool.wait_ge(s.pad_set, 2)
                c = Chain(pool, s.w2_step)
                pool.wait_ge(s.wscale_ready, 1)
                c.link(nc.gpsimd.tensor_scalar(w2[:, :, :], w2[:, :, :], wscale[:, 1:2], MAGIC, ALU.mult, ALU.add))
                c.link(nc.gpsimd.tensor_scalar(w2[:, :, :], w2[:, :, :], MAGIC, 1.0, ALU.subtract, ALU.min))
                nc.gpsimd.tensor_scalar(w2q[:, :, :], w2[:, :, :], -1.0, None, ALU.max).then_inc(s.w2q_ready, 1)
                with pool.Fori(0, B) as b:
                    pool.wait_ge(s.invb_ready, b + 1)
                    for n, m in enumerate(SHARED):
                        pool.wait_ge(s.copied, b * len(SHARED) + (n + 1))
                        nc.gpsimd.tensor_tensor(hs[:, m % 2, 1:S + 1], hs[:, m % 2, 1:S + 1], invb[:, :], ALU.mult).then_inc(s.hs_ready, 1)

            @block.tensor
            def _(pe):
                pe.wait_ge(s.wsum_ready, 1)
                pe.wait_ge(s.w2sum_ready, 1)
                nc.tensor.matmul(b6[:, 0:2], sh.ones[:, :], wsum[:, :], start=True, stop=True).then_inc(s.wtot_ps, 1)
                pe.wait_ge(s.wq_ready, 1)
                with pe.Fori(0, B) as b:
                    for j in range(TB):
                        n = b * TB + j
                        pe.wait_ge(s.q1_ready, n + 1)
                        if j >= 2:
                            pe.wait_ge(s.qt_ready, n - 1)
                        bank = (b6, b7)[j % 2][:, :].bitcast(BF16)
                        for c in range(DC):
                            ins = nc.tensor.transpose(bank[:, c * P:(c + 1) * P], q1[:, j % 2, c * P:(c + 1) * P], sh.identb[:, :])
                        ins.then_inc(s.qt_ps, 1)
                        pe.wait_ge(s.dg_ready, n + 1)
                        nc.tensor.matmul(bc[:, j * P:(j + 1) * P], sh.ones[:, :], dg[:, j, :], start=True, stop=True).then_inc(s.inv_ps, 1)
                    pe.wait_ge(s.qt_ready, b * TB + TB)
                    for m in range(M):
                        if m >= 2:
                            if m - 2 in SHARED:
                                pe.wait_ge(s.copied, b * len(SHARED) + (SHARED.index(m - 2) + 1))
                            else:
                                wait_hs(pe, b, m - 2)
                        for j in range(2):
                            for c in range(DC):
                                ins = nc.tensor.matmul(hb[m % 2][:, j * 512:(j + 1) * 512], w1q[:, c, m * P:(m + 1) * P],
                                                       qt[:, c, j * 512:(j + 1) * 512], start=(c == 0), stop=(c == DC - 1))
                        ins.then_inc(s.h_ps, 1)
                    pe.wait_ge(s.amax_ready, b * M + M)
                    for j in range(TB):
                        ins = nc.tensor.transpose(hb[0][:, j * P:(j + 1) * P], amax[:, j * P:(j + 1) * P], sh.ident[:, :])
                    ins.then_inc(s.am_ps, 1)
                    for j in range(TB):
                        pe.wait_ge(s.dg2_ready, b * TB + (j + 1))
                        nc.tensor.matmul(bc[:, j * P:(j + 1) * P], sh.ones[:, :], dg[:, j, :], start=True, stop=True).then_inc(s.bc_ps, 1)
                    pe.wait_ge(s.w2q_ready, 1)
                    for j in range(TB):
                        if j % (TB // 2) == 0:
                            pe.wait_ge(s.q2_ready, b * (2 * M) + (j // (TB // 2) + 1) * M)
                        if j >= 2:
                            pe.wait_ge(s.x_ready, b * TB + (j - 1))
                        for m in range(M):
                            ins = nc.tensor.matmul((b6, b7)[j % 2][:, 0:D], q2[:, m, j * P:(j + 1) * P], w2q[:, m, :],
                                                   start=(m == 0), stop=(m == M - 1))
                        ins.then_inc(s.y_ps, 1)

            @block.scalar
            def _(act):
                act.wait_ge(s.w_loaded, 32)
                nc.scalar.activation(z[:, 0:2, :], w2[:, :, :].rearrange("p m d -> p (m d)").rearrange("p (a b) -> p a b", a=2), ACT.Abs,
                                     accum_out=wsum[:, 1:2]).then_inc(s.w2sum_ready, 1)
                act.wait_ge(s.w2sum_ready, 1)
                act.wait_ge(s.small_loaded, 32)
                nc.scalar.activation(az[:, 0, 0:M], cb[:, :], ACT.Silu).then_inc(s.table_loaded, 1)
                act.wait_ge(s.table_loaded, 1)
                with act.Fori(0, B) as b:
                    for j in range(TB):
                        n = b * TB + j
                        act.wait_ge(s.qt_ps, n + 1)
                        bank = (b6, b7)[j % 2][:, :].bitcast(BF16)
                        nc.scalar.activation(qt[:, :, j * P:(j + 1) * P], bank[:, 0:D].rearrange("p (c n) -> p c n", c=DC),
                                             ACT.Copy).then_inc(s.qt_ready, 1)
                    act.wait_ge(s.inv_ps, b * TB + TB)
                    nc.scalar.activation(invb[:, :], bc[:, :], ACT.Copy).then_inc(s.invb_ready, 1)

                    def centre(m):
                        wait_hs(act, b, m)
                        if m >= 2:
                            act.wait_ge(s.z_ready, b * M + (m - 1))
                        nc.scalar.activation(a[:, m % 2, :], hs[:, m % 2, 1:S + 1], ACT.Identity, scale=cw[:, m, 1:2],
                                             bias=cb[:, m:m + 1]).then_inc(s.a_ready, 1)

                    def copy_h(m):
                        if m in SHARED:
                            act.wait_ge(s.h_ps, b * M + (m + 1))
                            if m >= 2:
                                act.wait_ge(s.conv_ready, b * M + (m - 1))
                            nc.scalar.activation(hs[:, m % 2, 1:S + 1], hb[m % 2][:, :], ACT.Copy).then_inc(s.copied, 1)

                    copy_h(1)
                    centre(0)
                    for m in range(M):
                        if m + 1 < M:
                            centre(m + 1)
                        act.wait_ge(s.conv_ready, b * M + (m + 1))
                        nc.scalar.activation(z[:, m, :], a[:, m % 2, :], ACT.Silu).then_inc(s.z_ready, 1)
                        copy_h(m + 2)
                        act.wait_ge(s.z_ready, b * M + (m + 1))
                        if m >= 2:
                            act.wait_ge(s.amax_ready, b * M + (m - 1))
                        nc.scalar.activation(az[:, m % 2, :], z[:, m, :], ACT.Abs).then_inc(s.abs_ready, 1)


def stage_l0_xattn(nc, io, sh):
    s = scope(nc, "l0x")
    SC = D ** -0.5
    GT = 4
    GW = GT * SK
    NG = TB // GT
    with s.ctx:
        norm_sems(s)
        names = ["wk_s", "wv_s", "wq_s", "wv_c", "wq", "wk"]
        w = {n: s.sb(n, [P, DC, D]) for n in names}
        wg = s.sb("wg", [P, 2 * DC, D])
        bq, bks, bqs, bkc = (s.sb(n, [P, DC]) for n in ("bq", "bks", "bqs", "bkc"))
        bvs_c, bvc_c = s.sb("bvs_c", [P, DC]), s.sb("bvc_c", [P, DC])
        bvs, bvc, bgr = s.sb("bvs", [SK, D]), s.sb("bvc", [SK, D]), s.sb("bgr", [SK, D])
        interp = s.sb("interp", [SK, S])
        bqb = s.sb("bqb", [P, DC, P])
        kst, qst, vst = (s.sb(n, [P, DC, B * SK]) for n in ("kst", "qst", "vst"))
        keys, queries = s.sb("keys", [P, DC * B * SK]), s.sb("queries", [P, DC, B * SK])
        crow = s.sb("crow", [P, B * SK])
        beta = s.sb("beta", [SK, B])
        r1 = s.sb("r1", [SK, B * 2 * D])
        qb = s.sb("qb", [P, DC, SK])
        xn = s.sb("xn", [P, TB, D])
        xt = s.sb("xt", [P, DC, S])
        p2 = s.sb("p2", [SK, S])
        m2, nb2, sum2, inv2 = (s.sb(n, [SK, 1]) for n in ("m2", "nb2", "sum2", "inv2"))
        p2t = s.sb("p2t", [P, TB, SK])
        uu = s.sb("uu", [SK, D])
        ut = s.sb("ut", [P, DC, SK])
        sct = s.sb("sct", [P, DC, SK])
        sc = s.sb("sc", [SK, D])
        r2 = s.sb("r2", [SK, 2 * D])
        r3 = s.sb("r3", [SK, D])
        p1 = s.sb("p1", [P, TB, SK])
        mx, rs, ri = (s.sb(n, [P, TB]) for n in ("mx", "rs", "ri"))
        p1t = s.sb("p1t", [SK, TB, P])
        th = s.sb("th", [P, 2, D])
        tmp = s.sb("tmp", [P, 2, D])
        halfg = s.sb("halfg", [P, 2])
        s2_bank = s.ps("s2_bank", [P, S])
        b0, b1 = s.ps("b0", [P, 512]), s.ps("b1", [P, 512])
        b4, b5 = s.ps("b4", [P, 512]), s.ps("b5", [P, 512])
        b6, b7 = s.ps("b6", [P, 512]), s.ps("b7", [P, 512])
        for n in [f"x_loaded{b}" for b in range(B)] + ["ident_loaded", "gates_loaded", "tanh_ready", "shared_set", "half_ready", "first_stats", "w_loaded", "rest_loaded", "small_loaded", "set_ready", "pre_ps", "pre_ready", "fold_ps", "fold_ready", "v_ps", "v_ready", "r1_ready", "r1_step",
                  "xn_ready", "xt_ps", "xt_ready", "qb_ready", "s2_ps", "step", "nb2_ready", "e2_ready",
                  "s1_ps", "shift_ready", "e1_ready", "inv1_ready", "p1_ready", "p2t_ps", "p2t_ready", "u_ps",
                  "u_ready", "ut_ps", "ut_ready", "sc_ps", "sct_ready", "sg_ps", "r2_ready", "p1t_ps", "p1t_ready",
                  "c_ps", "th_ready", "x_ready", "stats_ready"]:
            s[n] = s.sem(n)
        tg = sh.gates[:, 0:1]

        with nc.Block() as block:
            @block.sync
            def _(sp):
                sp.dma_start(sh.ctx_t[:, :, :], io.ctx_T.rearrange("(c p) n -> p c n", p=P)).then_inc(s.w_loaded, 16)
                for n in ("Wk_s", "Wq_s", "Wv_s"):
                    sp.dma_start(w[n.lower()][:, :, :], weight_view(io[f"L0_xattn_{n}_T"])).then_inc(s.w_loaded, 16)
                for a, n in ((bq, "bq_c"), (bks, "bk_s"), (bqs, "bq_s"), (bkc, "bk_c"), (bvs_c, "bv_s"), (bvc_c, "bv_c")):
                    sp.dma_start(a[:, :], io[f"L0_xattn_{n}_cols"]).then_inc(s.small_loaded, 16)
                for a, n in ((bvs, "bv_s"), (bvc, "bv_c"), (bgr, "bg")):
                    sp.dma_start(a[:, :], io[f"L0_xattn_{n}"].partition_broadcast(SK)).then_inc(s.small_loaded, 16)
                sp.dma_start(interp[:, :], io.interpolate).then_inc(s.small_loaded, 16)
                for b in range(B):
                    sp.dma_start(sh.x[:, b * TB * D:(b + 1) * TB * D].rearrange("p (t d) -> p t d", d=D),
                                 io.x[b].rearrange("(t p) d -> p t d", p=P)).then_inc(s[f"x_loaded{b}"], 16)

            @block.vector
            def _(dve):
                nc.vector.memset(sh.ones[:, :], 1.0).then_inc(s.shared_set, 1)
                dve.wait_ge(s.small_loaded, 160)
                nc.vector.tensor_copy(bqb[:, :, :], bq[:, :].unsqueeze(2).to_broadcast((P, DC, P))).then_inc(s.set_ready, 1)
                dve.wait_ge(s.tanh_ready, 1)
                nc.vector.tensor_scalar(halfg[:, 0:1], tg, 0.5, None, ALU.mult).then_inc(s.half_ready, 1)
                for t in range(T):
                    if t % TB == 0:
                        dve.wait_ge(s[f"x_loaded{t // TB}"], 16)
                    tile_stats(nc, sh, t).then_inc(s.first_stats, 1)
                dve.wait_ge(s.first_stats, T)
                dve.wait_ge(s.ident_loaded, 16)
                nc.vector.tensor_copy(sh.identb[:, :], sh.ident[:, :]).then_inc(s.shared_set, 1)
                dve.wait_ge(s.tanh_ready, 1)
                c = norm_vector(nc, dve, sh, s)
                c.link(nc.vector.tensor_scalar(halfg[:, 1:2], tg, -0.5, None, ALU.mult))
                dve.wait_ge(s.fold_ps, 5)
                c.link(nc.vector.tensor_scalar(crow[:, :], b4[:, 0:B * SK], SC, None, ALU.mult))
                nc.vector.tensor_scalar(beta[:, :], b5[0:SK, 0:B], SC, None, ALU.mult).then_inc(s.set_ready, 1)
                dve.sem_inc(s.x_ready, 2)
                dve.wait_ge(s.fold_ready, 2 * DC)
                dve.wait_ge(s.r1_ready, B)
                PER = 30

                with dve.Fori(0, B) as b:
                    k = TileChain(dve, s.step, b, PER)
                    for j in range(TB):
                        normalise(nc, sh, xn[:, j, :], b * TB + j).then_inc(s.xn_ready, 1)
                    for kk in range(DC):
                        nc.vector.tensor_copy(qb[:, kk, :], queries[:, kk, ds(b * SK, SK)]).then_inc(s.qb_ready, 1)
                    dve.wait_ge(s.s2_ps, b + 1)
                    k.link(nc.vector.tensor_reduce(m2[:, :], s2_bank[0:SK, :], AX.X, ALU.max))
                    k.link(nc.vector.tensor_tensor(m2[:, :], m2[:, :], beta[:, ds(b, 1)], ALU.add))
                    nc.vector.tensor_tensor(nb2[:, :], beta[:, ds(b, 1)], m2[:, :], ALU.subtract).then_inc(s.nb2_ready, 1)
                    for g in range(NG):
                        bank = (b4, b5)[g]
                        pg = p1[:, g * GT:(g + 1) * GT, :]
                        dve.wait_ge(s.s1_ps, b * NG + (g + 1))
                        k.link(nc.vector.tensor_tensor(pg, bank[:, 0:GW].rearrange("p (h k) -> p h k", k=SK),
                                                       crow[:, ds(b * SK, SK)].unsqueeze(1).to_broadcast((P, GT, SK)), ALU.add))
                        k.link(nc.vector.tensor_reduce(mx[:, g * GT:(g + 1) * GT], pg, AX.X, ALU.max))
                        nc.vector.tensor_tensor(pg, pg, mx[:, g * GT:(g + 1) * GT].unsqueeze(2).to_broadcast((P, GT, SK)),
                                                ALU.subtract).then_inc(s.shift_ready, 1)
                    for g in range(NG):
                        pg = p1[:, g * GT:(g + 1) * GT, :]
                        dve.wait_ge(s.e1_ready, b * NG + (g + 1))
                        k.link(nc.vector.tensor_reduce(rs[:, g * GT:(g + 1) * GT], pg, AX.X, ALU.add))
                        nc.vector.reciprocal(ri[:, g * GT:(g + 1) * GT], rs[:, g * GT:(g + 1) * GT]).then_inc(s.inv1_ready, 1)
                    dve.wait_ge(s.e2_ready, b + 1)
                    k.link(nc.vector.reciprocal(inv2[:, :], sum2[:, :]))
                    dve.wait_ge(s.u_ps, b + 1)
                    nc.vector.tensor_scalar(uu[:, :], b6[0:SK, 0:D], inv2[:, 0:1], None, ALU.mult).then_inc(s.u_ready, 1)
                    dve.wait_ge(s.sc_ps, b + 1)
                    k.link(nc.vector.tensor_tensor(sc[:, :], b6[0:SK, 0:D], bvc[:, :], ALU.add))
                    k.link(nc.vector.tensor_scalar(r2[:, 0:D], sc[:, :], halfg[0:SK, 1:2], None, ALU.mult))
                    k.link(nc.vector.tensor_scalar(r3[:, :], sc[:, :], sh.gates[0:SK, 0:1], None, ALU.mult))
                    dve.wait_ge(s.sg_ps, b + 1)
                    nc.vector.tensor_tensor(r2[:, D:2 * D], b7[0:SK, 0:D], bgr[:, :], ALU.add).then_inc(s.r2_ready, 1)
                    for j in range(TB):
                        u = j % 2
                        n = b * TB + j
                        dve.wait_ge(s.th_ready, n + 1)
                        k.link(nc.vector.scalar_tensor_tensor(tmp[:, u, :], th[:, u, :], 1.0, s2_bank[:, u * 512:u * 512 + D],
                                                              ALU.add, ALU.mult))
                        k.link(nc.vector.tensor_tensor(tmp[:, u, :], tmp[:, u, :], (b0, b1)[u][:, 0:D], ALU.add))
                        nc.vector.tensor_tensor(x_tile(sh, n), tmp[:, u, :], x_tile(sh, n), ALU.add).then_inc(s.x_ready, 1)
                        dve.wait_ge(s.x_ready, n + 3)
                        tile_stats(nc, sh, n).then_inc(s.stats_ready, 1)
                    assert k.n <= PER
                    if k.n < PER:
                        dve.sem_inc(s.step, PER - k.n)
                dve.wait_ge(s.stats_ready, T)

            @block.gpsimd
            def _(pool):
                c = Chain(pool, s.r1_step)
                pool.wait_ge(s.small_loaded, 160)
                pool.wait_ge(s.half_ready, 1)
                for b in range(B):
                    pool.wait_ge(s.v_ready, b + 1)
                    v = r1[:, b * 2 * D:b * 2 * D + D]
                    c.link(nc.gpsimd.tensor_tensor(v, v, bvs[:, :], ALU.add))
                    nc.gpsimd.tensor_scalar(v, v, halfg[0:SK, 0:1], None, ALU.mult).then_inc(s.r1_ready, 1)
                with pool.Fori(0, B) as b:
                    for g in range(NG):
                        pg = p1[:, g * GT:(g + 1) * GT, :]
                        pool.wait_ge(s.inv1_ready, b * NG + (g + 1))
                        nc.gpsimd.tensor_tensor(pg, pg, ri[:, g * GT:(g + 1) * GT].unsqueeze(2).to_broadcast((P, GT, SK)),
                                                ALU.mult).then_inc(s.p1_ready, 1)

            @block.tensor
            def _(pe):
                pe.wait_ge(s.w_loaded, 64)
                for n, (name, at) in enumerate((("wk_s", 0), ("wq_s", 1), ("wv_s", 2))):
                    for m in range(DC):
                        bank = [b0, b1, b4, b5, b6, b7][2 * n + m]
                        for k in range(DC):
                            ins = nc.tensor.matmul(bank[:, 0:B * SK], w[name][:, k, m * P:(m + 1) * P], sh.ctx_t[:, k, :],
                                                   start=(k == 0), stop=(k == DC - 1))
                        ins.then_inc(s.pre_ps, 1)
                pe.wait_ge(s.pre_ready, 6)
                pe.wait_ge(s.rest_loaded, 64)
                for n, (name, src) in enumerate((("wq", kst), ("wk", qst))):
                    for m in range(DC):
                        bank = (b0, b1)[m] if n == 0 else s2_bank[:, m * 512:(m + 1) * 512]
                        for k in range(DC):
                            ins = nc.tensor.matmul(bank[:, 0:B * SK], w[name][:, k, m * P:(m + 1) * P], src[:, k, :],
                                                   start=(k == 0), stop=(k == DC - 1))
                        ins.then_inc(s.fold_ps, 1)
                pe.wait_ge(s.set_ready, 1)
                for k in range(DC):
                    nc.tensor.matmul(b4[:, 0:B * SK], bqb[:, k, :], kst[:, k, :], start=(k == 0), stop=(k == DC - 1))
                for b in range(B):
                    for k in range(DC):
                        ins = nc.tensor.matmul(b5[0:SK, b:b + 1], qst[:, k, b * SK:(b + 1) * SK], bkc[:, k:k + 1],
                                               start=(k == 0), stop=(k == DC - 1))
                ins.then_inc(s.fold_ps, 1)
                for b in range(B):
                    bank = (b6, b7)[b % 2]
                    if b >= 2:
                        pe.wait_ge(s.v_ready, b - 1)
                    for k in range(DC):
                        nc.tensor.matmul(bank[0:SK, 0:D], sh.ctx_t[:, k, b * SK:(b + 1) * SK], w["wv_s"][:, k, :],
                                         start=(k == 0), stop=(k == DC - 1))
                    for k in range(DC):
                        ins = nc.tensor.matmul(bank[0:SK, D:2 * D], vst[:, k, b * SK:(b + 1) * SK], wg[:, k, :],
                                               start=(k == 0), stop=(k == DC - 1))
                    ins.then_inc(s.v_ps, 1)
                pe.wait_ge(s.fold_ready, 4)
                pe.wait_ge(s.set_ready, 2)
                pe.wait_ge(s.ident_loaded, 16)
                pe.wait_ge(s.r1_ready, B)
                pe.sem_inc(s.xt_ps, 2)

                with pe.Fori(0, B) as b:
                    for j in range(TB):
                        n = b * TB + j
                        pe.wait_ge(s.xn_ready, n + 1)
                        pe.wait_ge(s.xt_ready, n + 1)
                        for c in range(DC):
                            ins = nc.tensor.transpose((b0, b1)[j % 2][:, c * P:(c + 1) * P], xn[:, j, c * P:(c + 1) * P], sh.ident[:, :])
                        ins.then_inc(s.xt_ps, 1)
                    pe.wait_ge(s.xt_ready, b * TB + (TB + 2))
                    pe.wait_ge(s.qb_ready, b * DC + DC)
                    for j in range(2):
                        for k in range(DC):
                            ins = nc.tensor.matmul(s2_bank[0:SK, j * 512:(j + 1) * 512], qb[:, k, :],
                                                   xt[:, k, j * 512:(j + 1) * 512], start=(k == 0), stop=(k == DC - 1))
                    ins.then_inc(s.s2_ps, 1)
                    for g in range(NG):
                        for j in range(GT):
                            for k in range(DC):
                                ins = nc.tensor.matmul((b4, b5)[g][:, j * SK:(j + 1) * SK],
                                                       xt[:, k, (g * GT + j) * P:(g * GT + j + 1) * P],
                                                       keys[:, ds(b * SK + k * B * SK, SK)], start=(k == 0), stop=(k == DC - 1))
                        ins.then_inc(s.s1_ps, 1)
                    pe.wait_ge(s.e2_ready, b + 1)
                    for g in range(NG):
                        for j in range(GT):
                            t = g * GT + j
                            ins = nc.tensor.transpose((b0, b1)[g][:, j * SK:(j + 1) * SK], p2[:, t * P:(t + 1) * P], sh.ident[0:SK, 0:SK])
                        ins.then_inc(s.p2t_ps, 1)
                    for t in range(TB):
                        if t % GT == 0:
                            pe.wait_ge(s.p2t_ready, b * NG + (t // GT + 1))
                        ins = nc.tensor.matmul(b6[0:SK, 0:D], p2t[:, t, :], xn[:, t, :], start=(t == 0), stop=(t == TB - 1))
                    ins.then_inc(s.u_ps, 1)
                    for g in range(NG):
                        pe.wait_ge(s.p1_ready, b * NG + (g + 1))
                        for j in range(GT):
                            ins = nc.tensor.transpose((b4, b5)[g][0:SK, j * P:(j + 1) * P], p1[:, g * GT + j, :], sh.ident[:, :])
                        ins.then_inc(s.p1t_ps, 1)
                    pe.wait_ge(s.u_ready, b + 1)
                    for k in range(DC):
                        ins = nc.tensor.transpose(b7[:, k * SK:(k + 1) * SK], uu[:, k * P:(k + 1) * P], sh.ident[0:SK, 0:SK])
                    ins.then_inc(s.ut_ps, 1)
                    pe.wait_ge(s.ut_ready, b + 1)
                    for m in range(DC):
                        for k in range(DC):
                            nc.tensor.matmul(b7[:, m * SK:(m + 1) * SK], w["wv_c"][:, k, m * P:(m + 1) * P], ut[:, k, :],
                                             start=(k == 0), stop=(k == DC - 1))
                    for k in range(DC):
                        ins = nc.tensor.matmul(b6[0:SK, 0:D], ut[:, k, :], w["wv_c"][:, k, :], start=(k == 0), stop=(k == DC - 1))
                    ins.then_inc(s.sc_ps, 1)
                    pe.wait_ge(s.sct_ready, b * DC + DC)
                    for k in range(DC):
                        ins = nc.tensor.matmul(b7[0:SK, 0:D], sct[:, k, :], wg[:, DC + k, :], start=(k == 0), stop=(k == DC - 1))
                    ins.then_inc(s.sg_ps, 1)
                    pe.wait_ge(s.r2_ready, b + 1)
                    pe.wait_ge(s.p1t_ready, b * NG + NG)
                    for j in range(TB):
                        u = j % 2
                        pe.wait_ge(s.x_ready, b * TB + (j + 1))
                        nc.tensor.matmul(s2_bank[:, u * 512:(u + 1) * 512], p1t[:, j, :], r1[:, ds(b * 2 * D, 2 * D)], start=True, stop=False)
                        nc.tensor.matmul(s2_bank[:, u * 512:(u + 1) * 512], interp[:, j * P:(j + 1) * P], r2[:, :], start=False, stop=True)
                        nc.tensor.matmul((b0, b1)[u][:, 0:D], interp[:, j * P:(j + 1) * P], r3[:, :],
                                         start=True, stop=True).then_inc(s.c_ps, 1)

            @block.scalar
            def _(act):
                act.dma_start(sh.gates[:, 0:4], io.g_xattn.partition_broadcast(P)).then_inc(s.gates_loaded, 16)
                act.dma_start(sh.gates[:, 4:8], io.g_ffn.partition_broadcast(P)).then_inc(s.gates_loaded, 16)
                for n, src in (("wq", io.L0_xattn_Wq_c), ("wk", io.L0_xattn_Wk_c), ("wv_c", io.L0_xattn_Wv_c_T)):
                    act.dma_start(w[n][:, :, :], weight_view(src)).then_inc(s.rest_loaded, 16)
                act.dma_start(wg[:, :, :], weight_view(io.L0_xattn_Wg_T)).then_inc(s.rest_loaded, 16)
                act.dma_start(sh.ident[:, :], io.identity).then_inc(s.ident_loaded, 16)
                act.wait_ge(s.gates_loaded, 32)
                nc.scalar.activation(sh.gates[:, :], sh.gates[:, :], ACT.Tanh).then_inc(s.tanh_ready, 1)
                act.wait_ge(s.small_loaded, 160)
                for n, (dst, bias) in enumerate(((kst, bks), (qst, bqs), (vst, bvs_c))):
                    for m in range(DC):
                        bank = [b0, b1, b4, b5, b6, b7][2 * n + m]
                        act.wait_ge(s.pre_ps, 2 * n + m + 1)
                        nc.scalar.activation(dst[:, m, :], bank[:, 0:B * SK], ACT.Identity, bias=bias[:, m:m + 1]).then_inc(s.pre_ready, 1)
                for n, dst in enumerate((keys[:, :].rearrange("p (c n) -> p c n", c=DC), queries[:, :, :])):
                    for m in range(DC):
                        bank = (b0, b1)[m] if n == 0 else s2_bank[:, m * 512:(m + 1) * 512]
                        act.wait_ge(s.fold_ps, 2 * n + m + 1)
                        nc.scalar.activation(dst[:, m, :], bank[:, 0:B * SK], ACT.Copy, scale=SC).then_inc(s.fold_ready, 1)
                for b in range(B):
                    act.wait_ge(s.v_ps, b + 1)
                    nc.scalar.activation(r1[:, b * 2 * D:(b + 1) * 2 * D], (b6, b7)[b % 2][0:SK, :], ACT.Copy).then_inc(s.v_ready, 1)
                act.sem_inc(s.xt_ready, 2)
                with act.Fori(0, B) as b:
                    for j in range(TB):
                        n = b * TB + j
                        act.wait_ge(s.xt_ps, n + 3)
                        nc.scalar.activation(xt[:, :, j * P:(j + 1) * P], (b0, b1)[j % 2][:, 0:D].rearrange("p (c n) -> p c n", c=DC),
                                             ACT.Copy).then_inc(s.xt_ready, 1)
                    act.wait_ge(s.nb2_ready, b + 1)
                    nc.scalar.activation(p2[:, :], s2_bank[0:SK, :], ACT.Exp, bias=nb2[:, 0:1], accum_out=sum2[:, :]).then_inc(s.e2_ready, 1)
                    for g in range(NG):
                        act.wait_ge(s.shift_ready, b * NG + (g + 1))
                        pg = p1[:, g * GT:(g + 1) * GT, :]
                        nc.scalar.activation(pg, pg, ACT.Exp).then_inc(s.e1_ready, 1)
                    for g in range(NG):
                        act.wait_ge(s.p2t_ps, b * NG + (g + 1))
                        nc.scalar.activation(p2t[:, g * GT:(g + 1) * GT, :], (b0, b1)[g][:, 0:GW].rearrange("p (h k) -> p h k", k=SK),
                                             ACT.Copy).then_inc(s.p2t_ready, 1)
                    for g in range(NG):
                        act.wait_ge(s.p1t_ps, b * NG + (g + 1))
                        nc.scalar.activation(p1t[:, g * GT:(g + 1) * GT, :], (b4, b5)[g][0:SK, :].rearrange("p (h k) -> p h k", k=P),
                                             ACT.Copy).then_inc(s.p1t_ready, 1)
                    act.wait_ge(s.ut_ps, b + 1)
                    nc.scalar.activation(ut[:, :, :], b7[:, 0:DC * SK].rearrange("p (c n) -> p c n", c=DC), ACT.Copy).then_inc(s.ut_ready, 1)
                    act.wait_ge(s.sc_ps, b + 1)
                    for m in range(DC):
                        nc.scalar.activation(sct[:, m, :], b7[:, m * SK:(m + 1) * SK], ACT.Identity, bias=bvc_c[:, m:m + 1]).then_inc(s.sct_ready, 1)
                    for j in range(TB):
                        u = j % 2
                        n = b * TB + j
                        act.wait_ge(s.c_ps, n + 1)
                        act.wait_ge(s.x_ready, n + 1)
                        nc.scalar.activation(th[:, u, :], s2_bank[:, u * 512 + D:(u + 1) * 512], ACT.Tanh, scale=0.5).then_inc(s.th_ready, 1)


def stage_l1_ffn(nc, io, sh):
    s = scope(nc, "l1f")
    with s.ctx:
        norm_sems(s)
        w = s.sb("w", [P, DC, D])
        neg = s.sb("neg", [P, DC, D])
        alpha = s.sb("alpha", [P, 1])
        bias = s.sb("bias", [P, D])
        wsum = s.sb("wsum", [P, 1])
        delta = s.sb("delta", [P, 2])
        xn = s.sb("xn", [P, AHEAD, D])
        xt = s.sb("xt", [P, AHEAD, D])
        ps_t = [s.ps(f"ps_t{u}", [P, D]) for u in range(AHEAD)]
        ps_y = [s.ps(f"ps_y{u}", [P, D]) for u in range(AHEAD)]
        ps_w = s.ps("ps_w", [P, 8])
        loaded, wsum_ready, wtot_ready = s.sem("loaded"), s.sem("wsum_ready"), s.sem("wtot_ready")
        step = s.sem("step")
        w_ready = s.sem("w_ready")
        xn_ready, xt_ps, xt_ready, y_ready = s.sem("xn_ready"), s.sem("xt_ps"), s.sem("xt_ready"), s.sem("y_ready")
        biased, x_ready, stats_ready = s.sem("biased"), s.sem("x_ready"), s.sem("stats_ready")
        tg = sh.gates[:, 5:6]

        with nc.Block() as block:
            @block.sync
            def _(sp):
                sp.dma_start(w[:, :, :], weight_view(io.L1_ffn_weight_T)).then_inc(loaded, 16)
                sp.dma_start(alpha[:, :], io.L1_ffn_alpha.partition_broadcast(P)).then_inc(loaded, 16)
                sp.dma_start(bias[:, :], io.L1_ffn_bias.partition_broadcast(P)).then_inc(loaded, 16)

            @block.vector
            def _(dve):
                c = norm_vector(nc, dve, sh, s)
                dve.wait_ge(loaded, 48)
                nc.vector.tensor_reduce(wsum[:, :], w[:, :, :], AX.XY, ALU.add,
                                        apply_absolute_value=True).then_inc(wsum_ready, 1)
                dve.wait_ge(wtot_ready, 1)
                c.link(nc.vector.tensor_scalar(delta[:, 0:1], ps_w[:, 0:1], 1.0 / (D * D), 0.7, ALU.mult, ALU.mult))
                c.link(nc.vector.tensor_scalar(delta[:, 1:2], delta[:, 0:1], -1.0, None, ALU.mult))
                c.link(nc.vector.tensor_scalar(neg[:, :, :], w[:, :, :], delta[:, 1:2], None, ALU.is_lt))
                c.link(nc.vector.scalar_tensor_tensor(w[:, :, :], w[:, :, :], delta[:, 0:1], neg[:, :, :],
                                                      ALU.is_gt, ALU.subtract))
                nc.vector.tensor_scalar(w[:, :, :], w[:, :, :], alpha[:, 0:1], tg, ALU.mult,
                                        ALU.mult).then_inc(w_ready, 1)
                c.link(nc.vector.tensor_scalar(bias[:, :], bias[:, :], tg, None, ALU.mult))
                dve.sem_inc(xn_ready, AHEAD)
                dve.sem_inc(x_ready, AHEAD)

                def front(t, u):
                    dve.wait_ge(xt_ps, ev(t, back=2))
                    normalise(nc, sh, xn[:, u, :], t).then_inc(xn_ready, 1)

                def back(t, u):
                    dve.wait_ge(y_ready, ev(t))
                    dve.wait_ge(biased, ev(t))
                    nc.vector.tensor_tensor(x_tile(sh, t), ps_y[u][:, :], x_tile(sh, t), ALU.add).then_inc(x_ready, 1)
                    dve.wait_ge(x_ready, ev(t))
                    tile_stats(nc, sh, t).then_inc(stats_ready, 1)

                pipeline(dve, T, [(back, 0), (front, 4)])
                dve.wait_ge(stats_ready, T)

            @block.gpsimd
            def _(pool):
                pool.wait_ge(w_ready, 1)
                pool.wait_ge(xn_ready, AHEAD)
                pool.sem_inc(biased, AHEAD)

                def part(t, u):
                    pool.wait_ge(xn_ready, ev(t))
                    nc.gpsimd.tensor_tensor(x_tile(sh, t), x_tile(sh, t), bias[:, :], ALU.add).then_inc(biased, 1)

                pipeline(pool, T, [(part, 0)])

            @block.tensor
            def _(pe):
                pe.wait_ge(wsum_ready, 1)
                nc.tensor.matmul(ps_w[:, 0:1], sh.ones[:, :], wsum[:, :], start=True, stop=True).then_inc(wtot_ready, 1)
                pe.wait_ge(w_ready, 1)
                pe.sem_inc(xt_ps, AHEAD)
                pe.sem_inc(y_ready, AHEAD)

                def front(t, u):
                    pe.wait_ge(xn_ready, ev(t))
                    pe.wait_ge(xt_ready, ev(t, back=2))
                    for c in range(DC):
                        ins = nc.tensor.transpose(ps_t[u][:, c * P:(c + 1) * P], xn[:, u, c * P:(c + 1) * P], sh.ident[:, :])
                    ins.then_inc(xt_ps, 1)

                def back(t, u):
                    pe.wait_ge(xt_ready, ev(t))
                    pe.wait_ge(x_ready, ev(t, back=2))
                    for c in range(DC):
                        ins = nc.tensor.matmul(ps_y[u][:, :], xt[:, u, c * P:(c + 1) * P], w[:, c, :],
                                               start=(c == 0), stop=(c == DC - 1))
                    ins.then_inc(y_ready, 1)

                pipeline(pe, T, [(back, 0), (front, 2)])

            @block.scalar
            def _(act):
                act.sem_inc(xt_ready, AHEAD)

                def part(t, u):
                    act.wait_ge(xt_ps, ev(t))
                    act.wait_ge(y_ready, ev(t, back=2))
                    nc.scalar.activation(xt[:, u, :], ps_t[u][:, :], ACT.Copy).then_inc(xt_ready, 1)

                pipeline(act, T, [(part, 0)])


NF = S // 2 + 1
N0, N2, N1 = S // 8 + 1, S // 8, S // 4
NE = N0 + N2
FW = 103
FT = -(-NF // FW)
NFP = FT * FW
KINDS = [[f for f in range(FT) if f * FW < hi and (f + 1) * FW > lo] for lo, hi in ((0, N0), (N0, NE), (NE, NF))]
HT, QT = TB // 2, TB // 4
KF = SK // 2 + 1


def stage_l1_xattn(nc, io, sh):
    s = scope(nc, "l1x")
    GW = HH * KF
    NG = DC
    W = 104
    NW = HEADS * KF // W
    HWN = GW // W
    CUT = [(2 * N0, 0), (2 * N2, N0), (2 * N1, NE)]
    NS = 3
    HALF = [(0, 258), (258, NFP)]
    with s.ctx:
        norm_sems(s)
        w = {n: s.sb(n, [P, DC, D]) for n in ("Wkr", "Wki", "Wvr", "Wvi", "Wqr", "Wqi", "Wo")}
        bias = {n: s.sb(n, [P, DC]) for n in ("bqr", "bqi", "bkr", "bki", "gamma", "beta")}
        fwd_even = s.sb("fwd_even", [P, QT, 2 * NE])
        fwd_odd = s.sb("fwd_odd", [P, HT, 2 * N1])
        inv_even = s.sb("inv_even", [FW, 2, 2 * len(KINDS[0]), S // 4])
        inv_odd = s.sb("inv_odd", [FW, 2 * len(KINDS[2]), S // 2])
        f77 = s.sb("f77", [SK, 2 * KF])
        ctx = s.sb("ctx", [SK, B, D])
        hm = s.sb("hm", [P, HH])
        kvf = s.sb("kvf", [P, DC, B * 2 * KF])
        kt = s.sb("kt", [P, 2, DC, B * KF])
        vt = s.sb("vt", [P, 2, DC, B * KF])
        bvrow = s.sb("bvrow", [FW, DC, 2, P])
        kbd = s.sb("kbd", [P, 2, DC, GW])
        vbd = s.sb("vbd", [P, 2, DC, GW])
        vrow = s.sb("vrow", [W, NW, 2 * P])
        v2, scale2, shift2 = s.sb("v2", [P, T]), s.sb("scale2", [P, T]), s.sb("shift2", [P, T])
        xn = s.sb("xn", [P, 2, 2, D])
        halves = s.sb("halves", [P, HT, 2, D])
        quarters = s.sb("quarters", [P, QT, 2, D])
        part, even = s.sb("part", [P, S // 4]), s.sb("even", [P, S // 2])
        qf = s.sb("qf", [P, DC, 2, NFP])
        qt = s.sb("qt", [P, 2, DC, NFP])
        pr = s.sb("pr", [FW, NS, HEADS * KF])
        mx, rs, ri = (s.sb(n, [FW, NS, HEADS]) for n in ("mx", "rs", "ri"))
        pt = s.sb("pt", [W, 2, NW, FW])
        of = s.sb("of", [FW, FT, DC, 2, P])
        yt = s.sb("yt", [P, DC, S])
        bank = [s.ps(f"bank{k}", [P, 512]) for k in range(8)]
        for n in ["w_loaded", "small_loaded", "fwd_loaded", "inv_loaded", "kvf_ps", "kvf_ready", "kv_ps", "kv_ready",
                  "pad_set", "xn_ready", "halves_ready", "quarters_ready", "dft_ps", "qf_ready", "beta_ready", "q_ps", "q_ready",
                  "bd_ready", "v_ps", "v_ready", "s_ps", "max_ready", "shifted", "exp_ready", "sum_ready", "inv_ready",
                  "pt_ps", "pt_ready", "o_ps", "o_ready", "of_ready", "it_ps", "yt_ready", "y_ps", "x_ready", "stats_ready"]:
            s[n] = s.sem(n)
        tg = sh.gates[:, 1:2]
        SMALL = 16 * (5 + len(bias))

        def heads(ap):
            return ap.rearrange("p (h k) -> p h k", k=KF)

        def per_head(t_, u, g):
            return t_[:, u, g * HH:(g + 1) * HH].unsqueeze(2).to_broadcast((FW, HH, KF))

        def at(b, per, k):
            return b * per + (k + 1)

        with nc.Block() as block:
            @block.sync
            def _(sp):
                sp.dma_start(ctx[:, :, :], io.ctx.rearrange("b k d -> k b d")).then_inc(s.small_loaded, 16)
                sp.dma_start(f77[:, :], io.fourier_context).then_inc(s.small_loaded, 16)
                sp.dma_start(hm[:, :], io.head_mask).then_inc(s.small_loaded, 16)
                for r, n in enumerate(("bvr", "bvi")):
                    sp.dma_start(bvrow[:, :, r, :], io[f"L1_xattn_{n}_row"].partition_broadcast(FW)).then_inc(s.small_loaded, 16)
                for n, a in bias.items():
                    sp.dma_start(a[:, :], io[f"L1_xattn_{n}_cols"]).then_inc(s.small_loaded, 16)
                for n, a in w.items():
                    sp.dma_start(a[:, :, :], weight_view(io[f"L1_xattn_{n}_T"])).then_inc(s.w_loaded, 16)
                sp.dma_start(fwd_even[:, :, :], io.fourier_even.rearrange("(j p) n -> p j n", p=P)).then_inc(s.fwd_loaded, 16)
                sp.dma_start(fwd_odd[:, :, :], io.fourier_odd.rearrange("(j p) n -> p j n", p=P)).then_inc(s.fwd_loaded, 16)
                sp.dma_start(inv_even[:, :, :, :], io.inverse_even.rearrange("k f p n -> p k f n")).then_inc(s.inv_loaded, 16)
                sp.dma_start(inv_odd[:, :, :], io.inverse_odd.rearrange("f p n -> p f n")).then_inc(s.inv_loaded, 16)

            @block.vector
            def _(dve):
                c = norm_vector(nc, dve, sh, s)
                c.link(nc.vector.tensor_tensor(v2[:, :], sh.rstd[:, :], sh.rstd[:, :], ALU.mult))
                c.link(nc.vector.tensor_tensor(v2[:, :], v2[:, :], sh.var[:, :], ALU.mult))
                c.link(nc.vector.tensor_scalar(v2[:, :], v2[:, :], EPS, None, ALU.add))
                inverse_root(nc, c, scale2[:, :], v2[:, :], sh.norm_a[:, :])
                c.link(nc.vector.tensor_tensor(scale2[:, :], scale2[:, :], sh.rstd[:, :], ALU.mult))
                c.link(nc.vector.scalar_tensor_tensor(shift2[:, :], sh.mean[:, :], -1.0, scale2[:, :], ALU.mult, ALU.mult))
                dve.wait_ge(s.small_loaded, SMALL)
                for n in ("bkr", "bki"):
                    c.link(nc.vector.tensor_scalar(bias[n][:, :], bias[n][:, :], HD ** -0.5, None, ALU.mult))
                c.link(nc.vector.tensor_scalar(bias["beta"][:, :], bias["beta"][:, :], float(S) ** 0.5, None, ALU.mult))
                c.link(nc.vector.memset(qf[:, :, :, NF:NFP], 0.0))
                dve.sem_inc(s.pad_set, 1)
                dve.wait_ge(s.kv_ready, 8)
                hmb = hm[:, :].unsqueeze(2).to_broadcast((P, HH, KF))
                for n in (s.halves_ready, s.quarters_ready, s.beta_ready, s.bd_ready, s.max_ready, s.shifted, s.sum_ready, s.inv_ready, s.o_ready,
                          s.yt_ready, s.x_ready):
                    dve.sem_inc(n, 1)

                def prepare(b):
                    for j in range(HT):
                        for h in range(2):
                            n = b * TB + (h * HT + j)
                            nc.vector.tensor_scalar(xn[:, j % 2, h, :], x_tile(sh, n), scale2[:, ds(n, 1)], shift2[:, ds(n, 1)],
                                                    ALU.mult, ALU.add).then_inc(s.xn_ready, 1)
                        dve.wait_ge(s.xn_ready, b * TB + (2 * j + 2))
                        for h, op in enumerate((ALU.add, ALU.subtract)):
                            nc.vector.tensor_tensor(halves[:, j, h, :], xn[:, j % 2, 0, :], xn[:, j % 2, 1, :], op).then_inc(s.halves_ready, 1)
                    dve.wait_ge(s.halves_ready, at(b, TB, TB))
                    for j in range(QT):
                        for h, op in enumerate((ALU.add, ALU.subtract)):
                            nc.vector.tensor_tensor(quarters[:, j, h, :], halves[:, j, 0, :], halves[:, j + QT, 0, :], op).then_inc(s.quarters_ready, 1)
                    for r in range(2):
                        for k in range(DC):
                            for dst, src in ((kbd, kt), (vbd, vt)):
                                nc.vector.tensor_tensor(heads(dst[:, r, k, :]),
                                                        src[:, r, k, ds(b * KF, KF)].unsqueeze(1).to_broadcast((P, HH, KF)),
                                                        hmb, ALU.mult).then_inc(s.bd_ready, 1)

                def batch(b, last):
                    for k in range(DC):
                        dve.wait_ge(s.qf_ready, at(b, 6, 3 * k + 3))
                        nc.vector.tensor_scalar(qf[:, k, 0, 0:1], qf[:, k, 0, 0:1], bias["beta"][:, k:k + 1], None, ALU.add).then_inc(s.beta_ready, 1)

                    def shift(f):
                        u = f % NS
                        dve.wait_ge(s.pt_ps, at(b, FT * 2, 2 * (f - NS + 1) if f >= NS else 0))
                        for g in range(NG):
                            dve.wait_ge(s.s_ps, at(b, FT * NG, f * NG + g + 1))
                            nc.vector.tensor_reduce(mx[:, u, g * HH:(g + 1) * HH], heads(bank[g][0:FW, 0:GW]), AX.X, ALU.max).then_inc(s.max_ready, 1)
                            dve.wait_ge(s.max_ready, at(b, FT * NG, f * NG + g + 1))
                            nc.vector.tensor_tensor(heads(pr[:, u, g * GW:(g + 1) * GW]), heads(bank[g][0:FW, 0:GW]),
                                                    per_head(mx, u, g), ALU.subtract).then_inc(s.shifted, 1)

                    def sums(f):
                        u = f % NS
                        dve.wait_ge(s.exp_ready, at(b, FT * NG, f * NG + NG))
                        nc.vector.tensor_reduce(rs[:, u, :], heads(pr[:, u, :]), AX.X, ALU.add).then_inc(s.sum_ready, 1)
                        dve.wait_ge(s.sum_ready, at(b, FT, f + 1))
                        nc.vector.reciprocal(ri[:, u, :], rs[:, u, :]).then_inc(s.inv_ready, 1)

                    def result(f):
                        dve.wait_ge(s.o_ps, at(b, FT, f + 1))
                        dve.wait_ge(s.inv_ready, at(b, FT, f + 1))
                        for g in range(DC):
                            nc.vector.tensor_tensor(of[:, f, g, :, :].rearrange("p r (h d) -> p r h d", d=HD),
                                                    bank[4 + f % 2][0:FW, g * 2 * P:(g + 1) * 2 * P].rearrange("p (r h d) -> p r h d", r=2, d=HD),
                                                    ri[:, f % NS, g * HH:(g + 1) * HH].unsqueeze(1).unsqueeze(3).to_broadcast((FW, 2, HH, HD)),
                                                    ALU.mult).then_inc(s.o_ready, 1)

                    shift(0)
                    shift(1)
                    for f in range(FT):
                        if f + 2 < FT:
                            shift(f + 2)
                        sums(f)
                        result(f)
                    if not last:
                        prepare(b + 1)
                    for m in range(DC):
                        dve.wait_ge(s.it_ps, at(b, DC, m + 1))
                        kind0, kind2, odd = bank[2 * m][:, 0:S // 4], bank[2 * m][:, S // 4:S // 2], bank[2 * m + 1][:, :]
                        if m:
                            dve.wait_ge(s.yt_ready, at(b, 5 * DC, 5 * m))
                        nc.vector.tensor_copy(part[:, :], kind2).then_inc(s.yt_ready, 1)
                        dve.wait_ge(s.yt_ready, at(b, 5 * DC, 5 * m + 1))
                        nc.vector.tensor_tensor(even[:, 0:S // 4], kind0, part[:, :], ALU.add).then_inc(s.yt_ready, 1)
                        nc.vector.tensor_tensor(even[:, S // 4:], kind0, part[:, :], ALU.subtract).then_inc(s.yt_ready, 1)
                        dve.wait_ge(s.yt_ready, at(b, 5 * DC, 5 * m + 3))
                        nc.vector.tensor_tensor(yt[:, m, 0:S // 2], odd, even[:, :], ALU.add).then_inc(s.yt_ready, 1)
                        nc.vector.tensor_tensor(yt[:, m, S // 2:], even[:, :], odd, ALU.subtract).then_inc(s.yt_ready, 1)
                    for j in range(TB):
                        n = b * TB + j
                        dve.wait_ge(s.y_ps, n + 2)
                        nc.vector.scalar_tensor_tensor(x_tile(sh, n), bank[6 + j % 2][:, 0:D], tg, x_tile(sh, n),
                                                       ALU.mult, ALU.add).then_inc(s.x_ready, 1)
                        dve.wait_ge(s.x_ready, n + 2)
                        tile_stats(nc, sh, n).then_inc(s.stats_ready, 1)

                prepare(0)
                with dve.Fori(0, B - 1) as b:
                    batch(b, False)
                batch(B - 1, True)
                dve.wait_ge(s.stats_ready, T)

            @block.gpsimd
            def _(pool):
                pool.wait_ge(s.small_loaded, SMALL)
                pool.sem_inc(s.of_ready, 1)
                with pool.Fori(0, B) as b:
                    for f in range(FT):
                        pool.wait_ge(s.o_ready, at(b, FT * DC, f * DC + DC))
                        nc.gpsimd.tensor_tensor(of[:, f, :, :, :], of[:, f, :, :, :], bvrow[:, :, :, :], ALU.add).then_inc(s.of_ready, 1)

            @block.tensor
            def _(pe):
                pe.wait_ge(s.small_loaded, SMALL)
                for m in range(DC):
                    for b in range(B):
                        ins = nc.tensor.matmul(bank[m][:, b * 2 * KF:(b + 1) * 2 * KF], ctx[:, b, m * P:(m + 1) * P], f77[:, :],
                                               start=True, stop=True)
                    ins.then_inc(s.kvf_ps, 1)
                pe.wait_ge(s.w_loaded, 16 * 7)
                pe.wait_ge(s.kvf_ready, 2)
                for n, name in enumerate(("Wkr", "Wki", "Wvr", "Wvi")):
                    r = n % 2
                    for m in range(DC):
                        i = n * DC + m
                        if i >= 2:
                            pe.wait_ge(s.kv_ready, i - 1)
                        for k in range(DC):
                            part = kvf[:, k, :].rearrange("p (b r n) -> p b r n", b=B, r=2)[:, :, r, :]
                            ins = nc.tensor.matmul(bank[2 + m][:, 0:B * KF], w[name][:, k, m * P:(m + 1) * P], part,
                                                   start=(k == 0), stop=(k == DC - 1))
                        ins.then_inc(s.kv_ps, 1)
                pe.wait_ge(s.fwd_loaded, 32)
                pe.wait_ge(s.inv_loaded, 32)
                for n in (s.dft_ps, s.v_ps, s.q_ps, s.s_ps, s.pt_ps, s.o_ps, s.it_ps, s.y_ps):
                    pe.sem_inc(n, 1)

                with pe.Fori(0, B) as b:
                    pe.wait_ge(s.yt_ready, at(b, 5 * DC, 0))
                    for m in range(DC):
                        ch = slice(m * P, (m + 1) * P)
                        for j in range(HT):
                            if m == 0:
                                pe.wait_ge(s.halves_ready, at(b, TB, 2 * j + 2))
                            nc.tensor.matmul(bank[3 * m + 2][:, :], halves[:, j, 1, ch], fwd_odd[:, j, :],
                                             start=(j == 0), stop=(j == HT - 1))
                        for h in range(2):
                            for j in range(QT):
                                pe.wait_ge(s.quarters_ready, at(b, 2 * QT, 2 * j + h + 1))
                                ins = nc.tensor.matmul(bank[3 * m + h][:, 0:CUT[h][0]], quarters[:, j, h, ch],
                                                       fwd_even[:, j, 2 * CUT[h][1]:2 * CUT[h][1] + CUT[h][0]],
                                                       start=(j == 0), stop=(j == QT - 1))
                        ins.then_inc(s.dft_ps, 1)
                    pe.wait_ge(s.bd_ready, at(b, 8, 8))
                    for i in range(NW):
                        k, col = i // HWN, (i % HWN) * W
                        if i >= 2:
                            pe.wait_ge(s.v_ready, at(b, NW, i - 1))
                        else:
                            pe.wait_ge(s.x_ready, at(b, TB, 0))
                        for r in range(2):
                            ins = nc.tensor.transpose(bank[6 + i % 2][0:W, r * P:(r + 1) * P], vbd[:, r, k, col:col + W], sh.ident[:, :])
                        ins.then_inc(s.v_ps, 1)
                    pe.wait_ge(s.v_ready, at(b, NW, NW))
                    pe.wait_ge(s.beta_ready, at(b, DC, DC))
                    for i in range(8):
                        r, m, (lo, hi) = i // 4, i // 2 % 2, HALF[i % 2]
                        if i >= 2:
                            pe.wait_ge(s.q_ready, at(b, 8, i - 1))
                        for k in range(DC):
                            ins = nc.tensor.matmul(bank[6 + i % 2][:, 0:hi - lo], w[("Wqr", "Wqi")[r]][:, k, m * P:(m + 1) * P],
                                                   qf[:, k, r, lo:hi], start=(k == 0), stop=(k == DC - 1))
                        ins.then_inc(s.q_ps, 1)
                    pe.wait_ge(s.q_ready, at(b, 8, 8))

                    def scores(f):
                        for g in range(NG):
                            if f:
                                pe.wait_ge(s.shifted, at(b, FT * NG, (f - 1) * NG + g + 1))
                            for r in range(2):
                                ins = nc.tensor.matmul(bank[g][0:FW, 0:GW], qt[:, r, g, f * FW:(f + 1) * FW], kbd[:, r, g, :],
                                                       start=(r == 0), stop=(r == 1))
                            ins.then_inc(s.s_ps, 1)

                    def values(f):
                        for g in range(DC):
                            pe.wait_ge(s.exp_ready, at(b, FT * NG, f * NG + g + 1))
                            if f:
                                pe.wait_ge(s.pt_ready, at(b, FT * DC, (f - 1) * DC + g + 1))
                            for i in range(HWN):
                                ins = nc.tensor.transpose(bank[2 + g][0:W, i * FW:(i + 1) * FW],
                                                          pr[:, f % NS, (g * HWN + i) * W:(g * HWN + i + 1) * W], sh.ident[0:FW, 0:FW])
                            ins.then_inc(s.pt_ps, 1)
                        if f >= 2:
                            pe.wait_ge(s.o_ready, at(b, FT * DC, (f - 1) * DC))
                        for g in range(DC):
                            pe.wait_ge(s.pt_ready, at(b, FT * DC, f * DC + g + 1))
                            for i in range(HWN):
                                ins = nc.tensor.matmul(bank[4 + f % 2][0:FW, g * 2 * P:(g + 1) * 2 * P], pt[:, f % 2, g * HWN + i, :],
                                                       vrow[:, g * HWN + i, :], start=(i == 0), stop=(i == HWN - 1))
                        ins.then_inc(s.o_ps, 1)

                    scores(0)
                    scores(1)
                    for f in range(FT):
                        if f + 2 < FT:
                            scores(f + 2)
                        values(f)
                    for m in range(DC):
                        for kind in range(3):
                            out = bank[2 * m + 1][:, :] if kind == 2 else bank[2 * m][:, kind * S // 4:(kind + 1) * S // 4]
                            for n, f in enumerate(KINDS[kind]):
                                pe.wait_ge(s.of_ready, at(b, FT, f + 1))
                                for r in range(2):
                                    table = inv_odd[:, 2 * n + r, :] if kind == 2 else inv_even[:, kind, 2 * n + r, :]
                                    ins = nc.tensor.matmul(out, of[:, f, m, r, :], table, start=(n == 0 and r == 0),
                                                           stop=(r == 1 and n == len(KINDS[kind]) - 1))
                        ins.then_inc(s.it_ps, 1)
                    for j in range(TB):
                        if j < 2:
                            pe.wait_ge(s.yt_ready, at(b, 5 * DC, 5 * DC))
                        else:
                            pe.wait_ge(s.x_ready, at(b, TB, j - 1))
                        for k in range(DC):
                            ins = nc.tensor.matmul(bank[6 + j % 2][:, 0:D], yt[:, k, j * P:(j + 1) * P], w["Wo"][:, k, :],
                                                   start=(k == 0), stop=(k == DC - 1))
                        ins.then_inc(s.y_ps, 1)

            @block.scalar
            def _(act):
                act.wait_ge(s.small_loaded, SMALL)
                act.wait_ge(s.pad_set, 1)
                for m in range(DC):
                    act.wait_ge(s.kvf_ps, m + 1)
                    nc.scalar.activation(kvf[:, m, :], bank[m][:, 0:B * 2 * KF], ACT.Copy).then_inc(s.kvf_ready, 1)
                for i in range(8):
                    n, m = i // DC, i % DC
                    act.wait_ge(s.kv_ps, i + 1)
                    src = bank[2 + m][:, 0:B * KF]
                    if n < 2:
                        nc.scalar.activation(kt[:, n, m, :], src, ACT.Identity, scale=HD ** -0.5,
                                             bias=bias[("bkr", "bki")[n]][:, m:m + 1]).then_inc(s.kv_ready, 1)
                    else:
                        nc.scalar.activation(vt[:, n - 2, m, :], src, ACT.Copy).then_inc(s.kv_ready, 1)
                for n in (s.qf_ready, s.v_ready, s.q_ready, s.exp_ready, s.pt_ready):
                    act.sem_inc(n, 1)
                with act.Fori(0, B) as b:
                    act.wait_ge(s.q_ps, at(b, 8, 0))
                    for m in range(DC):
                        act.wait_ge(s.dft_ps, at(b, DC, m + 1))
                        for i in range(3):
                            n, first = CUT[i]
                            dst = qf[:, m, :, first:first + n // 2]
                            src = bank[3 * m + i][:, 0:n].rearrange("p (r n) -> p r n", r=2)
                            nc.scalar.activation(dst, src, ACT.Copy, scale=bias["gamma"][:, m:m + 1]).then_inc(s.qf_ready, 1)
                    for i in range(NW):
                        act.wait_ge(s.v_ps, at(b, NW, i + 1))
                        nc.scalar.activation(vrow[:, i, :], bank[6 + i % 2][0:W, 0:2 * P], ACT.Copy).then_inc(s.v_ready, 1)
                    for i in range(8):
                        r, m, (lo, hi) = i // 4, i // 2 % 2, HALF[i % 2]
                        act.wait_ge(s.q_ps, at(b, 8, i + 1))
                        nc.scalar.activation(qt[:, r, m, lo:hi], bank[6 + i % 2][:, 0:hi - lo], ACT.Identity,
                                             bias=bias[("bqr", "bqi")[r]][:, m:m + 1]).then_inc(s.q_ready, 1)

                    def exps(f):
                        for g in range(NG):
                            act.wait_ge(s.shifted, at(b, FT * NG, f * NG + g + 1))
                            pg = pr[:, f % NS, g * GW:(g + 1) * GW]
                            nc.scalar.activation(pg, pg, ACT.Exp).then_inc(s.exp_ready, 1)

                    def copy_p(f):
                        for g in range(DC):
                            act.wait_ge(s.pt_ps, at(b, FT * DC, f * DC + g + 1))
                            nc.scalar.activation(pt[:, f % 2, g * HWN:(g + 1) * HWN, :],
                                                 bank[2 + g][0:W, 0:HWN * FW].rearrange("p (a b) -> p a b", b=FW),
                                                 ACT.Copy).then_inc(s.pt_ready, 1)

                    exps(0)
                    exps(1)
                    for f in range(FT):
                        copy_p(f)
                        if f + 2 < FT:
                            exps(f + 2)


def stage_l3_ffn(nc, io, sh, out):
    s = scope(nc, "l3f")
    G = 512
    NJ = S // G
    HU = NJ * DC
    with s.ctx:
        norm_sems(s)
        wx = s.sb("wx", [P, 3, DC, D])
        wc = s.sb("wc", [P, 3, DC, D])
        wo = s.sb("wo", [P, DC, D])
        uo = s.sb("uo", [P, DC, D])
        bg = s.sb("bg", [P, 3, DC])
        c0 = s.sb("c0", [P, DC])
        bo = s.sb("bo", [P, D])
        xt_all = s.sb("xt_all", [P, DC, B * S])
        ct = s.sb("ct", [P, 2, DC, S])
        gate = s.sb("gate", [P, 2, 3, G])
        prod = s.sb("prod", [P, 2, 2, G])
        xn = s.sb("xn", [P, AHEAD, D])
        cu = s.sb("cu", [P, TB, D])
        xc = s.sb("xc", [P, AHEAD, DC, P])
        z = s.sb("z", [P, AHEAD, D])
        h = s.sb("h", [P, AHEAD, D])
        bank = [s.ps(f"bank{k}", [P, G]) for k in range(8)]
        loaded, small, stored = s.sem("loaded"), s.sem("small"), s.sem("stored")
        xn_ready, xt_ps, xt_ready = s.sem("xn_ready"), s.sem("xt_ps"), s.sem("xt_ready")
        gate_ps, gate_ready, ig_ready, fc_step, c_ready = (
            s.sem("gate_ps"), s.sem("gate_ready"), s.sem("ig_ready"), s.sem("fc_step"), s.sem("c_ready"))
        cc_ready, cu_ps, cu_ready = s.sem("cc_ready"), s.sem("cu_ps"), s.sem("cu_ready")
        xc_ready, y_ps, z_ready, h_ready, x_ready = (
            s.sem("xc_ready"), s.sem("y_ps"), s.sem("z_ready"), s.sem("h_ready"), s.sem("x_ready"))

        with nc.Block() as block:
            @block.sync
            def _(sp):
                for k, n in enumerate("fic"):
                    sp.dma_start(wx[:, k, :, :], weight_view(io[f"L3_ffn_w{n}_T"])).then_inc(loaded, 16)
                    sp.dma_start(wc[:, k, :, :], weight_view(io[f"L3_ffn_u{n}_T"])).then_inc(loaded, 16)
                sp.dma_start(wo[:, :, :], weight_view(io.L3_ffn_wo_T)).then_inc(loaded, 16)
                sp.dma_start(uo[:, :, :], weight_view(io.L3_ffn_uo_T)).then_inc(loaded, 16)
                sp.dma_start(bo[:, :], io.L3_ffn_bo.partition_broadcast(P)).then_inc(small, 16)
                sp.dma_start(c0[:, :], io.L3_ffn_in_c_cols).then_inc(small, 16)
                for k, n in enumerate("fic"):
                    sp.dma_start(bg[:, k, :], io[f"L3_ffn_b{n}_cols"]).then_inc(small, 16)
                for b in range(B):
                    sp.wait_ge(x_ready, AHEAD + (b + 1) * TB)
                    sp.dma_start(out[b].rearrange("(t p) d -> p t d", p=P),
                                 sh.x[:, b * TB * D:(b + 1) * TB * D].rearrange("p (t d) -> p t d", d=D)).then_inc(stored, 16)
                sp.wait_ge(stored, 16 * B)

            @block.vector
            def _(dve):
                norm_vector(nc, dve, sh, s)
                dve.sem_inc(xn_ready, AHEAD)

                def norm(t, u):
                    dve.wait_ge(xt_ps, ev(t, back=2))
                    normalise(nc, sh, xn[:, u, :], t).then_inc(xn_ready, 1)

                pipeline(dve, T, [(norm, 0)])
                dve.wait_ge(small, 16 * 5)
                for c in range(DC):
                    nc.vector.tensor_copy(ct[:, 0, c, :], c0[:, c:c + 1].to_broadcast((P, S))).then_inc(c_ready, HU - 1 if c else 1)

                def cell(b, v, j, m):
                    n = b * HU + (j * DC + m)
                    u = m
                    old, new = ct[:, v, m, j * G:(j + 1) * G], ct[:, 1 - v, m, j * G:(j + 1) * G]
                    dve.wait_ge(gate_ready, (n + 3) * 3)
                    dve.wait_ge(c_ready, n + HU)
                    nc.vector.tensor_tensor(prod[:, u, 0, :], gate[:, u, 0, :], old, ALU.mult).then_inc(fc_step, 1)
                    dve.wait_ge(fc_step, n + 1)
                    dve.wait_ge(ig_ready, n + 3)
                    nc.vector.tensor_tensor(new, prod[:, u, 0, :], prod[:, u, 1, :], ALU.add).then_inc(c_ready, 1)

                with dve.Fori(0, B // 2) as bb:
                    for v in range(2):
                        for j in range(NJ):
                            for m in range(DC):
                                cell(bb * 2 + v, v, j, m)

                dve.wait_ge(c_ready, (B + 1) * HU)
                for q in range(TB):
                    dve.wait_ge(cu_ps, q + 1)
                    nc.vector.tensor_tensor(cu[:, q, :], bank[q % 2][:, 0:D], bo[:, :], ALU.add).then_inc(cu_ready, 1)
                dve.wait_ge(cu_ready, TB)
                dve.sem_inc(z_ready, AHEAD)
                dve.sem_inc(x_ready, AHEAD)

                def pre(t, u):
                    dve.wait_ge(y_ps, ev(t))
                    dve.wait_ge(h_ready, ev(t, back=2))
                    nc.vector.tensor_tensor(z[:, u, :], bank[2 + u][:, 0:D], cu[:, ds(t % TB, 1), :].squeeze(1), ALU.add).then_inc(z_ready, 1)

                def update(t, u):
                    dve.wait_ge(h_ready, ev(t))
                    nc.vector.scalar_tensor_tensor(x_tile(sh, t), h[:, u, :], sh.gates[:, 7:8], x_tile(sh, t),
                                                   ALU.mult, ALU.add).then_inc(x_ready, 1)

                pipeline(dve, T, [(pre, 1), (update, 0)])
                dve.wait_ge(x_ready, T + AHEAD)

            @block.gpsimd
            def _(pool):
                pool.sem_inc(ig_ready, 2)

                def product(b, j, m):
                    n = b * HU + (j * DC + m)
                    pool.wait_ge(gate_ready, (n + 3) * 3)
                    pool.wait_ge(c_ready, n + HU - 1)
                    nc.gpsimd.tensor_tensor(prod[:, m, 1, :], gate[:, m, 1, :], gate[:, m, 2, :], ALU.mult).then_inc(ig_ready, 1)

                with pool.Fori(0, B) as b:
                    for j in range(NJ):
                        for m in range(DC):
                            product(b, j, m)
                pool.wait_ge(c_ready, (B + 1) * HU)
                pool.sem_inc(xc_ready, AHEAD)

                def copy(t, u):
                    pool.wait_ge(y_ps, ev(t, back=2))
                    nc.gpsimd.tensor_copy(xc[:, u, :, :], xt_all[:, :, ds(t * P, P)]).then_inc(xc_ready, 1)

                pipeline(pool, T, [(copy, 0)])

            @block.tensor
            def _(pe):
                pe.sem_inc(xt_ps, AHEAD)

                def front(t, u):
                    pe.wait_ge(xn_ready, ev(t))
                    pe.wait_ge(xt_ready, ev(t, back=2))
                    for c in range(DC):
                        ins = nc.tensor.transpose(bank[6 + u][:, c * P:(c + 1) * P], xn[:, u, c * P:(c + 1) * P], sh.ident[:, :])
                    ins.then_inc(xt_ps, 1)

                pipeline(pe, T, [(front, 0)])
                pe.wait_ge(xt_ready, T + AHEAD)
                pe.wait_ge(loaded, 16 * 8)

                def gates(b, v, j, m):
                    n = b * HU + (j * DC + m)
                    pe.wait_ge(gate_ready, (n + 1) * 3)
                    for k in range(3):
                        for c in range(DC):
                            nc.tensor.matmul(bank[3 * m + k][:, :], wx[:, k, c, m * P:(m + 1) * P],
                                             xt_all[:, c, ds(b * S + j * G, G)], start=(c == 0), stop=False)
                    pe.wait_ge(c_ready, b * HU + (j * DC + 2))
                    for k in range(3):
                        for c in range(DC):
                            ins = nc.tensor.matmul(bank[3 * m + k][:, :], wc[:, k, c, m * P:(m + 1) * P],
                                                   ct[:, v, c, j * G:(j + 1) * G], start=False, stop=(c == DC - 1))
                        ins.then_inc(gate_ps, 1)

                with pe.Fori(0, B // 2) as bb:
                    for v in range(2):
                        for j in range(NJ):
                            for m in range(DC):
                                gates(bb * 2 + v, v, j, m)

                pe.wait_ge(c_ready, (B + 1) * HU)
                for q in range(TB):
                    if q >= 2:
                        pe.wait_ge(cu_ready, q - 1)
                    else:
                        pe.wait_ge(gate_ready, (B * HU + 2) * 3)
                    for c in range(DC):
                        ins = nc.tensor.matmul(bank[q % 2][:, 0:D], ct[:, B % 2, c, q * P:(q + 1) * P], uo[:, c, :],
                                               start=(c == 0), stop=(c == DC - 1))
                    ins.then_inc(cu_ps, 1)
                pe.sem_inc(y_ps, AHEAD)

                def output(t, u):
                    pe.wait_ge(xc_ready, ev(t))
                    pe.wait_ge(z_ready, ev(t, back=2))
                    for c in range(DC):
                        ins = nc.tensor.matmul(bank[2 + u][:, 0:D], xc[:, u, c, :], wo[:, c, :],
                                               start=(c == 0), stop=(c == DC - 1))
                    ins.then_inc(y_ps, 1)

                pipeline(pe, T, [(output, 0)])

            @block.scalar
            def _(act):
                act.sem_inc(xt_ready, AHEAD)

                def copy(t, u):
                    act.wait_ge(xt_ps, ev(t))
                    nc.scalar.activation(xt_all[:, :, ds(t * P, P)], bank[6 + u][:, 0:D].rearrange("p (c n) -> p c n", c=DC),
                                         ACT.Copy).then_inc(xt_ready, 1)

                pipeline(act, T, [(copy, 0)])
                act.wait_ge(small, 16 * 5)
                act.sem_inc(gate_ready, 6)

                def squash(b, j, m):
                    n = b * HU + (j * DC + m)
                    act.wait_ge(c_ready, n + HU - 1)
                    act.wait_ge(ig_ready, n + 1)
                    for k, f in enumerate((ACT.Sigmoid, ACT.Sigmoid, ACT.Tanh)):
                        act.wait_ge(gate_ps, n * 3 + (k + 1))
                        nc.scalar.activation(gate[:, m, k, :], bank[3 * m + k][:, :], f, bias=bg[:, k, m:m + 1]).then_inc(gate_ready, 1)

                with act.Fori(0, B) as b:
                    for j in range(NJ):
                        for m in range(DC):
                            squash(b, j, m)
                act.sem_inc(h_ready, AHEAD)

                def tanh(t, u):
                    act.wait_ge(z_ready, ev(t))
                    act.wait_ge(x_ready, ev(t, back=2))
                    nc.scalar.activation(h[:, u, :], z[:, u, :], ACT.Tanh).then_inc(h_ready, 1)

                pipeline(act, T, [(tanh, 0)])


def stage_mha(nc, io, sh, name, names, gate, mask, key_padding, bias_names, masked):
    s = scope(nc, name)
    GH = 4
    NG = HEADS // GH
    GW = GH * SK
    HW_ = HH * SK
    NV = -(-HW_ // P)
    LAST = HW_ - (NV - 1) * P
    TURNS = [[(m, i) for i in range(NV - 1)] for m in range(DC)] + [[(m, NV - 1) for m in range(DC)]]
    NB = len(TURNS)
    VW = P + HH
    BIG = -2.0 ** 100
    wq_T, wk_T, wv_T, wo_T = names
    with s.ctx:
        norm_sems(s)
        wq, wk, wv, wo = (s.sb(n, [P, DC, D]) for n in ("wq", "wk", "wv", "wo"))
        bq, bk, bv = (s.sb(n, [P, DC]) for n in ("bq", "bk", "bv"))
        brow = s.sb("brow", [P, D])
        bvb = s.sb("bvb", [P, DC, P])
        hm = s.sb("hm", [P, HH])
        kt = s.sb("kt", [P, DC, B * SK])
        vt = s.sb("vt", [P, DC, B * SK])
        kbd = s.sb("kbd", [P, B * DC * HW_])
        vbd = s.sb("vbd", [P, 2, DC, HW_])
        vrow = s.sb("vrow", [P, B * DC * NV * VW])
        ones_row = s.sb("ones_row", [P, NV, HH])
        keyrow = s.sb("keyrow", [P, B, SK], U8)
        mraw = s.sb("mraw", [P, TB, SK], U8 if masked else F32)
        mask_t = s.sb("mask_t", [P, T, SK])
        xn = s.sb("xn", [P, AHEAD, D])
        xt = s.sb("xt", [P, AHEAD, D])
        qt = s.sb("qt", [P, AHEAD, D])
        mx = s.sb("mx", [P, AHEAD, HEADS])
        ri = s.sb("ri", [P, AHEAD, HEADS])
        pr = s.sb("pr", [P, AHEAD, HEADS * SK])
        pt = s.sb("pt", [P, AHEAD, NB, 4 * P])
        o = s.sb("o", [P, AHEAD, D])
        ot = s.sb("ot", [P, AHEAD, D])
        x_bank, o_bank = s.ps("x_bank", [P, 512]), s.ps("o_bank", [P, 512])
        score = s.ps("score", [P, NG, 512])
        p_bank = [s.ps(f"p_bank{k}", [P, 512]) for k in range(2)]
        sems = ["w_loaded", "small_loaded", "kv_ps", "kv_ready", "vbd_ready", "kbd_ready", "kbd_rest_ready", "v_ps", "v_ready", "brow_ps",
                "brow_ready", "bvb_ready", "set_step", "mask_set", "xn_ready", "xt_ps", "xt_ready", "q_ps", "q_ready",
                "s_ps", "added", "max_ready", "shifted", "exp_ready", "ones_set", "inv_ready", "pt_ps", "pt_ready",
                "o_ps", "o_ready", "ot_ps", "ot_ready", "y_ps", "biased", "x_ready", "stats_ready"]
        for n in sems:
            s[n] = s.sem(n)
        tg = sh.gates[:, gate:gate + 1]

        def heads(ap):
            return ap.rearrange("p (h k) -> p h k", k=SK)

        def prob(u, m):
            return pr[:, u, m * HW_:(m + 1) * HW_]

        def rows(i):
            return LAST if i == NV - 1 else P

        def key_blocks(eng, b, ready):
            for k in range(DC):
                at = (b * DC + k) * HW_
                eng.tensor_tensor(heads(kbd[:, at:at + HW_]), kt[:, k, b * SK:(b + 1) * SK].unsqueeze(1).to_broadcast((P, HH, SK)),
                                  hm[:, :].unsqueeze(2).to_broadcast((P, HH, SK)), ALU.mult).then_inc(ready, 1)

        with nc.Block() as block:
            @block.sync
            def _(sp):
                for a, n in ((wk, wk_T), (wv, wv_T), (wq, wq_T), (wo, wo_T)):
                    sp.dma_start(a[:, :, :], weight_view(io[n])).then_inc(s.w_loaded, 16)
                sp.dma_start(hm[:, :], io.head_mask).then_inc(s.small_loaded, 16)
                sp.dma_start(ones_row[:, :, :], io.head_rows.rearrange("(i p) h -> p i h", p=P)).then_inc(s.small_loaded, 16)
                sp.dma_start(mraw[:, :, :], mask.rearrange("(t p) k -> p t k", p=P)).then_inc(s.small_loaded, 16)
                if bias_names:
                    for a, n in zip((bq, bk, bv), bias_names):
                        sp.dma_start(a[:, :], io[n]).then_inc(s.small_loaded, 16)
                    sp.dma_start(brow[:, :], io[bias_names[3]].partition_broadcast(P)).then_inc(s.small_loaded, 16)
                if key_padding is not None:
                    sp.dma_start(keyrow[:, :, :], key_padding.partition_broadcast(P)).then_inc(s.small_loaded, 16)

            smalls = 16 * (3 + (4 if bias_names else 0) + (1 if key_padding is not None else 0))

            @block.vector
            def _(dve):
                c = norm_vector(nc, dve, sh, s)
                if not bias_names:
                    for a in (bq, bk, bv):
                        c.link(nc.vector.memset(a[:, :], 0.0))
                    c.link(nc.vector.memset(brow[:, :], 0.0))
                dve.wait_ge(s.small_loaded, smalls)
                c.link(nc.vector.tensor_scalar(bk[:, :], bk[:, :], HD ** -0.5, None, ALU.mult))
                nc.vector.tensor_copy(bvb[:, :, :], bv[:, :].unsqueeze(2).to_broadcast((P, DC, P))).then_inc(s.bvb_ready, 1)
                dve.wait_ge(s.kv_ready, 2 * DC)
                hmb = hm[:, :].unsqueeze(2).to_broadcast((P, HH, SK))
                for b in range(B):
                    if b >= 2:
                        dve.wait_ge(s.v_ps, (b - 1) * NB)
                    for k in range(DC):
                        nc.vector.tensor_tensor(heads(vbd[:, b % 2, k, :]),
                                                vt[:, k, b * SK:(b + 1) * SK].unsqueeze(1).to_broadcast((P, HH, SK)),
                                                hmb, ALU.mult).then_inc(s.vbd_ready, 1)
                key_blocks(nc.vector, 0, s.kbd_ready)
                for b in range(B):
                    mb = mask_t[:, b * TB:(b + 1) * TB, :]
                    if masked:
                        c.link(nc.vector.tensor_scalar(mb, mraw[:, :, :], -1.0, -BIG, ALU.add, ALU.mult))
                    else:
                        c.link(nc.vector.scalar_tensor_tensor(mb, keyrow[:, b:b + 1, :].to_broadcast((P, TB, SK)), BIG, mraw[:, :, :],
                                                              ALU.mult, ALU.add))
                dve.wait_ge(s.brow_ps, 1)
                c.link(nc.vector.tensor_tensor(brow[:, :], o_bank[:, 0:D], brow[:, :], ALU.add))
                nc.vector.tensor_scalar(brow[:, :], brow[:, :], tg, None, ALU.mult).then_inc(s.brow_ready, 1)
                for n, k in ((s.xn_ready, 1), (s.x_ready, 1), (s.added, DC), (s.shifted, DC), (s.inv_ready, 1), (s.max_ready, DC),
                             (s.o_ready, 1)):
                    dve.sem_inc(n, AHEAD * k)

                def norm(t, u):
                    dve.wait_ge(s.xt_ps, ev(t, back=2))
                    normalise(nc, sh, xn[:, u, :], t).then_inc(s.xn_ready, 1)

                def shift(m):
                    def part(t, u):
                        if m == 0:
                            dve.wait_ge(s.pt_ps, ev(t, NB, back=2))
                        pm = prob(u, m)
                        hw = pm.rearrange("p (g h k) -> p g h k", g=NG // DC, k=SK)
                        hs = heads(pm)
                        half = score[:, m * (NG // DC):(m + 1) * (NG // DC), 0:GW].rearrange("p g (h k) -> p g h k", k=SK)
                        tile_mask = mask_t[:, ds(t, 1), :].unsqueeze(1).to_broadcast((P, NG // DC, GH, SK))
                        mh = mx[:, u, m * HH:(m + 1) * HH]
                        dve.wait_ge(s.s_ps, ev(t, DC, m + 1))
                        nc.vector.tensor_tensor(hw, half, tile_mask, ALU.add).then_inc(s.added, 1)
                        dve.wait_ge(s.added, ev(t, DC, m + 1))
                        nc.vector.tensor_reduce(mh, hs, AX.X, ALU.max).then_inc(s.max_ready, 1)
                        dve.wait_ge(s.max_ready, ev(t, DC, m + 1))
                        nc.vector.tensor_tensor(hs, hs, mh.unsqueeze(2).to_broadcast((P, HH, SK)), ALU.subtract).then_inc(s.shifted, 1)
                    return part

                def scale_o(t, u):
                    blocks = o_bank[:, 0:DC * VW].rearrange("p (m c) -> p m c", c=VW)
                    dve.wait_ge(s.o_ps, ev(t))
                    nc.vector.reciprocal(ri[:, u, :].rearrange("p (m h) -> p m h", m=DC), blocks[:, :, P:VW]).then_inc(s.inv_ready, 1)
                    dve.wait_ge(s.inv_ready, ev(t))
                    dve.wait_ge(s.ot_ps, ev(t, back=2))
                    nc.vector.tensor_tensor(o[:, u, :].rearrange("p (m h d) -> p m h d", m=DC, d=HD),
                                            blocks[:, :, 0:P].rearrange("p m (h d) -> p m h d", d=HD),
                                            ri[:, u, :].rearrange("p (m h) -> p m h", m=DC).unsqueeze(3).to_broadcast((P, DC, HH, HD)),
                                            ALU.mult).then_inc(s.o_ready, 1)

                def update(t, u):
                    dve.wait_ge(s.y_ps, ev(t))
                    dve.wait_ge(s.biased, ev(t))
                    nc.vector.tensor_tensor(x_tile(sh, t), o_bank[:, 0:D], x_tile(sh, t), ALU.add).then_inc(s.x_ready, 1)
                    dve.wait_ge(s.x_ready, ev(t))
                    tile_stats(nc, sh, t).then_inc(s.stats_ready, 1)

                pipeline(dve, T, [(scale_o, 0), (norm, 4), (shift(0), 2), (update, 0), (shift(1), 2)])
                dve.wait_ge(s.stats_ready, T)

            @block.gpsimd
            def _(pool):
                pool.wait_ge(s.small_loaded, smalls)
                nc.gpsimd.tensor_copy(vrow[:, :].rearrange("p (b i c) -> p b i c", b=B * DC, c=VW)[:, :, :, P:VW],
                                      ones_row[:, :, :].unsqueeze(1).to_broadcast((P, B * DC, NV, HH))).then_inc(s.ones_set, 1)
                pool.wait_ge(s.kv_ready, 2 * DC)
                for b in range(1, B):
                    key_blocks(nc.gpsimd, b, s.kbd_rest_ready)
                pool.wait_ge(s.brow_ready, 1)
                pool.sem_inc(s.biased, AHEAD)

                def bias(t, u):
                    pool.wait_ge(s.xn_ready, ev(t))
                    nc.gpsimd.tensor_tensor(x_tile(sh, t), x_tile(sh, t), brow[:, :], ALU.add).then_inc(s.biased, 1)

                pipeline(pool, T, [(bias, 2)])

            @block.tensor
            def _(pe):
                pe.wait_ge(s.w_loaded, 64)
                for j, w_ in enumerate((wk, wv)):
                    for m in range(DC):
                        for k in range(DC):
                            ins = nc.tensor.matmul(score[:, j * DC + m, 0:B * SK], w_[:, k, m * P:(m + 1) * P], sh.ctx_t[:, k, :],
                                                   start=(k == 0), stop=(k == DC - 1))
                        ins.then_inc(s.kv_ps, 1)
                pe.wait_ge(s.bvb_ready, 1)
                for k in range(DC):
                    ins = nc.tensor.matmul(o_bank[:, 0:D], bvb[:, k, :], wo[:, k, :], start=(k == 0), stop=(k == DC - 1))
                ins.then_inc(s.brow_ps, 1)
                for b in range(B):
                    pe.wait_ge(s.vbd_ready, DC * (b + 1))
                    for n, turn_ in enumerate(TURNS):
                        if b * NB + n >= 2:
                            pe.wait_ge(s.v_ready, b * NB + n - 1)
                        for j, (m, i) in enumerate(turn_):
                            ins = nc.tensor.transpose(p_bank[(b * NB + n) % 2][0:rows(i), j * P:(j + 1) * P],
                                                      vbd[:, b % 2, m, i * P:i * P + rows(i)], sh.ident[:, :])
                        ins.then_inc(s.v_ps, 1)
                pe.wait_ge(s.brow_ready, 1)
                pe.wait_ge(s.kv_ready, 2 * DC)
                pe.wait_ge(s.v_ready, B * NB)
                pe.wait_ge(s.ones_set, 1)
                pe.wait_ge(s.kbd_ready, DC)
                pe.wait_ge(s.kbd_rest_ready, DC * (B - 1))
                for n, k in ((s.xt_ps, 1), (s.q_ps, 1), (s.s_ps, DC), (s.pt_ps, NB), (s.o_ps, 1), (s.ot_ps, 1), (s.y_ps, 1)):
                    pe.sem_inc(n, AHEAD * k)

                def turn(t, u):
                    pe.wait_ge(s.xn_ready, ev(t))
                    pe.wait_ge(s.q_ready, ev(t, back=1))
                    for c in range(DC):
                        ins = nc.tensor.transpose(x_bank[:, c * P:(c + 1) * P], xn[:, u, c * P:(c + 1) * P], sh.ident[:, :])
                    ins.then_inc(s.xt_ps, 1)

                def query(t, u):
                    pe.wait_ge(s.xt_ready, ev(t))
                    for m in range(DC):
                        for k in range(DC):
                            ins = nc.tensor.matmul(x_bank[:, D + m * P:D + (m + 1) * P], wq[:, k, m * P:(m + 1) * P],
                                                   xt[:, u, k * P:(k + 1) * P], start=(k == 0), stop=(k == DC - 1))
                    ins.then_inc(s.q_ps, 1)

                def scores(t, u):
                    pe.wait_ge(s.q_ready, ev(t))
                    for k in range(DC):
                        pe.wait_ge(s.added, ev(t, DC, k + 1, back=1))
                        for g in range(k * NG // DC, (k + 1) * NG // DC):
                            ins = nc.tensor.matmul(score[:, g, 0:GW], qt[:, u, k * P:(k + 1) * P],
                                                   kbd[:, ds((t // TB) * (DC * HW_) + g * GW, GW)], start=True, stop=True)
                        ins.then_inc(s.s_ps, 1)

                def values(t, u):
                    for n, turn_ in enumerate(TURNS):
                        pe.wait_ge(s.exp_ready, ev(t, DC, min(n + 1, DC)))
                        pe.wait_ge(s.pt_ready, ev(t, NB, NB - 1 + n, back=1) if n < 2 else ev(t, NB, n - 1))
                        for j, (m, i) in enumerate(turn_):
                            ins = nc.tensor.transpose(p_bank[n % 2][0:rows(i), j * P:(j + 1) * P],
                                                      pr[:, u, m * HW_ + i * P:m * HW_ + i * P + rows(i)], sh.ident[:, :])
                        ins.then_inc(s.pt_ps, 1)
                    pe.wait_ge(s.x_ready, ev(t, back=1))
                    for m in range(DC):
                        for i in range(NV):
                            n = [n for n in range(NB) if (m, i) in TURNS[n]][0]
                            j = TURNS[n].index((m, i))
                            if i in (0, NV - 1):
                                pe.wait_ge(s.pt_ready, ev(t, NB, n + 1))
                            ins = nc.tensor.matmul(o_bank[:, m * VW:(m + 1) * VW], pt[0:rows(i), u, n, j * P:(j + 1) * P],
                                                   vrow[0:rows(i), ds((t // TB) * (DC * NV * VW) + (m * NV + i) * VW, VW)],
                                                   start=(i == 0), stop=(i == NV - 1))
                    ins.then_inc(s.o_ps, 1)

                def turn_o(t, u):
                    pe.wait_ge(s.o_ready, ev(t))
                    for c in range(DC):
                        ins = nc.tensor.transpose(o_bank[:, D + c * P:D + (c + 1) * P], o[:, u, c * P:(c + 1) * P], sh.ident[:, :])
                    ins.then_inc(s.ot_ps, 1)

                def output(t, u):
                    pe.wait_ge(s.ot_ready, ev(t))
                    for k in range(DC):
                        ins = nc.tensor.matmul(o_bank[:, 0:D], ot[:, u, k * P:(k + 1) * P], wo[:, k, :], start=(k == 0), stop=(k == DC - 1))
                    ins.then_inc(s.y_ps, 1)

                pipeline(pe, T, [(turn, 3), (scores, 2), (turn_o, 0), (query, 3), (output, 0), (values, 1)])

            @block.scalar
            def _(act):
                act.wait_ge(s.small_loaded, smalls)
                act.wait_ge(s.bvb_ready, 1)
                for j, (a, scale) in enumerate(((kt, HD ** -0.5), (kt, HD ** -0.5), (vt, 1.0), (vt, 1.0))):
                    act.wait_ge(s.kv_ps, j + 1)
                    if j < 2:
                        nc.scalar.activation(a[:, j % 2, :], score[:, j, 0:B * SK], ACT.Identity, scale=scale,
                                             bias=bk[:, j:j + 1]).then_inc(s.kv_ready, 1)
                    else:
                        nc.scalar.activation(a[:, j % 2, :], score[:, j, 0:B * SK], ACT.Copy).then_inc(s.kv_ready, 1)
                for b in range(B):
                    for n, turn_ in enumerate(TURNS):
                        act.wait_ge(s.v_ps, b * NB + n + 1)
                        r = rows(turn_[0][1])
                        for j, (m, i) in enumerate(turn_ if n == NB - 1 else turn_[:1]):
                            k = 1 if n == NB - 1 else len(turn_)
                            at = (b * DC + m) * NV + i
                            ins = nc.scalar.activation(vrow[0:r, at * VW:(at + k) * VW].rearrange("p (i c) -> p i c", c=VW)[:, :, 0:P],
                                                       p_bank[(b * NB + n) % 2][0:r, j * P:(j + k) * P].rearrange("p (i c) -> p i c", c=P),
                                                       ACT.Copy, scale=sh.gates[0:r, gate:gate + 1])
                        ins.then_inc(s.v_ready, 1)
                for n, k in ((s.xt_ready, 1), (s.q_ready, 1), (s.exp_ready, DC), (s.pt_ready, NB), (s.ot_ready, 1)):
                    act.sem_inc(n, AHEAD * k)

                def copy_x(t, u):
                    act.wait_ge(s.xt_ps, ev(t))
                    act.wait_ge(s.q_ps, ev(t, back=2))
                    nc.scalar.activation(xt[:, u, :], x_bank[:, 0:D], ACT.Copy).then_inc(s.xt_ready, 1)

                def copy_q(t, u):
                    act.wait_ge(s.q_ps, ev(t))
                    act.wait_ge(s.s_ps, ev(t, DC, back=2))
                    for m in range(DC):
                        ins = nc.scalar.activation(qt[:, u, m * P:(m + 1) * P], x_bank[:, D + m * P:D + (m + 1) * P],
                                                   ACT.Identity, bias=bq[:, m:m + 1])
                    ins.then_inc(s.q_ready, 1)

                def copy_o(t, u):
                    act.wait_ge(s.ot_ps, ev(t))
                    act.wait_ge(s.y_ps, ev(t, back=2))
                    nc.scalar.activation(ot[:, u, :], o_bank[:, D:2 * D], ACT.Copy).then_inc(s.ot_ready, 1)

                def exps(m):
                    def part(t, u):
                        act.wait_ge(s.shifted, ev(t, DC, m + 1))
                        nc.scalar.activation(prob(u, m), prob(u, m), ACT.Exp).then_inc(s.exp_ready, 1)
                    return part

                def copy_p(t, u):
                    act.wait_ge(s.o_ps, ev(t, back=2))
                    for n, turn_ in enumerate(TURNS):
                        r, k = rows(turn_[0][1]), len(turn_)
                        act.wait_ge(s.pt_ps, ev(t, NB, n + 1))
                        nc.scalar.activation(pt[0:r, u, n, 0:k * P], p_bank[n % 2][0:r, 0:k * P], ACT.Copy).then_inc(s.pt_ready, 1)

                pipeline(act, T, [(copy_x, 3), (copy_o, 0), (copy_q, 3), (copy_p, 1), (exps(0), 2), (exps(1), 2)])


def stage_l2_xattn(nc, io, sh):
    stage_mha(nc, io, sh, "l2x", [f"L2_xattn_W{n}_T" for n in "qkvo"], 2, io.mask_SxS2_ff0, io.mask_BxS2_bf0,
              None, masked=False)


def stage_l3_xattn(nc, io, sh):
    stage_mha(nc, io, sh, "l3x", [f"L3_xattn_W_{n}_T" for n in "qkvo"], 3, io.mask_1x1xSxS2_bk0, None,
              ["L3_xattn_b_q_cols", "L3_xattn_b_k_cols", "L3_xattn_b_v_cols", "L3_xattn_b_o"], masked=True)


EXPERTS, TOP = 16, 2
HID = 512
ET = -(-(B * S * TOP) // P) + EXPERTS


def stage_l2_ffn(nc, io, sh):
    s = scope(nc, "moe")
    HC = HID // P
    ROW = D + 2
    RES = TOP * B * S
    SEL = 80
    with s.ctx:
        norm_sems(s)
        w1 = s.sb("w1", [P, EXPERTS * DC * HID])
        w2 = s.sb("w2", [P, EXPERTS * HC * D])
        wr = s.sb("wr", [P, DC, EXPERTS])
        brr = s.sb("brr", [P, EXPERTS])
        b1 = s.sb("b1", [P, EXPERTS * HC])
        bf = s.sb("bf", [SEL, D])
        bs = s.sb("bs", [SEL, D], BF16)
        zero = s.sb("zero", [P, ROW])
        xin, xt = s.sb("xin", [P, 2, ROW]), s.sb("xt", [P, 2, D])
        w1e = s.sb("w1e", [P, 2 * DC * HID])
        lg = w1e[:, 0:T * EXPERTS]
        cnt, run_a, run_b = (w1e[:, k * T * EXPERTS:(k + 1) * T * EXPERTS].rearrange("p (t e) -> p t e", e=EXPERTS)
                             for k in range(1, 4))
        v8 = s.sb("v8", [P, T, 8])
        i8 = s.sb("i8", [P, T, 8], U32)
        idx = s.sb("idx", [P, TOP, T])
        wt = s.sb("wt", [P, TOP, T])
        dv = s.sb("dv", [P, T])
        iota = s.sb("iota", [P, EXPERTS])
        oh = s.sb("oh", [P, TOP, T, EXPERTS])
        ohb = s.sb("ohb", [P, T * EXPERTS], BF16)
        tri, onesb = s.sb("tri", [P, P], BF16), s.sb("onesb", [P, P], BF16)
        tot_i = s.sb("tot_i", [P, EXPERTS], I32)
        nt, st_a, st_b = s.sb("nt", [P, EXPERTS]), s.sb("st_a", [P, EXPERTS]), s.sb("st_b", [P, EXPERTS])
        slot_f = s.sb("slot_f", [P, TOP, T])
        slot = s.sb("slot", [P, TOP * T], U32)
        tile_no = s.sb("tile_no", [P, ET])
        eid = s.sb("eid", [P, ET])
        eid_i = s.sb("eid_i", [P, ET], I32)
        pexp = s.sb("pexp", [SEL, 1])
        sel = s.sb("sel", [SEL, ET], BF16)
        cmp_ = oh[:, :, :, :].rearrange("p a t e -> p (a t e)")
        pay = s.sb("pay", [P, 2, TOP, ROW])
        ht = pay[:, :, :, :].rearrange("p u k r -> p u (k r)")[:, :, 0:HID]
        y = s.sb("y", [P, 2, D])
        slots = s.sb("slots", [P, 2 * TOP], U32)
        tag = s.sb("tag", [P, T, TOP, 2])
        keep, keep_b = s.sb("keep", [P, T]), s.sb("keep_b", [P, T])
        meta = s.sb("meta", [P, 2, ET])
        spare = s.sb("spare", [P, ET])
        unused = s.sb("unused", [P, 2])
        row = s.sb("row", [P, 2], U32)
        results = w1[:, :].rearrange("p (k t d) -> p k t d", k=TOP, d=D)
        xs = nc.dram_tensor("moe_sorted", (ET * P, ROW), F32, kind="Internal").ap()
        ys = nc.dram_tensor("moe_results", (RES + ET * P, D), F32, kind="Internal").ap()
        bank = [s.ps(f"bank{k}", [P, 512]) for k in range(8)]
        for n in ["w_loaded", "small_loaded", "b_loaded", "zero_ready", "zero_filled", "iota_ready", "xn_ready", "xt_ps", "xt_ready",
                  "lg_ps", "lg_ready", "max_step", "dv_ready", "wt_ready", "set_step", "oh_ready", "cnt_ps",
                  "pay0_ready", "pay1_ready", "slots_ready", "scatter_begun", "kept", "xs_loaded0", "xs_loaded1", "scattered0", "scattered1",
                  "et_ps", "et_ready", "meta_ready", "w1e_ready", "h_ps", "ht_ready", "y_ps", "y_ready", "unused_ready", "row_ready",
                  "store_begun", "y_stored0", "y_stored1", "summed", "x_ready", "stats_ready"] + [f"results_loaded{b}" for b in range(B)]:
            s[n] = s.sem(n)
        tg = sh.gates[:, 6:7]
        IOTAS = 11

        with nc.Block() as block:
            @block.sync
            def _(sp):
                sp.dma_start(wr[:, :, :], weight_view(io.L2_ffn_Wr)).then_inc(s.small_loaded, 16)
                sp.dma_start(brr[:, :], io.L2_ffn_br.partition_broadcast(P)).then_inc(s.small_loaded, 16)
                sp.dma_start(b1[:, :], io.L2_ffn_b1_cols).then_inc(s.w_loaded, 16)
                sp.wait_ge(s.zero_ready, 3)
                for k in range(3):
                    sp.dma_start(bf[32 * k:32 * k + EXPERTS, :], io.L2_ffn_b2).then_inc(s.b_loaded, 16)
                sp.dma_start(xs.rearrange("(t p) d -> p t d", p=P), zero[:, :].unsqueeze(1).to_broadcast((P, ET, ROW))).then_inc(s.zero_filled, 16)
                for e in range(EXPERTS):
                    sp.dma_start(w1[:, e * DC * HID:(e + 1) * DC * HID].rearrange("p (c n) -> p c n", c=DC),
                                 weight_view(io.L2_ffn_W1[e])).then_inc(s.w_loaded, 16)
                    sp.dma_start(w2[:, e * HC * D:(e + 1) * HC * D].rearrange("p (c n) -> p c n", c=HC),
                                 weight_view(io.L2_ffn_W2[e])).then_inc(s.w_loaded, 16)

            @block.vector
            def _(dve):
                nc.vector.memset(zero[:, :], 0.0).then_inc(s.zero_ready, 1)
                nc.vector.memset(bf[:, :], 0.0).then_inc(s.zero_ready, 1)
                nc.vector.memset(bs[:, :], 0.0).then_inc(s.zero_ready, 1)
                c = norm_vector(nc, dve, sh, s)
                dve.wait_ge(s.b_loaded, 48)
                for k in range(3):
                    rows = slice(32 * k, 32 * k + EXPERTS)
                    for i in range(k):
                        c.link(nc.vector.tensor_copy(bs[rows, :], bf[rows, :]))
                        c.link(nc.vector.tensor_tensor(bf[rows, :], bf[rows, :], bs[rows, :], ALU.subtract))
                    c.link(nc.vector.tensor_copy(bs[rows, :], bf[rows, :]))
                dve.wait_ge(s.small_loaded, 32)
                dve.sem_inc(s.xn_ready, AHEAD)
                dve.sem_inc(s.lg_ready, AHEAD)

                def norm(t, u):
                    dve.wait_ge(s.xt_ps, ev(t, back=2))
                    normalise(nc, sh, xin[:, u, 0:D], t).then_inc(s.xn_ready, 1)

                def logits(t, u):
                    dve.wait_ge(s.lg_ps, ev(t))
                    nc.vector.tensor_tensor(lg[:, ds(t * EXPERTS, EXPERTS)], bank[2 + u][:, 0:EXPERTS], brr[:, :], ALU.add).then_inc(s.lg_ready, 1)

                pipeline(dve, T, [(norm, 4), (logits, 0)])
                dve.wait_ge(s.lg_ready, T + AHEAD)
                for t in range(T):
                    nc.vector.max(v8[:, t, :], lg[:, t * EXPERTS:(t + 1) * EXPERTS]).then_inc(s.max_step, 1)
                dve.wait_ge(s.max_step, T)
                for t in range(T):
                    nc.vector.max_index(i8[:, t, :], v8[:, t, :], lg[:, t * EXPERTS:(t + 1) * EXPERTS]).then_inc(s.max_step, 1)
                dve.wait_ge(s.max_step, 2 * T)
                nc.vector.tensor_tensor(dv[:, :], v8[:, :, 0], v8[:, :, 1], ALU.subtract).then_inc(s.dv_ready, 1)
                for k in range(TOP):
                    c.link(nc.vector.tensor_copy(idx[:, k, :], i8[:, :, k]))
                dve.wait_ge(s.iota_ready, IOTAS)
                for k in range(TOP):
                    c.link(nc.vector.tensor_tensor(oh[:, k, :, :], idx[:, k, :].unsqueeze(2).to_broadcast((P, T, EXPERTS)),
                                                   iota[:, :].unsqueeze(1).to_broadcast((P, T, EXPERTS)), ALU.is_equal))
                nc.vector.tensor_tensor(ohb[:, :].rearrange("p (t e) -> p t e", e=EXPERTS), oh[:, 0, :, :], oh[:, 1, :, :], ALU.add).then_inc(s.oh_ready, 1)
                dve.wait_ge(s.cnt_ps, 1)
                c.link(nc.vector.tensor_copy(cnt[:, :, :].rearrange("p t e -> p (t e)"), bank[1][:, :]))
                src, dst = cnt, run_a
                for shift in (1, 2, 4, 8, 16):
                    c.link(nc.vector.tensor_tensor(dst[:, shift:T, :], src[:, shift:T, :], src[:, 0:T - shift, :], ALU.add))
                    c.link(nc.vector.tensor_copy(dst[:, 0:shift, :], src[:, 0:shift, :]))
                    src, dst = dst, (run_b if dst is run_a else run_a)
                total = src
                c.link(nc.vector.tensor_scalar(tot_i[:, :], total[:, T - 1, :], float(P - 1), None, ALU.add))
                c.link(nc.vector.tensor_scalar(tot_i[:, :], tot_i[:, :], 7, None, ALU.arith_shift_right))
                c.link(nc.vector.tensor_copy(nt[:, :], tot_i[:, :]))
                a, b_ = nt, st_a
                for shift in (1, 2, 4, 8):
                    c.link(nc.vector.tensor_tensor(b_[:, shift:], a[:, shift:], a[:, 0:EXPERTS - shift], ALU.add))
                    c.link(nc.vector.tensor_copy(b_[:, 0:shift], a[:, 0:shift]))
                    a, b_ = b_, (st_b if b_ is st_a else st_a)
                c.link(nc.vector.tensor_tensor(b_[:, :], a[:, :], nt[:, :], ALU.subtract))
                start = b_
                c.link(nc.vector.tensor_tensor(dst[:, :, :], total[:, :, :], cnt[:, :, :], ALU.subtract))
                c.link(nc.vector.scalar_tensor_tensor(dst[:, :, :], start[:, :].unsqueeze(1).to_broadcast((P, T, EXPERTS)), float(P),
                                                      dst[:, :, :], ALU.mult, ALU.add))
                c.link(nc.vector.tensor_tensor(dst[:, :, :].rearrange("p t e -> p (t e)"), dst[:, :, :].rearrange("p t e -> p (t e)"),
                                               bank[0][:, :], ALU.add))
                for k in range(TOP):
                    c.link(nc.vector.tensor_tensor(oh[:, k, :, :], oh[:, k, :, :], dst[:, :, :], ALU.mult))
                    c.link(nc.vector.tensor_reduce(slot_f[:, k, :], oh[:, k, :, :], AX.X, ALU.add))
                c.link(nc.vector.tensor_copy(slot[:, :].rearrange("p (t k) -> p k t", k=TOP), slot_f[:, :, :]))
                ge = cmp_[:, 0:EXPERTS * (ET // 2)].rearrange("p (j e) -> p j e", e=EXPERTS)
                for half in range(2):
                    part = slice(half * (ET // 2), (half + 1) * (ET // 2))
                    c.link(nc.vector.tensor_tensor(ge, tile_no[:, part].unsqueeze(2).to_broadcast((P, ET // 2, EXPERTS)),
                                                   start[:, :].unsqueeze(1).to_broadcast((P, ET // 2, EXPERTS)), ALU.is_ge))
                    c.link(nc.vector.tensor_reduce(eid[:, part], ge, AX.X, ALU.add))
                c.link(nc.vector.tensor_scalar(eid[:, :], eid[:, :], -1.0, None, ALU.add))
                c.link(nc.vector.tensor_copy(eid_i[:, :], eid[:, :]))
                c.link(nc.vector.tensor_scalar(sel[:, :], eid[0:SEL, :], pexp[:, 0:1], None, ALU.is_equal))
                dve.wait_ge(s.wt_ready, 2)
                for k in range(TOP):
                    c.link(nc.vector.tensor_scalar(tag[:, :, k, 1], wt[:, k, :], tg, None, ALU.mult))
                c.link(nc.vector.tensor_scalar(keep[:, :], sh.rstd[:, :], tg, 1.0, ALU.mult, ALU.add))
                c.link(nc.vector.tensor_scalar(keep_b[:, :], sh.shift[:, :], tg, None, ALU.mult))

            @block.gpsimd
            def _(pool):
                c = Chain(pool, s.iota_ready)
                c.link(nc.gpsimd.iota(iota[:, :], [[1, EXPERTS]], base=0, channel_multiplier=0, allow_small_or_imprecise_dtypes=True))
                c.link(nc.gpsimd.iota(tile_no[:, :], [[1, ET]], base=0, channel_multiplier=0, allow_small_or_imprecise_dtypes=True))
                c.link(nc.gpsimd.memset(pexp[:, :], -1.0))
                for k in range(3):
                    c.link(nc.gpsimd.iota(pexp[32 * k:32 * k + EXPERTS, :], [[0, 1]], base=0, channel_multiplier=1,
                                          allow_small_or_imprecise_dtypes=True))
                for k in range(TOP):
                    c.link(nc.gpsimd.iota(tag[:, :, k, 0], [[P, T]], base=k * B * S + 1, channel_multiplier=1,
                                          allow_small_or_imprecise_dtypes=True))
                c.link(nc.gpsimd.iota(spare[:, :], [[P, ET]], base=RES + 1, channel_multiplier=1, allow_small_or_imprecise_dtypes=True))
                c.link(nc.gpsimd.memset(onesb[:, :], 1.0))
                c.link(nc.gpsimd.affine_select(out=tri[:, :], in_=onesb[:, :], compare_op=ALU.is_gt, fill=0.0, base=0, pattern=[[1, P]],
                                               channel_multiplier=-1))

            @block.tensor
            def _(pe):
                pe.wait_ge(s.small_loaded, 32)
                pe.sem_inc(s.xt_ps, AHEAD)
                pe.sem_inc(s.lg_ps, AHEAD)

                def front(t, u):
                    pe.wait_ge(s.xn_ready, ev(t))
                    pe.wait_ge(s.xt_ready, ev(t, back=2))
                    for c in range(DC):
                        ins = nc.tensor.transpose(bank[u][:, c * P:(c + 1) * P], xin[:, u, c * P:(c + 1) * P], sh.ident[:, :])
                    ins.then_inc(s.xt_ps, 1)

                def back(t, u):
                    pe.wait_ge(s.xt_ready, ev(t))
                    pe.wait_ge(s.lg_ready, ev(t, back=2))
                    for c in range(DC):
                        ins = nc.tensor.matmul(bank[2 + u][:, 0:EXPERTS], xt[:, u, c * P:(c + 1) * P], wr[:, c, :],
                                               start=(c == 0), stop=(c == DC - 1))
                    ins.then_inc(s.lg_ps, 1)

                pipeline(pe, T, [(back, 0), (front, 2)])
                pe.wait_ge(s.oh_ready, 1)
                pe.wait_ge(s.iota_ready, IOTAS)
                pe.wait_ge(s.xt_ready, T + AHEAD)
                nc.tensor.matmul(bank[0][:, :], tri[:, :], ohb[:, :], start=True, stop=True)
                nc.tensor.matmul(bank[1][:, :], onesb[:, :], ohb[:, :], start=True, stop=True).then_inc(s.cnt_ps, 1)

            @block.scalar
            def _(act):
                act.sem_inc(s.xt_ready, AHEAD)

                def part(t, u):
                    act.wait_ge(s.xt_ps, ev(t))
                    act.wait_ge(s.lg_ps, ev(t, back=2))
                    nc.scalar.activation(xt[:, u, :], bank[u][:, 0:D], ACT.Copy).then_inc(s.xt_ready, 1)

                pipeline(act, T, [(part, 0)])
                act.wait_ge(s.dv_ready, 1)
                nc.scalar.activation(wt[:, 0, :], dv[:, :], ACT.Sigmoid).then_inc(s.wt_ready, 1)
                nc.scalar.activation(wt[:, 1, :], dv[:, :], ACT.Sigmoid, scale=-1.0).then_inc(s.wt_ready, 1)
                act.wait_ge(s.wt_ready, 2)

        with nc.Block() as block:
            @block.vector
            def _(dve):
                dve.sem_inc(s.slots_ready, AHEAD)
                dve.sem_inc(s.pay0_ready, AHEAD)

                def fill(t, u):
                    if not (isinstance(t, int) and t < 2):
                        dve.wait_ge((s.scattered0, s.scattered1)[u], (t // 2) * 32)
                    normalise(nc, sh, pay[:, u, 0, 0:D], t)
                    nc.vector.tensor_copy(pay[:, u, :, D:ROW], tag[:, ds(t, 1), :, :].rearrange("p t k r -> p (t k) r")).then_inc(s.pay0_ready, 1)
                    nc.vector.tensor_copy(slots[:, u * TOP:(u + 1) * TOP], slot[:, ds(t * TOP, TOP)]).then_inc(s.slots_ready, 1)

                def residual(t, u):
                    dve.wait_ge(s.pay1_ready, ev(t))
                    dve.wait_ge(s.pay0_ready, ev(t))
                    nc.vector.tensor_scalar(x_tile(sh, t), x_tile(sh, t), keep[:, ds(t, 1)], keep_b[:, ds(t, 1)],
                                            ALU.mult, ALU.add).then_inc(s.kept, 1)

                pipeline(dve, T, [(fill, 2), (residual, 0)])
                dve.wait_ge(s.kept, T)

            @block.scalar
            def _(act):
                act.sem_inc(s.pay1_ready, AHEAD)

                def fill(t, u):
                    if not (isinstance(t, int) and t < 2):
                        act.wait_ge((s.scattered0, s.scattered1)[u], (t // 2) * 32)
                    nc.scalar.activation(pay[:, u, 1, 0:D], x_tile(sh, t), ACT.Identity, bias=sh.shift[:, ds(t, 1)],
                                         scale=sh.rstd[:, ds(t, 1)]).then_inc(s.pay1_ready, 1)

                pipeline(act, T, [(fill, 2)])

            @block.gpsimd
            def _(pool):
                pool.wait_ge(s.zero_filled, 16)

                def part(t, u):
                    pool.wait_ge(s.pay0_ready, ev(t))
                    pool.wait_ge(s.pay1_ready, ev(t))
                    pool.wait_ge(s.slots_ready, ev(t))
                    pool.sem_inc(s.scatter_begun, 1)
                    for k in range(TOP):
                        nc.gpsimd.indirect_dma_start(
                            out=xs, out_offset=bass.IndirectOffsetOnAxis(ap=slots[:, u * TOP + k:u * TOP + k + 1], axis=0),
                            in_=pay[:, u, k, :], in_offset=None).then_inc((s.scattered0, s.scattered1)[u], 16)

                pipeline(pool, T, [(part, 0)])
                pool.wait_ge(s.scattered0, 32 * (T // 2))
                pool.wait_ge(s.scattered1, 32 * (T // 2))

        with nc.Block() as block:
            @block.sync
            def _(sp):
                def load(t, u):
                    sp.wait_ge(s.et_ps, ev(t, back=2))
                    sp.wait_ge(s.meta_ready, ev(t, back=2))
                    sp.dma_start(xin[:, u, :], xs[ds(t * P, P), :]).then_inc((s.xs_loaded0, s.xs_loaded1)[u], 16)

                pipeline(sp, ET, [(load, 2)])

            @block.gpsimd
            def _(pool):
                def store(t, u):
                    pool.wait_ge(s.y_ready, ev(t))
                    pool.wait_ge(s.row_ready, ev(t))
                    pool.sem_inc(s.store_begun, 1)
                    nc.gpsimd.indirect_dma_start(
                        out=ys, out_offset=bass.IndirectOffsetOnAxis(ap=row[:, u:u + 1], axis=0),
                        in_=y[:, u, :], in_offset=None).then_inc((s.y_stored0, s.y_stored1)[u], 16)

                pipeline(pool, ET, [(store, 0)])
                pool.wait_ge(s.y_stored0, 16 * (ET // 2))
                pool.wait_ge(s.y_stored1, 16 * (ET // 2))

            @block.tensor
            def _(pe):
                pe.wait_ge(s.w_loaded, 32 * EXPERTS + 16)
                for n in (s.et_ps, s.h_ps, s.y_ps):
                    pe.sem_inc(n, AHEAD)

                def turn(t, u):
                    pe.wait_ge((s.xs_loaded0, s.xs_loaded1)[u], (t // 2) * 16 + 16)
                    pe.wait_ge(s.et_ready, ev(t, back=1))
                    for c in range(DC):
                        ins = nc.tensor.transpose(bank[0][:, c * P:(c + 1) * P], xin[:, u, c * P:(c + 1) * P], sh.ident[:, :])
                    ins.then_inc(s.et_ps, 1)

                def up(t, u):
                    pe.wait_ge(s.et_ready, ev(t))
                    pe.wait_ge(s.w1e_ready, ev(t))
                    pe.wait_ge(s.ht_ready, ev(t, back=2))
                    for m in range(HC):
                        out = bank[1 + u][:, m * P:(m + 1) * P]
                        for c in range(DC):
                            at = (u * DC + c) * HID + m * P
                            ins = nc.tensor.matmul(out, w1e[:, at:at + P], xt[:, u, c * P:(c + 1) * P],
                                                   start=(c == 0), stop=(c == DC - 1))
                    ins.then_inc(s.h_ps, 1)

                def down(t, u):
                    e = pe.value_load(eid_i[0:1, ds(t, 1)], min_val=0, max_val=EXPERTS - 1)
                    pe.wait_ge(s.ht_ready, ev(t))
                    pe.wait_ge(s.y_ready, ev(t, back=2))
                    nc.tensor.matmul(bank[5 + u][:, 0:D], sel[:, ds(t, 1)].to_broadcast((SEL, P)), bs[:, :], start=True, stop=False)
                    for c in range(HC):
                        ins = nc.tensor.matmul(bank[5 + u][:, 0:D], ht[:, u, c * P:(c + 1) * P], w2[:, ds(e * (HC * D) + c * D, D)],
                                               start=False, stop=(c == HC - 1))
                    ins.then_inc(s.y_ps, 1)

                pipeline(pe, ET, [(up, 1), (turn, 2), (down, 0)])

            @block.scalar
            def _(act):
                act.sem_inc(s.w1e_ready, AHEAD)
                act.sem_inc(s.ht_ready, AHEAD)
                act.wait_ge(s.w_loaded, 32 * EXPERTS + 16)

                def weights(t, u):
                    e = act.value_load(eid_i[0:1, ds(t, 1)], min_val=0, max_val=EXPERTS - 1)
                    act.wait_ge(s.h_ps, ev(t, back=2))
                    nc.scalar.activation(w1e[:, u * DC * HID:(u + 1) * DC * HID], w1[:, ds(e * (DC * HID), DC * HID)], ACT.Copy).then_inc(s.w1e_ready, 1)

                def gelu(t, u):
                    e = act.value_load(eid_i[0:1, ds(t, 1)], min_val=0, max_val=EXPERTS - 1)
                    act.wait_ge(s.h_ps, ev(t))
                    act.wait_ge(s.y_ps, ev(t, back=2))
                    for m in range(HC):
                        ins = nc.scalar.activation(ht[:, u, m * P:(m + 1) * P], bank[1 + u][:, m * P:(m + 1) * P], ACT.Gelu,
                                                   bias=b1[:, ds(e * HC + m, 1)])
                    ins.then_inc(s.ht_ready, 1)

                pipeline(act, ET, [(weights, 2), (gelu, 1)])

            @block.vector
            def _(dve):
                for n in (s.et_ready, s.meta_ready, s.unused_ready, s.row_ready, s.y_ready):
                    dve.sem_inc(n, AHEAD)

                def copy_x(t, u):
                    dve.wait_ge(s.et_ps, ev(t))
                    dve.wait_ge(s.h_ps, ev(t, back=2))
                    nc.vector.tensor_copy(xt[:, u, :], bank[0][:, 0:D]).then_inc(s.et_ready, 1)
                    nc.vector.tensor_copy(meta[:, :, ds(t, 1)], xin[:, u, D:ROW].unsqueeze(2)).then_inc(s.meta_ready, 1)

                def result(t, u):
                    if not (isinstance(t, int) and t < 2):
                        dve.wait_ge((s.y_stored0, s.y_stored1)[u], (t // 2) * 16)
                    dve.wait_ge(s.meta_ready, ev(t))
                    nc.vector.tensor_scalar(unused[:, u:u + 1], meta[:, 0, ds(t, 1)], 0.0, spare[:, ds(t, 1)], ALU.is_equal, ALU.mult).then_inc(s.unused_ready, 1)
                    dve.wait_ge(s.unused_ready, ev(t))
                    nc.vector.scalar_tensor_tensor(row[:, u:u + 1], unused[:, u:u + 1], -1.0, meta[:, 0, ds(t, 1)], ALU.add, ALU.add).then_inc(s.row_ready, 1)
                    dve.wait_ge(s.y_ps, ev(t))
                    nc.vector.tensor_scalar(y[:, u, :], bank[5 + u][:, 0:D], meta[:, 1, ds(t, 1)], None, ALU.mult).then_inc(s.y_ready, 1)

                pipeline(dve, ET, [(copy_x, 4), (result, 2)])

        with nc.Block() as block:
            @block.sync
            def _(sp):
                for b in range(B):
                    for k in range(TOP):
                        at = (k * B + b) * S
                        sp.dma_start(results[:, k, b * TB:(b + 1) * TB, :],
                                     ys[at:at + S, :].rearrange("(t p) d -> p t d", p=P)).then_inc(s[f"results_loaded{b}"], 32 // TOP)

            @block.gpsimd
            def _(pool):
                for b in range(B):
                    pool.wait_ge(s[f"results_loaded{b}"], 32)
                    with pool.Fori(b * TB, (b + 1) * TB) as t:
                        r = [results[:, k, ds(t, 1), :].rearrange("p t d -> p (t d)") for k in range(TOP)]
                        nc.gpsimd.tensor_tensor(r[0], r[0], r[1], ALU.add).then_inc(s.summed, 1)

            @block.vector
            def _(dve):
                dve.sem_inc(s.x_ready, AHEAD)

                def add(t, u):
                    dve.wait_ge(s.summed, t + 1)
                    nc.vector.tensor_tensor(x_tile(sh, t), x_tile(sh, t), results[:, 0, ds(t, 1), :].rearrange("p t d -> p (t d)"),
                                            ALU.add).then_inc(s.x_ready, 1)

                def stats(t, u):
                    dve.wait_ge(s.x_ready, ev(t))
                    tile_stats(nc, sh, t).then_inc(s.stats_ready, 1)

                pipeline(dve, T, [(add, 1), (stats, 0)])
                dve.wait_ge(s.stats_ready, T)


TRANSPOSED = ["L0_xattn_Wk_s", "L0_xattn_Wv_s", "L0_xattn_Wq_s", "L0_xattn_Wv_c", "L0_xattn_Wg", "L0_ffn_w1", "L0_ffn_w2",
              "L1_xattn_Wqr", "L1_xattn_Wqi", "L1_xattn_Wkr", "L1_xattn_Wki", "L1_xattn_Wvr", "L1_xattn_Wvi",
              "L1_xattn_Wo", "L1_ffn_weight", "L2_xattn_Wq", "L2_xattn_Wk", "L2_xattn_Wv", "L2_xattn_Wo",
              "L3_xattn_W_q", "L3_xattn_W_k", "L3_xattn_W_v", "L3_xattn_W_o", "L3_ffn_wf", "L3_ffn_uf",
              "L3_ffn_wi", "L3_ffn_ui", "L3_ffn_wc", "L3_ffn_uc", "L3_ffn_wo", "L3_ffn_uo"]

COLUMNS = ["L3_ffn_in_c", "L3_ffn_bf", "L3_ffn_bi", "L3_ffn_bc", "L0_ffn_conv_b", "L0_xattn_bq_c", "L0_xattn_bk_s",
           "L0_xattn_bq_s", "L0_xattn_bk_c", "L0_xattn_bv_s", "L0_xattn_bv_c", "L1_xattn_bqr", "L1_xattn_bqi", "L1_xattn_bkr", "L1_xattn_bki",
           "L3_xattn_b_q", "L3_xattn_b_k", "L3_xattn_b_v", "L1_xattn_gamma", "L1_xattn_beta"]


def host_layout(inputs):
    a = {k: np.asarray(v) for k, v in inputs.items()}
    laid = {}
    for k, v in a.items():
        if k in TRANSPOSED:
            laid[k + "_T"] = v.T
        elif k in COLUMNS:
            laid[k + "_cols"] = v.reshape(-1, P).T
            if k in ("L0_xattn_bv_s", "L0_xattn_bv_c"):
                laid[k] = v
        elif k in ("L1_xattn_bvr", "L1_xattn_bvi"):
            laid[k + "_row"] = v.reshape(DC, P)
        elif k == "L2_ffn_b1":
            laid[k + "_cols"] = v.reshape(-1, P).T
        elif k == "ctx_1024":
            laid["ctx_T"] = v.reshape(B * SK, D).T
            laid["ctx"] = v
        elif k == "mask_1x1xSxS2_bk0":
            laid[k] = v[0, 0]
        else:
            laid[k] = v
    return laid


def shape_constants():
    c = {"identity": np.eye(P, dtype=np.float32)}
    c["head_mask"] = (np.arange(P)[:, None] // HD == np.arange(HH)[None, :]).astype(np.float32)
    rows = np.arange(-(-HH * SK // P) * P)
    c["head_rows"] = (rows[:, None] // SK == np.arange(HH)[None, :]).astype(np.float32)
    pos = (np.arange(S, dtype=np.float32) + np.float32(0.5)) * np.float32(SK / S) - np.float32(0.5)
    pos = np.clip(pos, np.float32(0.0), np.float32(SK - 1))
    lo = np.floor(pos).astype(np.int32)
    hi = np.minimum(lo + 1, SK - 1)
    w = (pos - lo.astype(np.float32)).astype(np.float32)
    m = np.zeros((SK, S), np.float32)
    m[lo, np.arange(S)] += np.float32(1) - w
    m[hi, np.arange(S)] += w
    c["interpolate"] = m
    def forward(n, rows, freqs):
        angle = 2 * np.pi * (np.outer(np.arange(rows), freqs) % n) / n
        return np.concatenate([np.cos(angle), -np.sin(angle)], 1) / np.sqrt(n)

    kinds = [np.arange(first, NF, step) for first, step in ((0, 4), (2, 4), (1, 2))]
    c["fourier_even"] = np.concatenate([forward(S, S // 4, f) for f in kinds[:2]], 1).astype(np.float32)
    c["fourier_odd"] = forward(S, S // 2, kinds[2]).astype(np.float32)
    c["fourier_context"] = forward(SK, SK, np.arange(KF)).astype(np.float32)
    order = np.concatenate(kinds)
    edge = (order == 0) | (order == S // 2)
    twice = np.where(edge, 1.0, 2.0)[:, None] / np.sqrt(S)
    tables = []
    for kind, rows in enumerate((S // 4, S // 4, S // 2)):
        angle = 2 * np.pi * (np.outer(order, np.arange(rows)) % S) / S
        mine = np.isin(order, kinds[kind]).astype(np.float64)[:, None]
        g = np.zeros((2, NFP, rows))
        g[0, :NF] = mine * twice * np.cos(angle)
        g[1, :NF] = mine * np.where(edge, 0.0, 1.0)[:, None] * -twice * np.sin(angle)
        g = g.reshape(2, FT, FW, rows)[:, KINDS[kind]].transpose(1, 0, 2, 3)
        tables.append(g.reshape(-1, FW, rows).astype(np.float32))
    c["inverse_even"] = np.stack(tables[:2])
    c["inverse_odd"] = tables[2]
    return c


def program(nc, io, out):
    sh = scope(nc, "all")
    with sh.ctx:
        sh.x = sh.sb("x", [P, T * D])
        sh.stats = sh.sb("stats", [P, T * 6])
        for n in ("mean", "var", "vare", "norm_a", "rstd", "shift"):
            sh[n] = sh.sb(n, [P, T])
        sh.gates = sh.sb("gates", [P, 8])
        sh.ident = sh.sb("ident", [P, P])
        sh.identb = sh.sb("identb", [P, P], BF16)
        sh.ones = sh.sb("ones", [P, P])
        sh.ctx_t = sh.sb("ctx_t", [P, DC, B * SK])
        stage_l0_xattn(nc, io, sh)
        stage_l0_ffn(nc, io, sh)
        stage_l1_xattn(nc, io, sh)
        stage_l1_ffn(nc, io, sh)
        stage_l2_xattn(nc, io, sh)
        stage_l2_ffn(nc, io, sh)
        stage_l3_xattn(nc, io, sh)
        stage_l3_ffn(nc, io, sh, out)


def kernel(**inputs):
    import numpy as _np
    import concourse.bacc as _bacc
    from concourse import mybir as _mybir
    from concourse.bass_utils import run_bass_kernel_spmd as _run

    nc = _bacc.Bacc("TRN2", target_bir_lowering=False, num_devices=1)
    laid = host_layout(inputs)
    laid.update(shape_constants())
    arrays, io = {}, Names()
    for name, a in laid.items():
        a = _np.ascontiguousarray(a)
        arrays[f"in_{name}"] = a
        io[name] = nc.dram_tensor(f"in_{name}", a.shape, _mybir.dt.from_np(a.dtype), kind="ExternalInput").ap()
    out = nc.dram_tensor("out_x", (B, S, D), F32, kind="ExternalOutput").ap()
    program(nc, io, out)
    r = _run(nc, [arrays], core_ids=[0])
    return r.results[0]["out_x"]
```
